# Optimizing a Trainium2 kernel written in Bass

```python
import numpy as np
import jax
import jax.numpy as jnp

def _softmax(x, axis=-1):
    return jax.nn.softmax(x, axis=axis)

def _gelu(x):
    return jax.nn.gelu(x, approximate=True)

def _silu(x):
    return jax.nn.silu(x)

def _sigmoid(x):
    return jax.nn.sigmoid(x)

def _layernorm(x, axis=-1, eps=1e-05):
    m = jnp.mean(x, axis=axis, keepdims=True)
    v = jnp.var(x, axis=axis, keepdims=True)
    return (x - m) / jnp.sqrt(v + eps)

def _scatter_add(tgt, idx, src, axis=0):
    return tgt.at[idx].add(src)

def _segment_sum(src, seg, n):
    return jax.ops.segment_sum(src, seg, n)
kernel_name = 'mk_xattn_ffn_d2_seqx_r8_094b08'

def setup_inputs(seed: int=0):
    np.random.seed(seed)
    _w = jnp.asarray

    def _rec_inputs():
        import jax
        import jax.numpy as jnp
        _rk = jax.random.key(seed)
        x = -0.0002928 + 1 * jax.random.normal(jax.random.fold_in(_rk, 1), (4, 512, 128), jnp.float32)
        _lenS = 512 - jax.random.randint(jax.random.fold_in(_rk, 7), (4,), 0, max(1, 512 // 4) + 1, jnp.int32)
        _lenS2 = 154 - jax.random.randint(jax.random.fold_in(_rk, 8), (4,), 0, max(1, 154 // 4) + 1, jnp.int32)
        _ctx_1024P = jax.random.normal(jax.random.fold_in(_rk, 11), (4, 16, 128), jnp.float32)
        _ctx_1024c = jax.random.dirichlet(jax.random.fold_in(_rk, 511), 0.3 * jnp.ones((16,), jnp.float32), (4, 154))
        _ctx_1024t = jnp.einsum('bsk,bkd->bsd', _ctx_1024c, _ctx_1024P)
        _ctx_1024t = _ctx_1024t * jax.lax.rsqrt(jnp.mean(jnp.square(_ctx_1024t)) + 1e-12) * 0.953939
        ctx_1024 = -1.39393e-06 + 0.999914 * (_ctx_1024t + 0.3 * jax.random.normal(jax.random.fold_in(_rk, 611), (4, 154, 128), jnp.float32))
        _validS = jnp.arange(512)[None, :] < _lenS[:, None]
        _validS2 = jnp.arange(154)[None, :] < _lenS2[:, None]
        _causal = jnp.tril(jnp.ones((512, 512), dtype=bool))
        mask_BxSxS2_if1 = jnp.where(jnp.ones((4, 512, 154), dtype=bool), 1, 0).astype(jnp.int32)
        return (x, ctx_1024, mask_BxSxS2_if1)
    x, ctx_1024, mask_BxSxS2_if1 = _rec_inputs()

    def _L0_xattn_setup():
        import jax, jax.numpy as jnp
        import numpy as np
        D_MODEL = 128
        D_K = 64
        D_V = 64
        N_HEADS = 16
        LN_EPS = 1e-05
        key = jax.random.key(seed)
        ks = jax.random.split(key, 9)
        B, S = (2, 256)
        scale = 0.02
        return {'input_Q': jax.random.normal(ks[0], (B, S, D_MODEL), dtype=jnp.float32), 'input_K': jax.random.normal(ks[1], (B, S, D_MODEL), dtype=jnp.float32), 'input_V': jax.random.normal(ks[2], (B, S, D_MODEL), dtype=jnp.float32), 'W_Q': jax.random.normal(ks[3], (D_MODEL, N_HEADS * D_K), dtype=jnp.float32) * scale, 'W_K': jax.random.normal(ks[4], (D_MODEL, N_HEADS * D_K), dtype=jnp.float32) * scale, 'W_V': jax.random.normal(ks[5], (D_MODEL, N_HEADS * D_V), dtype=jnp.float32) * scale, 'W_O': jax.random.normal(ks[6], (N_HEADS * D_V, D_MODEL), dtype=jnp.float32) * scale, 'ln_gamma': jnp.ones((D_MODEL,), dtype=jnp.float32), 'ln_beta': jnp.zeros((D_MODEL,), dtype=jnp.float32)}
    _L0_xattn_all = _L0_xattn_setup()
    _L0_xattn_in = {k: v for k, v in _L0_xattn_all.items() if k in ('W_Q', 'W_K', 'W_V', 'W_O', 'ln_gamma', 'ln_beta')}
    del _L0_xattn_all

    def _L0_ffn_setup():
        import jax, jax.numpy as jnp
        import numpy as np
        HIDDEN = 128
        HEAD_DIM = 64
        N_EXPERTS = 16
        MIN_EXPERTS = 2
        B, T = (4, 256)

        def _normalize(x, axis):
            n = jnp.sqrt(jnp.sum(x * x, axis=axis, keepdims=True))
            return x / jnp.maximum(n, 1e-12)

        def _ste(x):
            hard = jax.lax.stop_gradient((x > 0).astype(x.dtype))
            return hard + x - jax.lax.stop_gradient(x)

        def _gating(hidden_states, sim_matrix, gates):
            b, t, c = hidden_states.shape
            flat = hidden_states.reshape(b * t, c)
            logits = _normalize(flat, -1) @ _normalize(sim_matrix, 0) - jax.nn.sigmoid(gates)
            gated = jax.nn.relu(logits)
            mask = _ste(gated)
            inactive = jnp.sum(mask, axis=1) == 0
            _, fb_idx = jax.lax.top_k(logits, MIN_EXPERTS)
            fb = jnp.zeros_like(mask).at[jnp.arange(b * t)[:, None], fb_idx].set(1.0)
            fb_applied = inactive[:, None] & (fb > 0)
            mask = jnp.where(fb_applied, 1.0, mask)
            masked_logits = jnp.where(mask > 0, gated, -jnp.inf)
            return jax.nn.softmax(masked_logits, axis=-1).reshape(b, t, -1)
        key = jax.random.key(seed)
        ks = jax.random.split(key, 6)
        xav_qkv = float(np.sqrt(6.0 / (HIDDEN + HEAD_DIM)))
        return {'hidden_states': jax.random.normal(ks[0], (B, T, HIDDEN), dtype=jnp.float32), 'sim_matrix': jax.random.normal(ks[1], (HIDDEN, N_EXPERTS), dtype=jnp.float32), 'gates': jnp.zeros((N_EXPERTS,), dtype=jnp.float32), 'q_proj': jax.random.uniform(ks[2], (N_EXPERTS, HIDDEN, HEAD_DIM), jnp.float32, -xav_qkv, xav_qkv), 'k_proj': jax.random.uniform(ks[3], (N_EXPERTS, HIDDEN, HEAD_DIM), jnp.float32, -xav_qkv, xav_qkv), 'v_proj': jax.random.uniform(ks[4], (N_EXPERTS, HIDDEN, HEAD_DIM), jnp.float32, -xav_qkv, xav_qkv), 'o_proj': jax.random.uniform(ks[5], (N_EXPERTS, HEAD_DIM, HIDDEN), jnp.float32, -xav_qkv, xav_qkv)}
    _L0_ffn_all = _L0_ffn_setup()
    _L0_ffn_in = {k: v for k, v in _L0_ffn_all.items() if k in ('sim_matrix', 'gates', 'q_proj', 'k_proj', 'v_proj', 'o_proj')}
    del _L0_ffn_all

    def _L1_xattn_setup():
        import jax, jax.numpy as jnp
        import numpy as np
        HEAD_NUM = 16
        D_MODEL = 128
        NEG = -1000000000.0
        key = jax.random.key(seed)
        ks = jax.random.split(key, 12)
        B, S, D = (2, 256, D_MODEL)
        inp = {'query': jax.random.normal(ks[0], (B, S, D), jnp.float32), 'key': jax.random.normal(ks[1], (B, S, D), jnp.float32), 'value': jax.random.normal(ks[2], (B, S, D), jnp.float32), 'mask': jnp.ones((B, S, S), jnp.int32)}
        scale = 1.0 / np.sqrt(D)
        for i in range(4):
            inp[f'W{i}'] = jax.random.normal(ks[3 + i], (D, D), jnp.float32) * scale
            inp[f'b{i}'] = jnp.zeros((D,), jnp.float32)
        return inp
    _L1_xattn_all = _L1_xattn_setup()
    _L1_xattn_in = {k: v for k, v in _L1_xattn_all.items() if k in ('W0', 'b0', 'W1', 'b1', 'W2', 'b2', 'W3', 'b3')}
    del _L1_xattn_all

    def _L1_ffn_setup():
        import jax, jax.numpy as jnp
        import numpy as np
        B, S, D, F, E = (2, 256, 128, 512, 8)
        LN_EPS = 1e-05

        def _layer_norm(x, gamma, beta):
            mu = jnp.mean(x, axis=-1, keepdims=True)
            var = jnp.mean(jnp.square(x - mu), axis=-1, keepdims=True)
            return (x - mu) * jax.lax.rsqrt(var + LN_EPS) * gamma + beta
        key = jax.random.key(seed)
        ks = jax.random.split(key, 8)

        def xavier(k, shape):
            fan_in, fan_out = (shape[-1], shape[-2])
            a = jnp.sqrt(6.0 / (fan_in + fan_out))
            return jax.random.uniform(k, shape, jnp.float32, -a, a)
        return {'tgt': jax.random.normal(ks[0], (B, S, D), jnp.float32), 'Wr': xavier(ks[1], (E, D)), 'br': jnp.zeros((E,), jnp.float32), 'W1': xavier(ks[2], (E, F, D)), 'b1': jnp.zeros((E, F), jnp.float32), 'W2': xavier(ks[3], (E, D, F)), 'b2': jnp.zeros((E, D), jnp.float32), 'gamma': jnp.ones((D,), jnp.float32), 'beta': jnp.zeros((D,), jnp.float32)}
    _L1_ffn_all = _L1_ffn_setup()
    _L1_ffn_in = {k: v for k, v in _L1_ffn_all.items() if k in ('Wr', 'br', 'W1', 'b1', 'W2', 'b2', 'gamma', 'beta')}
    del _L1_ffn_all
    return {'x': x, 'ctx_1024': ctx_1024, 'mask_BxSxS2_if1': mask_BxSxS2_if1, 'L0_xattn_W_Q': _L0_xattn_in['W_Q'], 'L0_xattn_W_K': _L0_xattn_in['W_K'], 'L0_xattn_W_V': _L0_xattn_in['W_V'], 'L0_xattn_W_O': _L0_xattn_in['W_O'], 'L0_xattn_ln_gamma': _L0_xattn_in['ln_gamma'], 'L0_xattn_ln_beta': _L0_xattn_in['ln_beta'], 'L0_ffn_sim_matrix': _L0_ffn_in['sim_matrix'], 'L0_ffn_gates': _L0_ffn_in['gates'], 'L0_ffn_q_proj': _L0_ffn_in['q_proj'], 'L0_ffn_k_proj': _L0_ffn_in['k_proj'], 'L0_ffn_v_proj': _L0_ffn_in['v_proj'], 'L0_ffn_o_proj': _L0_ffn_in['o_proj'], 'L1_xattn_W0': _L1_xattn_in['W0'], 'L1_xattn_b0': _L1_xattn_in['b0'], 'L1_xattn_W1': _L1_xattn_in['W1'], 'L1_xattn_b1': _L1_xattn_in['b1'], 'L1_xattn_W2': _L1_xattn_in['W2'], 'L1_xattn_b2': _L1_xattn_in['b2'], 'L1_xattn_W3': _L1_xattn_in['W3'], 'L1_xattn_b3': _L1_xattn_in['b3'], 'L1_ffn_Wr': _L1_ffn_in['Wr'], 'L1_ffn_br': _L1_ffn_in['br'], 'L1_ffn_W1': _L1_ffn_in['W1'], 'L1_ffn_b1': _L1_ffn_in['b1'], 'L1_ffn_W2': _L1_ffn_in['W2'], 'L1_ffn_b2': _L1_ffn_in['b2'], 'L1_ffn_gamma': _L1_ffn_in['gamma'], 'L1_ffn_beta': _L1_ffn_in['beta']}

def reference(x, ctx_1024, mask_BxSxS2_if1, L0_xattn_W_Q, L0_xattn_W_K, L0_xattn_W_V, L0_xattn_W_O, L0_xattn_ln_gamma, L0_xattn_ln_beta, L0_ffn_sim_matrix, L0_ffn_gates, L0_ffn_q_proj, L0_ffn_k_proj, L0_ffn_v_proj, L0_ffn_o_proj, L1_xattn_W0, L1_xattn_b0, L1_xattn_W1, L1_xattn_b1, L1_xattn_W2, L1_xattn_b2, L1_xattn_W3, L1_xattn_b3, L1_ffn_Wr, L1_ffn_br, L1_ffn_W1, L1_ffn_b1, L1_ffn_W2, L1_ffn_b2, L1_ffn_gamma, L1_ffn_beta):
    import jax
    import jax.numpy as jnp

    def _L0_xattn_ref(input_Q, input_K, input_V, W_Q, W_K, W_V, W_O, ln_gamma, ln_beta):
        import jax, jax.numpy as jnp
        import numpy as np
        D_MODEL = 128
        D_K = 64
        D_V = 64
        N_HEADS = 16
        LN_EPS = 1e-05
        B, Lq, _ = input_Q.shape
        Lk = input_K.shape[1]
        Q = (input_Q @ W_Q).reshape(B, Lq, N_HEADS, D_K).transpose(0, 2, 1, 3)
        K = (input_K @ W_K).reshape(B, Lk, N_HEADS, D_K).transpose(0, 2, 1, 3)
        V = (input_V @ W_V).reshape(B, Lk, N_HEADS, D_V).transpose(0, 2, 1, 3)
        scores = jnp.einsum('bhqd,bhkd->bhqk', Q, K) / jnp.sqrt(jnp.float32(D_K))
        attn = jax.nn.softmax(scores, axis=1)
        context = jnp.einsum('bhqk,bhkv->bhqv', attn, V)
        context = context.transpose(0, 2, 1, 3).reshape(B, Lq, N_HEADS * D_V)
        output = context @ W_O
        x = output + input_Q
        mu = jnp.mean(x, axis=-1, keepdims=True)
        var = jnp.mean(jnp.square(x - mu), axis=-1, keepdims=True)
        return (x - mu) / jnp.sqrt(var + LN_EPS) * ln_gamma + ln_beta

    def _L0_ffn_ref(hidden_states, sim_matrix, gates, q_proj, k_proj, v_proj, o_proj):
        import jax, jax.numpy as jnp
        import numpy as np
        HIDDEN = 128
        HEAD_DIM = 64
        N_EXPERTS = 16
        MIN_EXPERTS = 2
        B, T = (4, 256)

        def _normalize(x, axis):
            n = jnp.sqrt(jnp.sum(x * x, axis=axis, keepdims=True))
            return x / jnp.maximum(n, 1e-12)

        def _ste(x):
            hard = jax.lax.stop_gradient((x > 0).astype(x.dtype))
            return hard + x - jax.lax.stop_gradient(x)

        def _gating(hidden_states, sim_matrix, gates):
            b, t, c = hidden_states.shape
            flat = hidden_states.reshape(b * t, c)
            logits = _normalize(flat, -1) @ _normalize(sim_matrix, 0) - jax.nn.sigmoid(gates)
            gated = jax.nn.relu(logits)
            mask = _ste(gated)
            inactive = jnp.sum(mask, axis=1) == 0
            _, fb_idx = jax.lax.top_k(logits, MIN_EXPERTS)
            fb = jnp.zeros_like(mask).at[jnp.arange(b * t)[:, None], fb_idx].set(1.0)
            fb_applied = inactive[:, None] & (fb > 0)
            mask = jnp.where(fb_applied, 1.0, mask)
            masked_logits = jnp.where(mask > 0, gated, -jnp.inf)
            return jax.nn.softmax(masked_logits, axis=-1).reshape(b, t, -1)
        b, t, c = hidden_states.shape
        rw = _gating(hidden_states, sim_matrix, gates)
        q = jnp.einsum('bte,bted->btd', rw, jnp.einsum('btc,ecd->bted', hidden_states, q_proj))
        k = jnp.einsum('bte,bted->btd', rw, jnp.einsum('btc,ecd->bted', hidden_states, k_proj))
        v = jnp.einsum('bte,bted->btd', rw, jnp.einsum('btc,ecd->bted', hidden_states, v_proj))
        scale = 1.0 / jnp.sqrt(jnp.asarray(HEAD_DIM, dtype=q.dtype))
        scores = jnp.einsum('bqd,bkd->bqk', q, k) * scale
        causal = jnp.tril(jnp.ones((t, t), dtype=bool))
        scores = jnp.where(causal, scores, -jnp.inf)
        attn = jnp.einsum('bqk,bkd->bqd', jax.nn.softmax(scores, axis=-1), v)
        mixed = attn[:, :, None, :] * rw[..., None]
        return jnp.einsum('bted,edc->btc', mixed, o_proj)

    def _L1_xattn_ref(query, key, value, mask, W0, b0, W1, b1, W2, b2, W3, b3):
        import jax, jax.numpy as jnp
        import numpy as np
        HEAD_NUM = 16
        D_MODEL = 128
        NEG = -1000000000.0
        B, Sq, D = query.shape
        Sk = key.shape[1]
        H, dk = (HEAD_NUM, D // HEAD_NUM)
        q = (query @ W0.T + b0).reshape(B, Sq, H, dk).transpose(0, 2, 1, 3)
        k = (key @ W1.T + b1).reshape(B, Sk, H, dk).transpose(0, 2, 1, 3)
        v = (value @ W2.T + b2).reshape(B, Sk, H, dk).transpose(0, 2, 1, 3)
        scores = jnp.einsum('bhqd,bhkd->bhqk', q, k) / jnp.sqrt(jnp.float32(dk))
        scores = jnp.where(mask[:, None, :, :] == 0, NEG, scores)
        p_attn = jax.nn.softmax(scores, axis=-1)
        x = jnp.einsum('bhqk,bhkd->bhqd', p_attn, v)
        x = x.transpose(0, 2, 1, 3).reshape(B, Sq, D)
        return x @ W3.T + b3

    def _L1_ffn_ref(tgt, Wr, br, W1, b1, W2, b2, gamma, beta):
        import jax, jax.numpy as jnp
        import numpy as np
        B, S, D, F, E = (2, 256, 128, 512, 8)
        LN_EPS = 1e-05

        def _layer_norm(x, gamma, beta):
            mu = jnp.mean(x, axis=-1, keepdims=True)
            var = jnp.mean(jnp.square(x - mu), axis=-1, keepdims=True)
            return (x - mu) * jax.lax.rsqrt(var + LN_EPS) * gamma + beta
        logits = jnp.einsum('bsd,ed->bse', tgt, Wr) + br
        top_v, top_i = jax.lax.top_k(logits, 2)
        top_w = jax.nn.softmax(top_v, axis=-1)
        n_exp = logits.shape[-1]
        router_w = jnp.sum(jax.nn.one_hot(top_i, n_exp, dtype=top_w.dtype) * top_w[..., None], axis=-2)
        h = jnp.einsum('bsd,efd->bsef', tgt, W1) + b1
        h = jax.nn.relu(h)
        o = jnp.einsum('bsef,edf->bsed', h, W2) + b2
        tgt2 = jnp.einsum('bsed,bse->bsd', o, router_w)
        return _layer_norm(tgt + tgt2, gamma, beta)
    x = x + _L0_xattn_ref(_layernorm(x, axis=-1), ctx_1024, ctx_1024, L0_xattn_W_Q, L0_xattn_W_K, L0_xattn_W_V, L0_xattn_W_O, L0_xattn_ln_gamma, L0_xattn_ln_beta)
    x = x + _L0_ffn_ref(_layernorm(x, axis=-1), L0_ffn_sim_matrix, L0_ffn_gates, L0_ffn_q_proj, L0_ffn_k_proj, L0_ffn_v_proj, L0_ffn_o_proj)
    x = x + _L1_xattn_ref(_layernorm(x, axis=-1), ctx_1024, ctx_1024, mask_BxSxS2_if1, L1_xattn_W0, L1_xattn_b0, L1_xattn_W1, L1_xattn_b1, L1_xattn_W2, L1_xattn_b2, L1_xattn_W3, L1_xattn_b3)
    x = x + _L1_ffn_ref(_layernorm(x, axis=-1), L1_ffn_Wr, L1_ffn_br, L1_ffn_W1, L1_ffn_b1, L1_ffn_W2, L1_ffn_b2, L1_ffn_gamma, L1_ffn_beta)
    return x

_drawn_inputs = setup_inputs


def setup_inputs(seed=0):
    import zlib

    import numpy as np

    out = dict(_drawn_inputs(seed))
    spreads = {'L0_xattn_ln_gamma': (1.0, 0.2),
     'L0_xattn_ln_beta': (0.0, 0.1),
     'L0_ffn_gates': (0.0, 0.1),
     'L1_xattn_b0': (0.0, 0.425),
     'L1_xattn_b1': (0.0, 0.8),
     'L1_xattn_b2': (0.0, 0.1),
     'L1_xattn_b3': (0.0, 0.1),
     'L1_ffn_br': (0.0, 0.3),
     'L1_ffn_b1': (0.0, 0.37),
     'L1_ffn_b2': (0.0, 0.332),
     'L1_ffn_gamma': (1.0, 0.2),
     'L1_ffn_beta': (0.0, 0.1)}
    factors = {'L0_xattn_W_Q': 3.997,
     'L0_xattn_W_K': 3.808,
     'L0_ffn_q_proj': 2.796,
     'L0_ffn_k_proj': 2.809}
    for name, (base, spread) in spreads.items():
        noise = np.random.default_rng([zlib.crc32(name.encode()), seed]).standard_normal(out[name].shape)
        drawn = base * np.exp(spread * noise) if base else spread * noise
        out[name] = jnp.asarray(drawn.astype(out[name].dtype))
    for name, factor in factors.items():
        out[name] = (out[name] * factor).astype(out[name].dtype)
    return out
```

```python
from contextlib import ExitStack

import numpy as np

import concourse.bass as bass
from concourse import mybir

ALU = mybir.AluOpType
ACT = mybir.ActivationFunctionType
AX = mybir.AxisListType
F32 = mybir.dt.float32
F32R = mybir.dt.float32r
BF16 = mybir.dt.bfloat16
I32 = mybir.dt.int32

B, S, D, SK = 4, 512, 128, 154
P = 128
NT = S // P
KT = 32
KP = P + KT
TAIL = SK - P
H0, DK0 = 16, 64
NE = 16
DH = 64
H1, DK1 = 16, 8
NG = 4
NX, F = 8, 512
FC = F // P
VZP = P + DK1
VTP = P + 4 * DK1
LN_EPS = 1e-5
NEG = -1e9
HUGE = 1e30
MAGIC = 1597463007.0
SCALE1 = float(DK1) ** -0.5


def constants():
    i = np.arange(P)
    eye = np.eye(P, dtype=np.float32)
    q, r = i // 32, i % 32
    perm64 = (i[:, None] == (i[None, :] + 64) % P)
    perm32 = (i[:, None] == (i[None, :] ^ 32))
    same = r[:, None] == r[None, :]
    after = i[None, :] > i[:, None]
    mats = np.stack([eye, perm64, perm32, same, after], 1).astype(np.float32)
    into = [[0, 2], [1], [0, 1], [2]]
    rep = np.zeros((P, 4, P), np.float32)
    for n, quads in enumerate(into):
        for z in quads:
            rep[i, n, 32 * z + r] = 1
    band = (r[:, None] // DK1 == np.arange(4)[None, :]).astype(np.float32)
    maxrow = np.zeros((32, 4, KP), np.float32)
    for j in range(4):
        maxrow[j, j] = maxrow[4 + j, j] = 1
    pick = np.tile(np.eye(NE, dtype=np.float32), (3, 1))
    pick8 = np.tile(np.eye(NX, dtype=np.float32), (3, 1))
    first = np.zeros((P, NT, NE), np.float32)
    first[:] = NE - np.arange(NE)
    vz = np.zeros((P, H1 * VZP), np.float32)
    vzt = np.zeros((P, NG * VTP), np.float32)
    for h in range(H1):
        at = 64 + DK1 * h if h < 8 else DK1 * (h - 8)
        vz[:, P * h + at:P * h + at + DK1] = 1
        g, j = divmod(h, 4)
        vzt[32 * j:32 * j + TAIL, P * g + at:P * g + at + DK1] = 1
    return {"c_mats": mats, "c_rep": rep, "c_band": band, "c_maxrow": maxrow, "c_pick": pick, 
            "c_pick8": pick8, "c_first": first, "c_vz": vz, "c_vzt": vzt}


DVE_STEPS, POOL_STEPS = 202, 4


class Signal:

    def __init__(self, sem, per_batch):
        self.sem, self.per_batch = sem, per_batch

    def after(self, b, k):
        assert 1 <= k <= self.per_batch
        return b * self.per_batch + k


def program(nc, a, out):
    ctx = ExitStack()
    with ctx:
        def sb(name, shape, dt=F32):
            return ctx.enter_context(nc.sbuf_tensor(name, shape, dt))

        def sem(name):
            return ctx.enter_context(nc.semaphore(name))

        def sig(name, per_batch):
            return Signal(sem(name), per_batch)

        bank = [ctx.enter_context(nc.psum_tensor(f"bank{n}", [P, 512], F32)) for n in range(4)]
        duo = [ctx.enter_context(nc.psum_tensor(f"duo{n}", [P, 2, 512], F32)) for n in range(2)]
        bank += [duo[0][:, 0], duo[0][:, 1], duo[1][:, 0], duo[1][:, 1]]
        bank = [t[:] if n < 4 else t for n, t in enumerate(bank)]

        mats = sb("mats", [P, 5, P])
        ident, perm64, perm32, same, after_ = (mats[:, n, :] for n in range(5))
        ident_b = sb("ident_b", [P, P], BF16)
        causal_b = sb("causal_b", [P, P], BF16)
        neg_b = sb("neg_b", [P, P], BF16)
        ones_b = sb("ones_b", [P, P], BF16)
        rep = sb("rep", [P, 4, P], F32R)
        band = sb("band", [P, 4])
        pick = sb("pick", [3 * NE, NE], BF16)
        pick8 = sb("pick8", [3 * NX, NX], BF16)
        first = sb("first", [P, NT, NE])
        mq = sb("mq", [P, H0, P])
        mo = sb("mo", [P, H0, P])
        qk_w = sb("qk_w", [P, NE, 2 * DH])
        v_w = sb("v_w", [P, NE, DH])
        o_w = sb("o_w", [P, NE // 2, D])
        sim = sb("sim", [P, NE])
        sim_n = sb("sim_n", [P, NE])
        gate = sb("gate", [P, NE])
        ln0 = sb("ln0", [P, 2, D])
        w_att = sb("w_att", [P, 4, D])
        b_att = sb("b_att", [P, 4])
        bq = sb("bq", [P, 1])
        bo = sb("bo", [P, 1])
        w_r = sb("w_r", [P, NX])
        b_r = sb("b_r", [P, NX])
        w1_hi = sb("w1_hi", [P, NX * F], F32R)
        w1_lo = sb("w1_lo", [P, NX * F], F32R)
        b1 = sb("b1", [P, NX * FC])
        b2 = sb("b2", [3 * NX, D])
        b2_parts = sb("b2_parts", [3 * NX, 3, D], BF16)
        ln1 = sb("ln1", [P, 2, D])
        vz = sb("vz", [P, H1 * VZP])
        vz_t = sb("vz_t", [P, NG * VTP])

        x_in = sb("x_in", [P, NT, D])
        h_rows = sb("h_rows", [P, NT, D])
        y_rows = sb("y_rows", [P, NT, D])
        x_rows = sb("x_rows", [P, NT, D])
        out_rows = sb("out_rows", [P, NT, D])
        ctx_T = sb("ctx_T", [P, KP])
        mask_i = sb("mask_i", [P, NT, SK], I32)
        maskT_i = sb("maskT_i", [P, 2, S], I32)
        hT = sb("hT", [P, S])
        hT_hi = sb("hT_hi", [P, S], F32R)
        hT_lo = sb("hT_lo", [P, S], F32R)
        oT = den_p = hT
        ks = sb("ks", [P, NG, 4, KP], F32R)
        qs = sb("qs", [P, NG, S], F32R)
        nm = sb("nm", [P, NT, NG, 32])
        stats = sb("stats", [P, NT, 6])
        mv = sb("mv", [P, NT, 2])
        nv = sb("nv", [P, NT])
        ny = sb("ny", [P, NT])
        nt_ = sb("nt_", [P, NT])
        nu = sb("nu", [P, NT])
        lg = sb("lg", [P, NT, NE])
        lg2 = sb("lg2", [P, NT, NE])
        eq = sb("eq", [P, NT, NE])
        pr = sb("pr", [P, NT, NE])
        s1 = sb("s1", [P, NT, NE])
        s2 = sb("s2", [P, NT, NE])
        gated = sb("gated", [P, NT, NE])
        rw = sb("rw", [P, NT, NE])
        top = sb("top", [P, 2, NT])
        col = sb("col", [P, 4, NT])
        rw_parts = sb("rw_parts", [P, NT, 3 * NE], BF16)
        rw_rest = sb("rw_rest", [P, 2, NT, NE])
        rwT = sb("rwT", [3 * NE, S], BF16)

        def arena(*specs):
            with ExitStack() as own:
                return [own.enter_context(nc.sbuf_tensor(n, sh, dt)) for n, sh, dt in specs]

        cst, wq_T, wk_T, wv_T, wo_n, w1_raw = arena(
            ("cst", [P, 40 * P], F32), ("wq_T", [P, H0 // 2, D], F32), ("wk_T", [P, H0 // 2, D], F32),
            ("wv_T", [P, H0 // 2, D], F32), ("wo_n", [P, H0 // 2, D], F32), ("w1_raw", [P, NX * F], F32))
        rep_raw = cst[:, 0:4 * P].rearrange("p (n c) -> p n c", n=4)
        pick_raw = cst[0:3 * NE, 4 * P:4 * P + NE]
        pick8_raw = cst[0:3 * NX, 5 * P:5 * P + NX]
        maxrow_raw = cst[96:P, 28 * P:28 * P + 4 * KP].rearrange("p (j k) -> p j k", j=4)
        ones_f = cst[:, 36 * P:37 * P]
        sim_sq = cst[:, 37 * P:37 * P + NE]
        sim_ss = cst[:, 37 * P + 16:37 * P + 32]
        sim_t = cst[:, 37 * P + 32:37 * P + 48]
        sim_u = cst[:, 37 * P + 48:37 * P + 64]
        sim_r = cst[:, 37 * P + 64:37 * P + 80]
        b2_rest = cst[0:3 * NX, 38 * P:40 * P].rearrange("p (n c) -> p n c", n=2)
        g_hi, g_lo, u_main, u_tail, sc, top_m, top_t = arena(
            ("g_hi", [P, H0 * KP], F32R), ("g_lo", [P, H0 * KP], F32R), ("u_main", [P, H0, D], F32),
            ("u_tail", [P, NG, D], F32), ("sc", [P, NG + H0, S], F32), ("top_m", [P, S], F32),
            ("top_t", [P, S], F32))
        rh, q_T, k_T, v_T, v_dup, pa, p_T, a_T = arena(
            ("rh", [P, 3, S], F32), ("q_T", [DH, S], F32), ("k_T", [DH, S], F32), ("v_T", [DH, S], F32),
            ("v_dup", [P, NT, 2, DH], F32), ("pa", [P, NT, S], F32), ("p_T", [P, NT, S], F32),
            ("a_T", [P, S], F32))
        w2, ks_t, kv_f, k_hi, k_lo, qf, qm, q_hi, q_lo, pm, mz, mz_T, mx, rz = arena(
            ("w2", [P, NX * FC, D], F32), ("ks_t", [P, NG, P], F32R), ("kv_f", [P, KP], F32),
            ("k_hi", [P, KP], F32R), ("k_lo", [P, KP], F32R), ("qf", [P, S], F32), ("qm", [P, S], F32),
            ("q_hi", [P, S], F32R), ("q_lo", [P, S], F32R), ("pm", [P, 4, S], F32),
            ("mz", [P, NT, SK], BF16), ("mz_T", [P, 2, S], BF16), ("mx", [P, NT, H1], F32), ("rz", [P, S], F32))
        _, hid, rw_b, part, acc = arena(
            ("w2_again", [P, NX * FC, D], F32), ("hid", [P, 4, S], F32), ("rw_b", [P, 2, S], F32),
            ("part", [P, S], F32), ("acc", [P, S], F32))

        passed = sem("passed")
        mats_loaded, fold_loaded, tables_loaded, direct_loaded = (
            sem(n) for n in ("mats_loaded", "fold_loaded", "tables_loaded", "direct_loaded"))
        gated_loaded, experts_loaded, pads_zeroed = (
            sem(n) for n in ("gated_loaded", "experts_loaded", "pads_zeroed"))
        x_loaded, ctx_loaded, mask_loaded = sig("x_loaded", 16), sig("ctx_loaded", 16), sig("mask_loaded", 16 * 6)
        w2_loaded, out_ready, out_stored = sig("w2_loaded", 16), sig("out_ready", 1), sig("out_stored", 16)
        set_step, fold_ready, fold_stored, set_ready, set_act, set_pe, set_dve = (
            sem(n) for n in ("set_step", "fold_ready", "fold_stored", "set_ready", "set_act", "set_pe", "set_dve"))
        dve_step = sig("dve_step", DVE_STEPS)
        pool_step = sig("pool_step", POOL_STEPS)
        h_ready, hT_psum, hT_full, hT_hi_ready, hT_lo_ready = (
            sig("h_ready", 16), sig("hT_psum", 4), sig("hT_full", 3), sig("hT_hi_ready", 2), sig("hT_lo_ready", 2))
        o_psum, oT_stored, back_psum = sig("o_psum", 3), sig("oT_stored", 3), sig("back_psum", 4)
        g_psum, g_hi_ready, g_lo_ready = sig("g_psum", 6), sig("g_hi_ready", 6), sig("g_lo_ready", 6)
        u_psum, u_stored = sig("u_psum", 5), sig("u_stored", 5)
        sc_psum, sc_stored = sig("sc_psum", 20), sig("sc_stored", 20)
        tail_max, tail_turned = sig("tail_max", 2), sig("tail_turned", 2)
        top_t_ready, top_m_ready = sig("top_t_ready", 1), sig("top_m_ready", 1)
        less_dve, less_pool, exp_ready = sig("less_dve", 12), sig("less_pool", 8), sig("exp_ready", 20)
        tail_sum, pool_sum, tail_den = sig("tail_sum", 1), sig("pool_sum", 1), sig("tail_den", 1)
        inv_t_ready, inv_m_ready = sig("inv_t_ready", 1), sig("inv_m_ready", 1)
        attn_dve, attn_pool = sig("attn_dve", 12), sig("attn_pool", 8)
        logit_psum, gate_arg, gate_exp = sig("logit_psum", 2), sig("gate_arg", 2), sig("gate_exp", 2)
        rw_ready, rwT_psum, rwT_stored = sig("rw_ready", 2), sig("rwT_psum", 2), sig("rwT_stored", 2)
        bc_psum, rh_ready, rh_used = sig("bc_psum", 24), sig("rh_ready", 24), sig("rh_used", 23)
        qkv_stored, v_psum, v_stored = (
            sig("qkv_stored", 1), sig("v_psum", 1), sig("v_stored", 1))
        s_psum, s_max, p_exp, p_norm = sig("s_psum", 4), sig("s_max", 4), sig("p_exp", 4), sig("p_norm", 4)
        pT_psum, pT_stored, att_psum, att_stored = (
            sig("pT_psum", 4), sig("pT_stored", 4), sig("att_psum", 1), sig("att_stored", 1))
        mz_ready, k_psum, k_full, k_hi_ready, k_lo_ready = (
            sig("mz_ready", 2), sig("k_psum", 1), sig("k_full", 1), sig("k_hi_ready", 1), sig("k_lo_ready", 1))
        krep_psum, ks_ready, kst_ready, v8_psum, v8_stored = (
            sig("krep_psum", 4), sig("ks_ready", 4), sig("kst_ready", 1), sig("v8_psum", 1), sig("v8_stored", 1))
        q_psum, qf_ready, count_psum, q_masked, q_hi_ready, q_lo_ready = (
            sig("q_psum", 1), sig("qf_ready", 1), sig("count_psum", 1), sig("q_masked", 1), sig("q_hi_ready", 1),
            sig("q_lo_ready", 1))
        qrep_psum, qs_ready, smax_psum, smax_used = (
            sig("qrep_psum", 4), sig("qs_ready", 4), sig("smax_psum", 16), sig("smax_used", 16))
        nm_ready, nmT_psum, nm_stored = sig("nm_ready", 1), sig("nmT_psum", 1), sig("nm_stored", 1)
        st_psum, pm_ready, pm_used = sig("st_psum", 20), sig("pm_ready", 20), sig("pm_used", 20)
        pv_normed = sig("pv_normed", 1)
        l1_psum, hid_ready, hid_used = sig("l1_psum", 32), sig("hid_ready", 32), sig("hid_used", 32)
        ex_used, bc4_psum, rwb_stored = sig("ex_used", 8), sig("bc4_psum", 8), sig("rwb_stored", 8)
        b2_psum, acc_begun, acc_done = sig("b2_psum", 1), sig("acc_begun", 1), sig("acc_done", 1)

        POOL_HEADS = [12, 13, 14, 15]
        DVE_HEADS = [h for h in range(H0) if h not in POOL_HEADS]
        MIXED = [DVE_HEADS[3 * (n // 4) + n % 4] if n % 4 < 3 else POOL_HEADS[n // 4] for n in range(H0)]

        FOLD_HEADS = [0, 1, 8, 9]
        S_BANK, PT_BANK = [1, 2, 3, 1], [0, 2, 3, 0]
        BC_BANK = [0, 1] * (NE // 2) + [0, 2] * (NE // 4)
        KREP_BANK = [5, 6, 7, 4]
        ST_TILES = [(0, None), (1, None)] + [(h // 4, h % 4) for h in range(8)] + \
            [(2, None), (3, None)] + [(h // 4, h % 4) for h in range(8, H1)]
        v_bank = bank[0][:, 0:NT * DH].rearrange("p (i d) -> p i d", d=DH)
        vzt_own = vz_t[:].rearrange("p (g c) -> p g c", c=VTP)

        def rwT_bank(n, rows_):
            return bank[n].bitcast(BF16)[0:rows_, 0:S]

        def apart(eng):
            eng.sem_inc(passed, 1)

        def one(table, e, n=P):
            return table[:, e:e + 1].to_broadcast([table.shape[0], n])

        def g_main(t, h, k):
            return t[:, h * P:(h + k) * P].rearrange("p (h c) -> p h c", c=P)

        def g_tail(t, h, k):
            at = H0 * P + h * KT
            return t[:, at:at + k * KT].rearrange("p (h c) -> p h c", c=KT)

        def rows(t):
            return t.rearrange("p (t c) -> p t c", c=D)

        block = ctx.enter_context(nc.Block())

        @block.sync
        def _(sp):
            def load_x(b):
                sp.dma_start(x_in[:], a["x"][b].rearrange("(t p) c -> p t c", p=P)).then_inc(x_loaded.sem, 16)

            def load_ctx(b):
                sp.dma_start(ctx_T[:, 0:SK], a["ctx_T"][b]).then_inc(ctx_loaded.sem, 16)

            def load_masks(b):
                sp.dma_start(mask_i[:], a["mask"][b].rearrange("(t p) k -> p t k", p=P)).then_inc(mask_loaded.sem, 16)
                sp.dma_start(maskT_i[:, 0, :], a["mask_T"][b][0:P, :]).then_inc(mask_loaded.sem, 16)
                for j in range(4):
                    sp.dma_start(maskT_i[32 * j:32 * j + TAIL, 1, :], a["mask_T"][b][P:SK, :]).then_inc(
                        mask_loaded.sem, 16)

            sp.dma_start(mats[:], a["c_mats"]).then_inc(mats_loaded, 16)
            for dst, name in ((wk_T, "wk_T"), (wq_T, "wq_T"), (wv_T, "wv_T"), (wo_n, "wo")):
                sp.dma_start(dst[:], a[name].rearrange("(n p) c -> p n c", p=P)).then_inc(fold_loaded, 16)
            load_ctx(0)
            load_x(0)
            for dst, name in ((rep_raw, "c_rep"), (band[:], "c_band"), (maxrow_raw, "c_maxrow"),
                              (pick_raw, "c_pick"), (pick8_raw, "c_pick8"),
                              (first[:], "c_first")):
                sp.dma_start(dst, a[name]).then_inc(tables_loaded, 16)
            for dst, src in ((sim[:], a["sim"]), (gate[:], a["gates"].partition_broadcast(P)),
                             (ln0[:, 0], a["gamma0"].partition_broadcast(P)),
                             (ln0[:, 1], a["beta0"].partition_broadcast(P)),
                             (ln1[:, 0], a["gamma1"].partition_broadcast(P)),
                             (ln1[:, 1], a["beta1"].partition_broadcast(P)),
                             (w_att[:], a["w_att"]), (b_att[:], a["b_att"]), (w_r[:], a["w_r"]),
                             (b_r[:], a["b_r"].partition_broadcast(P)), (b1[:], a["b1"]),
                             (b2[0:NX], a["b2"]), (b2[NX:2 * NX], a["b2"]), (b2[2 * NX:3 * NX], a["b2"]),
                             (vz[:], a["c_vz"]), (vz_t[:], a["c_vzt"])):
                sp.dma_start(dst, src).then_inc(direct_loaded, 16)
            sp.dma_start(w1_raw[:], a["w1"]).then_inc(experts_loaded, 16)
            sp.dma_start(qk_w[:, :, 0:DH], a["q_proj"].rearrange("e c d -> c e d")).then_inc(gated_loaded, 16)
            sp.dma_start(qk_w[:, :, DH:], a["k_proj"].rearrange("e c d -> c e d")).then_inc(gated_loaded, 16)
            sp.dma_start(v_w[:], a["v_proj"].rearrange("e c d -> c e d")).then_inc(gated_loaded, 16)
            sp.dma_start(o_w[:], a["o_proj"].rearrange("(n w) d c -> (w d) n c", w=2)).then_inc(gated_loaded, 16)
            sp.wait_ge(pads_zeroed, 2)
            load_masks(0)

            def batch(b, more):
                sp.wait_ge(h_ready.sem, h_ready.after(b, 12))
                apart(sp)
                sp.dma_start(w2[:], a["w2"]).then_inc(w2_loaded.sem, 16)
                if more:
                    load_x(b + 1)
                    sp.wait_ge(h_ready.sem, h_ready.after(b, 16))
                    apart(sp)
                    load_ctx(b + 1)
                    load_masks(b + 1)
                sp.wait_ge(out_ready.sem, out_ready.after(b, 1))
                apart(sp)
                sp.dma_start(out[b].rearrange("(t p) c -> p t c", p=P), out_rows[:]).then_inc(out_stored.sem, 16)
                sp.wait_ge(out_stored.sem, out_stored.after(b, 16))
                apart(sp)

            with sp.Fori(0, B - 1) as b:
                batch(b, True)
            batch(B - 1, False)

        @block.gpsimd
        def _(pool):
            pool.memset(ctx_T[:, SK:KP], 0.0).then_inc(pads_zeroed, 1)
            pool.memset(maskT_i[:, 1, :], 0).then_inc(pads_zeroed, 1)

            def batch(b):
                steps = [0]

                def link(ins):
                    steps[0] += 1
                    ins.then_inc(pool_step.sem, 1)
                    pool.wait_ge(pool_step.sem, pool_step.after(b, steps[0]))

                pool.wait_ge(top_t_ready.sem, top_t_ready.after(b, 1))
                for g in range(NG):
                    pool.tensor_tensor(sc[:, g], sc[:, g], top_t[:], ALU.subtract).then_inc(less_pool.sem, 1)
                pool.wait_ge(top_m_ready.sem, top_m_ready.after(b, 1))
                for h in POOL_HEADS:
                    pool.tensor_tensor(sc[:, NG + h], sc[:, NG + h], top_m[:], ALU.subtract).then_inc(less_pool.sem, 1)
                pool.wait_ge(exp_ready.sem, exp_ready.after(b, NG))
                link(pool.tensor_tensor(top_t[:], sc[:, 0], sc[:, 1], ALU.add))
                link(pool.tensor_tensor(top_t[:], top_t[:], sc[:, 2], ALU.add))
                pool.tensor_tensor(top_t[:], top_t[:], sc[:, 3], ALU.add).then_inc(tail_sum.sem, 1)
                pool.wait_ge(exp_ready.sem, exp_ready.after(b, NG + H0))
                p0, p1, p2, p3 = (sc[:, NG + h] for h in POOL_HEADS)
                link(pool.tensor_tensor(den_p[:], p0, p1, ALU.add))
                link(pool.tensor_tensor(den_p[:], den_p[:], p2, ALU.add))
                pool.tensor_tensor(den_p[:], den_p[:], p3, ALU.add).then_inc(pool_sum.sem, 1)
                pool.wait_ge(inv_t_ready.sem, inv_t_ready.after(b, 1))
                for g in range(NG):
                    pool.tensor_tensor(sc[:, g], sc[:, g], top_t[:], ALU.mult).then_inc(attn_pool.sem, 1)
                pool.wait_ge(inv_m_ready.sem, inv_m_ready.after(b, 1))
                for h in POOL_HEADS:
                    pool.tensor_tensor(sc[:, NG + h], sc[:, NG + h], top_m[:], ALU.mult).then_inc(attn_pool.sem, 1)
                pool.wait_ge(mask_loaded.sem, mask_loaded.after(b, 96))
                pool.wait_ge(h_ready.sem, h_ready.after(b, 12))
                apart(pool)
                pool.tensor_scalar(mz[:], mask_i[:], 0.0, None, ALU.is_equal).then_inc(mz_ready.sem, 1)
                pool.tensor_scalar(mz_T[:], maskT_i[:], 0.0, None, ALU.is_equal).then_inc(mz_ready.sem, 1)
                assert steps[0] == POOL_STEPS

            with pool.Fori(0, B) as b:
                batch(b)

        @block.scalar
        def _(act):
            for n in range(8):
                act.wait_ge(fold_ready, n + 1)
                dst, scale = (mq, DK0 ** -0.5) if n < 4 else (mo, 1.0)
                h = FOLD_HEADS[n % 4]
                act.activation(dst[:, h:h + 7:2], bank[n].rearrange("p (h c) -> p h c", c=D), ACT.Copy,
                               scale=scale).then_inc(fold_stored, 1)
            act.wait_ge(direct_loaded, 16 * 16)
            act.activation(gate[:], gate[:], ACT.Exp, scale=-1.0).then_inc(set_act, 1)
            act.wait_ge(experts_loaded, 16)
            for n in range(4):
                act.activation(w1_hi[:, bass.ts(n, 1024)], w1_raw[:, bass.ts(n, 1024)], ACT.Copy).then_inc(set_act, 1)
            act.wait_ge(set_dve, 1)

            def batch(b):
                for n in range(6):
                    k = min(3, H0 - 3 * n)
                    act.wait_ge(g_psum.sem, g_psum.after(b, n + 1))
                    src = bank[1 + n % 3][:, 0:KP * k].rearrange("p (h c) -> p h c", c=KP)
                    act.activation(g_main(g_hi, 3 * n, k), src[:, :, 0:P], ACT.Copy)
                    act.activation(g_tail(g_hi, 3 * n, k), src[:, :, P:KP], ACT.Copy).then_inc(g_hi_ready.sem, 1)
                for n in range(5):
                    act.wait_ge(u_psum.sem, u_psum.after(b, n + 1))
                    dst = u_main[:, 4 * n:4 * n + 4] if n < 4 else u_tail[:]
                    act.activation(dst.rearrange("p h c -> p (h c)"), bank[1 + n % 3], ACT.Copy).then_inc(u_stored.sem, 1)
                act.wait_ge(hT_psum.sem, hT_psum.after(b, 1))
                act.activation(hT_hi[:], bank[0], ACT.Copy).then_inc(hT_hi_ready.sem, 1)
                for t in range(NG + H0):
                    act.wait_ge(sc_psum.sem, sc_psum.after(b, t + 1))
                    act.activation(sc[:, t], bank[1 + t % 3], ACT.Copy).then_inc(sc_stored.sem, 1)
                for g in range(NG):
                    act.wait_ge(less_pool.sem, less_pool.after(b, g + 1))
                    act.activation(sc[:, g], sc[:, g], ACT.Exp).then_inc(exp_ready.sem, 1)
                for h in MIXED:
                    if h in POOL_HEADS:
                        act.wait_ge(less_pool.sem, less_pool.after(b, NG + POOL_HEADS.index(h) + 1))
                    else:
                        act.wait_ge(less_dve.sem, less_dve.after(b, DVE_HEADS.index(h) + 1))
                    act.activation(sc[:, NG + h], sc[:, NG + h], ACT.Exp).then_inc(exp_ready.sem, 1)
                act.wait_ge(o_psum.sem, o_psum.after(b, 1))
                act.activation(oT[:], bank[0], ACT.Copy).then_inc(oT_stored.sem, 1)

                act.wait_ge(hT_psum.sem, hT_psum.after(b, 2))
                act.activation(hT[:], bank[0], ACT.Copy).then_inc(hT_full.sem, 1)
                act.wait_ge(gate_arg.sem, gate_arg.after(b, 1))
                act.activation(gated[:], gated[:], ACT.Exp).then_inc(gate_exp.sem, 1)
                act.wait_ge(rwT_psum.sem, rwT_psum.after(b, 1))
                act.activation(rwT[:], rwT_bank(2, 3 * NE), ACT.Copy).then_inc(rwT_stored.sem, 1)
                act.wait_ge(rh_used.sem, rh_used.after(b, NE))
                act.activation(q_T[:], bank[2][0:DH], ACT.Copy)
                act.activation(k_T[:], bank[2][DH:P], ACT.Copy)
                act.activation(v_T[:], bank[3][0:DH], ACT.Copy).then_inc(qkv_stored.sem, 1)
                act.wait_ge(v_psum.sem, v_psum.after(b, 1))
                act.activation(v_dup[:, :, 0], v_bank, ACT.Copy)
                act.activation(v_dup[:, :, 1], v_bank, ACT.Copy).then_inc(v_stored.sem, 1)
                for i in range(NT):
                    n = P * (i + 1)
                    act.wait_ge(s_max.sem, s_max.after(b, i + 1))
                    act.activation(pa[:, i, 0:n], bank[S_BANK[i]][:, 0:n], ACT.Exp, bias=col[:, 0, i:i + 1],
                                   scale=DH ** -0.5, accum_out=col[:, 1, i:i + 1]).then_inc(p_exp.sem, 1)
                for i in range(NT):
                    act.wait_ge(pT_psum.sem, pT_psum.after(b, i + 1))
                    act.activation(p_T[:, 0:i + 1, bass.ts(i, P)],
                                   bank[PT_BANK[i]][:, 0:P * (i + 1)].rearrange("p (j q) -> p j q", q=P),
                                   ACT.Copy).then_inc(pT_stored.sem, 1)
                act.wait_ge(att_psum.sem, att_psum.after(b, 1))
                act.activation(a_T[:], bank[1], ACT.Copy).then_inc(att_stored.sem, 1)
                act.wait_ge(o_psum.sem, o_psum.after(b, 2))
                act.activation(oT[:], bank[3], ACT.Copy).then_inc(oT_stored.sem, 1)

                act.wait_ge(hT_psum.sem, hT_psum.after(b, 3))
                act.activation(hT[:], bank[4], ACT.Copy).then_inc(hT_full.sem, 1)
                act.wait_ge(k_psum.sem, k_psum.after(b, 1))
                act.activation(kv_f[:], bank[5][:, 0:KP], ACT.Identity, bias=b_att[:, 1:2]).then_inc(k_full.sem, 1)
                act.wait_ge(k_full.sem, k_full.after(b, 1))
                act.activation(k_hi[:], kv_f[:], ACT.Copy).then_inc(k_hi_ready.sem, 1)
                act.wait_ge(v8_psum.sem, v8_psum.after(b, 1))
                act.activation(vz[:].rearrange("p (h c) -> p h c", c=VZP)[:, :, 0:DK1],
                               bank[7][:, 0:P].rearrange("p (h d) -> p h d", d=DK1), ACT.Copy)
                for j in range(4):
                    q = slice(32 * j, 32 * j + 32)
                    ins = act.activation(vzt_own[q, :, DK1 * j:DK1 * j + DK1],
                                         bank[7][q, P:2 * P].rearrange("p (g c) -> p g c", g=NG)[
                                             :, :, DK1 * j:DK1 * j + DK1], ACT.Copy)
                ins.then_inc(v8_stored.sem, 1)
                act.wait_ge(q_psum.sem, q_psum.after(b, 1))
                act.activation(qf[:], bank[5], ACT.Identity, bias=bq[:], scale=SCALE1).then_inc(qf_ready.sem, 1)
                act.wait_ge(ks_ready.sem, ks_ready.after(b, 4))
                act.activation(ks_t[:].rearrange("p g (j k) -> p g j k", j=4), ks[:, :, :, P:KP], ACT.Copy).then_inc(
                    kst_ready.sem, 1)
                act.wait_ge(q_masked.sem, q_masked.after(b, 1))
                act.activation(q_hi[:], qm[:], ACT.Copy).then_inc(q_hi_ready.sem, 1)
                for g in range(NG):
                    act.wait_ge(qrep_psum.sem, qrep_psum.after(b, g + 1))
                    act.activation(qs[0:96, g], bank[4 + g][0:96], ACT.Copy).then_inc(qs_ready.sem, 1)
                act.wait_ge(nmT_psum.sem, nmT_psum.after(b, 1))
                for g in range(NG):
                    ins = act.activation(qs[96:104, g], bank[4][32 * g:32 * g + 8], ACT.Copy)
                ins.then_inc(nm_stored.sem, 1)
                for t in range(NG + H1):
                    act.wait_ge(st_psum.sem, st_psum.after(b, t + 1))
                    if t >= 4:
                        act.wait_ge(pm_used.sem, pm_used.after(b, t - 3))
                    act.activation(pm[:, t % 4], bank[4 + t % 2], ACT.Exp).then_inc(pm_ready.sem, 1)
                act.wait_ge(o_psum.sem, o_psum.after(b, 3))
                act.activation(oT[:], bank[4], ACT.Identity, bias=bo[:]).then_inc(oT_stored.sem, 1)

                act.wait_ge(hT_psum.sem, hT_psum.after(b, 4))
                act.activation(hT[:], bank[4], ACT.Copy).then_inc(hT_full.sem, 1)
                act.activation(hT_hi[:], bank[4], ACT.Copy).then_inc(hT_hi_ready.sem, 1)
                act.wait_ge(gate_arg.sem, gate_arg.after(b, 2))
                act.activation(col[:, 1], col[:, 0], ACT.Exp).then_inc(gate_exp.sem, 1)
                act.wait_ge(rwT_psum.sem, rwT_psum.after(b, 2))
                act.activation(rwT[0:3 * NX], rwT_bank(6, 3 * NX), ACT.Copy).then_inc(rwT_stored.sem, 1)
                act.wait_ge(b2_psum.sem, b2_psum.after(b, 1))
                act.activation(acc[:], bank[7], ACT.Copy).then_inc(acc_begun.sem, 1)
                for e in range(NX):
                    for j in range(FC):
                        c = FC * e + j
                        act.wait_ge(l1_psum.sem, l1_psum.after(b, c + 1))
                        if c >= 4:
                            act.wait_ge(hid_used.sem, hid_used.after(b, c - 3))
                        act.activation(hid[:, c % 4], bank[4 + c % 2], ACT.Relu, bias=b1[:, c:c + 1]).then_inc(
                            hid_ready.sem, 1)
                    act.wait_ge(bc4_psum.sem, bc4_psum.after(b, e + 1))
                    if e >= 2:
                        act.wait_ge(ex_used.sem, ex_used.after(b, e - 1))
                    act.activation(rw_b[:, e % 2], bank[7], ACT.Copy).then_inc(rwb_stored.sem, 1)

            with act.Fori(0, B) as b:
                batch(b)

        @block.tensor
        def _(pe):
            pe.wait_ge(fold_loaded, 64)
            for n in range(8):
                for i in range(4):
                    h = FOLD_HEADS[n % 4] + 2 * i
                    q = slice(DK0 * (h % 2), DK0 * (h % 2) + DK0)
                    l, r = (wk_T, wq_T) if n < 4 else (wv_T, wo_n)
                    mm = pe.matmul(bank[n][:, bass.ts(i, P)], l[q, h // 2], r[q, h // 2], start=True, stop=True)
                mm.then_inc(fold_ready, 1)
            pe.wait_ge(fold_stored, 8)
            pe.wait_ge(set_ready, 1)
            pe.matmul(bank[0][:, 0:NE], ones_f, sim_sq, start=True, stop=True).then_inc(set_pe, 1)
            pe.matmul(bank[1][:, 0:1], w_att[:, 3], b_att[:, 2:3], start=True, stop=True).then_inc(set_pe, 1)
            pe.wait_ge(set_dve, 1)
            pe.wait_ge(pads_zeroed, 2)
            pe.wait_ge(gated_loaded, 64)

            def turn_in(b, n, dst):
                pe.wait_ge(h_ready.sem, h_ready.after(b, 4 * n))
                for i in range(NT):
                    mm = pe.transpose(dst[:, bass.ts(i, P)], h_rows[:, i], ident)
                mm.then_inc(hT_psum.sem, 1)

            def turn_back(b, n, src, dst):
                for i in range(NT):
                    mm = pe.transpose(dst[:, bass.ts(i, P)], src[:, bass.ts(i, P)], ident)
                mm.then_inc(back_psum.sem, 1)

            def split3(dst, hi, lo, m_hi, m_lo):
                pe.matmul(dst, hi, m_hi, start=True, stop=False)
                pe.matmul(dst, hi, m_lo, start=False, stop=False)
                return pe.matmul(dst, lo, m_hi, start=False, stop=True)

            def router(b, k, dst_lg, w, n, dst_rw):
                for i in range(NT):
                    mm = pe.matmul(dst_lg[:, n * i:n * i + n], hT[:, bass.ts(i, P)], w, start=True, stop=True)
                mm.then_inc(logit_psum.sem, 1)
                pe.wait_ge(rw_ready.sem, rw_ready.after(b, k))
                apart(pe)
                for i in range(NT):
                    mm = pe.transpose(dst_rw[:, bass.ts(i, P)], rw_parts[:, i, 0:3 * n], ident_b[:])
                mm.then_inc(rwT_psum.sem, 1)

            def batch(b):
                pe.wait_ge(ctx_loaded.sem, ctx_loaded.after(b, 16))
                for n in range(6):
                    if n >= 3:
                        pe.wait_ge(g_lo_ready.sem, g_lo_ready.after(b, n - 2))
                    for i in range(min(3, H0 - 3 * n)):
                        mm = pe.matmul(bank[1 + n % 3][:, KP * i:KP * i + KP], mq[:, 3 * n + i], ctx_T[:], start=True,
                                       stop=True)
                    mm.then_inc(g_psum.sem, 1)
                for n in range(5):
                    if n < 3:
                        pe.wait_ge(g_lo_ready.sem, g_lo_ready.after(b, n + 4))
                    else:
                        pe.wait_ge(u_stored.sem, u_stored.after(b, n - 2))
                    dst = bank[1 + n % 3]
                    if n < 4:
                        mm = pe.matmul(dst, ctx_T[:, 0:P], mo[:, 4 * n:4 * n + 4].rearrange("p h c -> p (h c)"),
                                       start=True, stop=True)
                    else:
                        for j in range(4):
                            mm = pe.matmul(dst[32 * j:32 * j + 32].rearrange("p (g c) -> p g c", g=NG),
                                           ctx_T[:, P:KP], mo[:].rearrange("p (g j) c -> p j g c", j=4)[:, j],
                                           start=True, stop=True, tile_position=(0, 32 * j))
                    mm.then_inc(u_psum.sem, 1)
                turn_in(b, 1, bank[0])
                pe.wait_ge(hT_lo_ready.sem, hT_lo_ready.after(b, 1))
                pe.wait_ge(u_stored.sem, u_stored.after(b, 5))
                for t in range(NG + H0):
                    if t >= 3:
                        pe.wait_ge(sc_stored.sem, sc_stored.after(b, t - 2))
                    at = H0 * P + t * P if t < NG else (t - NG) * P
                    hi, lo = (g[:, at:at + P] for g in (g_hi, g_lo))
                    split3(bank[1 + t % 3], hi, lo, hT_hi[:], hT_lo[:]).then_inc(sc_psum.sem, 1)
                pe.wait_ge(tail_max.sem, tail_max.after(b, 1))
                pe.matmul(bank[0], perm64, top_t[:], start=True, stop=True).then_inc(tail_turned.sem, 1)
                pe.wait_ge(tail_max.sem, tail_max.after(b, 2))
                pe.matmul(bank[0], perm32, top_t[:], start=True, stop=True).then_inc(tail_turned.sem, 1)
                pe.wait_ge(tail_sum.sem, tail_sum.after(b, 1))
                pe.matmul(bank[1], same, top_t[:], start=True, stop=True).then_inc(tail_den.sem, 1)
                for n, h in enumerate(MIXED):
                    if n % 4 == 0:
                        g = n // 4
                        pe.wait_ge(attn_pool.sem, attn_pool.after(b, g + 1))
                        pe.matmul(bank[0], u_tail[:, g], sc[:, g], start=(n == 0), stop=False)
                    if h in POOL_HEADS:
                        pe.wait_ge(attn_pool.sem, attn_pool.after(b, NG + POOL_HEADS.index(h) + 1))
                    else:
                        pe.wait_ge(attn_dve.sem, attn_dve.after(b, DVE_HEADS.index(h) + 1))
                    mm = pe.matmul(bank[0], u_main[:, h], sc[:, NG + h], start=False, stop=(n == H0 - 1))
                mm.then_inc(o_psum.sem, 1)
                pe.wait_ge(oT_stored.sem, oT_stored.after(b, 1))
                turn_back(b, 1, oT, bank[2])

                turn_in(b, 2, bank[0])
                pe.wait_ge(hT_full.sem, hT_full.after(b, 1))
                router(b, 1, bank[1], sim_n[:], NE, rwT_bank(2, 3 * NE))
                pe.wait_ge(rwT_stored.sem, rwT_stored.after(b, 1))

                def spread(table, n):
                    pe.matmul(bank[BC_BANK[n]], table, rwT[:], start=True, stop=True).then_inc(bc_psum.sem, 1)

                def spread_pair(n):
                    m = NE + n
                    pe.matmul(bank[BC_BANK[m]][0:DH], one(pick, 2 * n, DH), rwT[:], start=True, stop=True)
                    pe.matmul(bank[BC_BANK[m]][DH:P], one(pick, 2 * n + 1, DH), rwT[:], start=True,
                              stop=True).then_inc(bc_psum.sem, 1)

                spread(one(pick, 0), 0)
                spread(one(pick, 1), 1)
                for e in range(NE):
                    pe.wait_ge(rh_ready.sem, rh_ready.after(b, e + 1))
                    pe.matmul(bank[2], qk_w[:, e], rh[:, e % 3], start=(e == 0), stop=(e == NE - 1))
                    mm = pe.matmul(bank[3][0:DH], v_w[:, e], rh[:, e % 3], start=(e == 0), stop=(e == NE - 1))
                    mm.then_inc(rh_used.sem, 1)
                    if e + 2 < NE:
                        spread(one(pick, e + 2), e + 2)
                pe.wait_ge(qkv_stored.sem, qkv_stored.after(b, 1))
                apart(pe)
                for i in range(NT):
                    mm = pe.transpose(v_bank[:, i], v_T[:, bass.ts(i, P)], ident[0:DH, 0:DH])
                mm.then_inc(v_psum.sem, 1)
                for i in range(NT):
                    if i == 3:
                        pe.wait_ge(p_exp.sem, p_exp.after(b, 1))
                    dst = bank[S_BANK[i]]
                    pe.matmul(dst[:, 0:P * (i + 1)], q_T[:, bass.ts(i, P)], k_T[:, 0:P * (i + 1)], start=True,
                              stop=False)
                    pe.matmul(dst[:, bass.ts(i, P)], ident_b[:], causal_b[:], start=False, stop=True).then_inc(
                        s_psum.sem, 1)
                pe.wait_ge(v_stored.sem, v_stored.after(b, 1))
                for i in range(NT):
                    pe.wait_ge(p_norm.sem, p_norm.after(b, i + 1))
                    if i == 3:
                        pe.wait_ge(pT_stored.sem, pT_stored.after(b, 1))
                    for j in range(i + 1):
                        mm = pe.transpose(bank[PT_BANK[i]][:, bass.ts(j, P)], pa[:, i, bass.ts(j, P)], ident)
                    mm.then_inc(pT_psum.sem, 1)
                pe.wait_ge(pT_stored.sem, pT_stored.after(b, 4))
                for j in range(NT):
                    mm = pe.matmul(bank[1][:, P * j:S], v_dup[:, j].rearrange("p a d -> p (a d)"),
                                   p_T[:, j, P * j:S], start=(j == 0), stop=(j == NT - 1))
                mm.then_inc(att_psum.sem, 1)
                spread_pair(0)
                spread_pair(1)
                for n in range(NE // 2):
                    pe.wait_ge(rh_ready.sem, rh_ready.after(b, NE + n + 1))
                    mm = pe.matmul(bank[3], o_w[:, n], rh[:, (NE + n) % 3], start=(n == 0), stop=(n == NE // 2 - 1))
                    if n < NE // 2 - 1:
                        mm.then_inc(rh_used.sem, 1)
                    else:
                        mm.then_inc(o_psum.sem, 1)
                    if n + 2 < NE // 2:
                        spread_pair(n + 2)
                pe.wait_ge(oT_stored.sem, oT_stored.after(b, 2))
                turn_back(b, 2, oT, bank[1])

                pe.matmul(bank[5][:, 0:KP], w_att[:, 1], ctx_T[:], start=True, stop=True).then_inc(k_psum.sem, 1)
                pe.matmul(bank[7][:, 0:P], ctx_T[:, 0:P], w_att[:, 2], start=True, stop=True)
                for j in range(4):
                    mm = pe.matmul(bank[7][32 * j:32 * j + 32, P:2 * P], ctx_T[:, P:KP], w_att[:, 2], start=True,
                                   stop=True, tile_position=(0, 32 * j))
                mm.then_inc(v8_psum.sem, 1)
                turn_in(b, 3, bank[4])
                pe.wait_ge(k_lo_ready.sem, k_lo_ready.after(b, 1))
                for g in range(NG):
                    q = slice(32 * g, 32 * g + 32)
                    if g == 2:
                        pe.wait_ge(v8_stored.sem, v8_stored.after(b, 1))
                    if g == 3:
                        pe.wait_ge(hT_full.sem, hT_full.after(b, 2))
                    dst = bank[KREP_BANK[g]][:, 0:KP]
                    pe.matmul(dst, rep[q, 0], k_hi[q], start=True, stop=False)
                    pe.matmul(dst, rep[q, 1], k_lo[q], start=False, stop=True).then_inc(krep_psum.sem, 1)
                pe.wait_ge(ks_ready.sem, ks_ready.after(b, 4))
                pe.matmul(bank[5], w_att[:, 0], hT[:], start=True, stop=True).then_inc(q_psum.sem, 1)
                pe.wait_ge(mz_ready.sem, mz_ready.after(b, 2))
                pe.matmul(bank[6], ones_b[:], mz_T[:, 0], start=True, stop=False)
                pe.matmul(bank[6], ones_b[0:32], mz_T[0:32, 1], start=False, stop=True).then_inc(count_psum.sem, 1)
                pe.wait_ge(q_lo_ready.sem, q_lo_ready.after(b, 1))
                pe.wait_ge(v8_stored.sem, v8_stored.after(b, 1))
                for g in range(NG):
                    q = slice(32 * g, 32 * g + 32)
                    pe.matmul(bank[4 + g], rep[q, 2], q_hi[q], start=True, stop=False)
                    pe.matmul(bank[4 + g], rep[q, 3], q_lo[q], start=False, stop=True).then_inc(qrep_psum.sem, 1)
                pe.wait_ge(qs_ready.sem, qs_ready.after(b, 4))
                for i in range(NT):
                    for g in range(NG):
                        n = NG * i + g
                        if n >= 2:
                            pe.wait_ge(smax_used.sem, smax_used.after(b, n - 1))
                        for w in range(2):
                            dst = duo[n % 2][:, w, 0:2 * SK].rearrange("p (j k) -> p j k", j=2)
                            pe.matmul(dst, qs[0:96, g, bass.ts(i, P)], ks[0:96, g, 2 * w:2 * w + 2, 0:SK], start=True,
                                      stop=False)
                            mm = pe.matmul(dst, neg_b[:], mz[:, i].unsqueeze(1).to_broadcast([P, 2, SK]),
                                           start=False, stop=True)
                        mm.then_inc(smax_psum.sem, 1)
                pe.wait_ge(nm_ready.sem, nm_ready.after(b, 1))
                for i in range(NT):
                    mm = pe.transpose(bank[4][:, bass.ts(i, P)], nm[:, i].rearrange("p g c -> p (g c)"), ident)
                mm.then_inc(nmT_psum.sem, 1)
                pe.wait_ge(nm_stored.sem, nm_stored.after(b, 1))

                def scores_T(t):
                    g, j = ST_TILES[t]
                    if t >= 2:
                        pe.wait_ge(pm_ready.sem, pm_ready.after(b, t - 1))
                    keys = ks_t[:, g] if j is None else ks[:, g, j, 0:P]
                    pe.matmul(bank[4 + t % 2], keys, qs[:, g], start=True, stop=False)
                    pe.matmul(bank[4 + t % 2], neg_b[:], mz_T[:, int(j is None)], start=False, stop=True).then_inc(
                        st_psum.sem, 1)

                scores_T(0)
                scores_T(1)
                for t, (g, j) in enumerate(ST_TILES):
                    pe.wait_ge(pm_ready.sem, pm_ready.after(b, t + 1))
                    w = vz_t[:, P * g:P * g + P] if j is None else vz[:, P * (4 * g + j):P * (4 * g + j) + P]
                    mm = pe.matmul(bank[6 + g // 2], w, pm[:, t % 4], start=(t % 10 == 0), stop=(t % 10 == 9))
                    mm.then_inc(pm_used.sem, 1)
                    if t + 2 < NG + H1:
                        scores_T(t + 2)
                pe.wait_ge(pv_normed.sem, pv_normed.after(b, 1))
                pe.matmul(bank[4], w_att[:, 3], qf[:], start=True, stop=True).then_inc(o_psum.sem, 1)
                pe.wait_ge(oT_stored.sem, oT_stored.after(b, 3))
                turn_back(b, 3, oT, bank[5])

                turn_in(b, 4, bank[4])
                pe.wait_ge(hT_full.sem, hT_full.after(b, 3))
                router(b, 2, bank[5], w_r[:], NX, rwT_bank(6, 3 * NX))
                pe.wait_ge(rwT_stored.sem, rwT_stored.after(b, 2))
                for n in range(3):
                    mm = pe.matmul(bank[7], b2_parts[:, n], rwT[0:3 * NX], start=(n == 0), stop=(n == 2))
                mm.then_inc(b2_psum.sem, 1)
                pe.wait_ge(hT_lo_ready.sem, hT_lo_ready.after(b, 2))
                pe.wait_ge(w2_loaded.sem, w2_loaded.after(b, 16))

                def layer1(c):
                    if c >= 2:
                        pe.wait_ge(hid_ready.sem, hid_ready.after(b, c - 1))
                    w = bass.ts(c, P)
                    split3(bank[4 + c % 2], w1_hi[:, w], w1_lo[:, w], hT_hi[:], hT_lo[:]).then_inc(l1_psum.sem, 1)

                layer1(0)
                layer1(1)
                for c in range(NX * FC):
                    e, j = divmod(c, FC)
                    if j == 0:
                        if e == 0:
                            pe.wait_ge(acc_begun.sem, acc_begun.after(b, 1))
                        else:
                            pe.wait_ge(rwb_stored.sem, rwb_stored.after(b, e))
                            pe.wait_ge(ex_used.sem, ex_used.after(b, e))
                        pe.matmul(bank[7], one(pick8, e), rwT[0:3 * NX], start=True, stop=True).then_inc(bc4_psum.sem, 1)
                    pe.wait_ge(hid_ready.sem, hid_ready.after(b, c + 1))
                    mm = pe.matmul(bank[6], w2[:, c], hid[:, c % 4], start=(j == 0), stop=(j == FC - 1))
                    mm.then_inc(hid_used.sem, 1)
                    if c + 2 < NX * FC:
                        layer1(c + 2)
                pe.wait_ge(acc_done.sem, acc_done.after(b, 1))
                turn_back(b, 4, acc, bank[4])

            with pe.Fori(0, B) as b:
                batch(b)

        @block.vector
        def _(dve):
            def rsqrt(v, y, t, u, link):
                link(dve.tensor_scalar(t.bitcast(I32), v.bitcast(I32), 1, None, ALU.arith_shift_right))
                link(dve.tensor_scalar(y.bitcast(I32), t.bitcast(I32), -1.0, MAGIC, ALU.mult, ALU.add))
                for _ in range(3):
                    link(dve.scalar_tensor_tensor(t, y, -0.5, v, ALU.mult, ALU.mult))
                    link(dve.tensor_tensor(u, t, y, ALU.mult))
                    link(dve.scalar_tensor_tensor(y, u, 1.5, y, ALU.add, ALU.mult))

            done = [0]

            def set_link(ins):
                done[0] += 1
                ins.then_inc(set_step, 1)
                dve.wait_ge(set_step, done[0])

            dve.memset(ones_b[:], 1.0)
            dve.memset(ones_f, 1.0)
            dve.memset(nm[:], 0.0)
            dve.memset(qs[:].bitcast(F32), 0.0)
            dve.wait_ge(mats_loaded, 16)
            dve.tensor_copy(ident_b[:], ident)
            dve.tensor_scalar(causal_b[:], after_, -HUGE, None, ALU.mult)
            dve.tensor_scalar(neg_b[:], ident, NEG, None, ALU.mult)
            dve.wait_ge(tables_loaded, 16 * 6)
            dve.tensor_copy(rep[:], rep_raw)
            dve.tensor_copy(pick[:], pick_raw)
            dve.tensor_copy(pick8[:], pick8_raw)
            for g in range(NG):
                dve.tensor_copy(ks[96:P, g], maxrow_raw)
            dve.wait_ge(direct_loaded, 16 * 16)
            dve.tensor_scalar(bq[:], b_att[:, 0:1], SCALE1, None, ALU.mult)
            set_link(dve.tensor_copy(b2_parts[:, 0], b2[:]))
            set_link(dve.tensor_tensor(b2_rest[:, 0], b2[:], b2_parts[:, 0], ALU.subtract))
            set_link(dve.tensor_copy(b2_parts[:, 1], b2_rest[:, 0]))
            set_link(dve.tensor_tensor(b2_rest[:, 1], b2_rest[:, 0], b2_parts[:, 1], ALU.subtract))
            dve.tensor_copy(b2_parts[:, 2], b2_rest[:, 1])
            dve.tensor_tensor(sim_sq, sim[:], sim[:], ALU.mult).then_inc(set_ready, 1)
            dve.wait_ge(set_pe, 2)
            dve.tensor_tensor(bo[:], bank[1][:, 0:1], b_att[:, 3:4], ALU.add)
            set_link(dve.tensor_scalar(sim_ss, bank[0][:, 0:NE], 1e-24, None, ALU.max))
            rsqrt(sim_ss, sim_r, sim_t, sim_u, set_link)
            dve.tensor_tensor(sim_n[:], sim[:], sim_r, ALU.mult)
            dve.wait_ge(set_act, 1)
            set_link(dve.tensor_scalar(gate[:], gate[:], 1.0, None, ALU.add))
            dve.reciprocal(gate[:], gate[:])
            for n in range(4):
                w = bass.ts(n, 1024)
                dve.wait_ge(set_act, n + 2)
                ins = dve.tensor_tensor(w1_lo[:, w], w1_raw[:, w], w1_hi[:, w], ALU.subtract)
            ins.then_inc(set_dve, 1)

            def batch(b):
                steps = [0]

                def link(ins):
                    steps[0] += 1
                    ins.then_inc(dve_step.sem, 1)
                    dve.wait_ge(dve_step.sem, dve_step.after(b, steps[0]))

                def over_tokens(v, n):
                    return v.unsqueeze(2).to_broadcast([P, NT, n])

                def over_tiles(v, n):
                    return v.unsqueeze(1).to_broadcast([P, NT, n])

                def normalise(src, dst, k):
                    for t in range(NT):
                        ins = dve.bn_stats(stats[:, t], src[:, t])
                    link(ins)
                    apart(dve)
                    for t in range(NT):
                        ins = dve.bn_aggr(mv[:, t], stats[:, t])
                    link(ins)
                    link(dve.tensor_scalar(nv[:], mv[:, :, 1], LN_EPS, None, ALU.add))
                    rsqrt(nv[:], ny[:], nt_[:], nu[:], link)
                    for t in range(NT):
                        ins = dve.tensor_scalar(dst[:, t], src[:, t], mv[:, t, 0:1], ny[:, t:t + 1], ALU.subtract,
                                                ALU.mult)
                        if k is not None:
                            ins.then_inc(h_ready.sem, 1)
                    if k is None:
                        link(ins)
                    else:
                        dve.wait_ge(h_ready.sem, h_ready.after(b, 4 * k))

                def first_best(src, n, best, sel):
                    link(dve.tensor_reduce(best, src, AX.X, ALU.max))
                    link(dve.tensor_tensor(eq[:, :, 0:n], src, over_tokens(best, n), ALU.is_equal))
                    link(dve.tensor_tensor(pr[:, :, 0:n], eq[:, :, 0:n], first[:, :, 0:n], ALU.mult))
                    link(dve.tensor_reduce(col[:, 3], pr[:, :, 0:n], AX.X, ALU.max))
                    link(dve.tensor_tensor(sel, pr[:, :, 0:n], over_tokens(col[:, 3], n), ALU.is_equal))

                def best_two(n):
                    v, v2 = lg[:, :, 0:n], lg2[:, :, 0:n]
                    first_best(v, n, top[:, 0], s1[:, :, 0:n])
                    link(dve.scalar_tensor_tensor(v2, s1[:, :, 0:n], -HUGE, v, ALU.mult, ALU.add))
                    first_best(v2, n, top[:, 1], s2[:, :, 0:n])

                def split_weights(n):
                    w, rest = rw[:, :, 0:n], [rw_rest[:, k, :, 0:n] for k in range(2)]
                    part_of = [rw_parts[:, :, n * k:n * k + n] for k in range(3)]
                    link(dve.tensor_copy(part_of[0], w))
                    link(dve.tensor_tensor(rest[0], w, part_of[0], ALU.subtract))
                    link(dve.tensor_copy(part_of[1], rest[0]))
                    link(dve.tensor_tensor(rest[1], rest[0], part_of[1], ALU.subtract))
                    dve.tensor_copy(part_of[2], rest[1]).then_inc(rw_ready.sem, 1)

                dve.wait_ge(x_loaded.sem, x_loaded.after(b, 16))
                normalise(x_in, h_rows, 1)
                for n in range(6):
                    k = min(3, H0 - 3 * n)
                    dve.wait_ge(g_hi_ready.sem, g_hi_ready.after(b, n + 1))
                    src = bank[1 + n % 3][:, 0:KP * k].rearrange("p (h c) -> p h c", c=KP)
                    dve.tensor_tensor(g_main(g_lo, 3 * n, k), src[:, :, 0:P], g_main(g_hi, 3 * n, k), ALU.subtract)
                    dve.tensor_tensor(g_tail(g_lo, 3 * n, k), src[:, :, P:KP], g_tail(g_hi, 3 * n, k),
                                      ALU.subtract).then_inc(g_lo_ready.sem, 1)
                dve.wait_ge(hT_hi_ready.sem, hT_hi_ready.after(b, 1))
                dve.tensor_tensor(hT_lo[:], bank[0], hT_hi[:], ALU.subtract).then_inc(hT_lo_ready.sem, 1)
                dve.wait_ge(sc_stored.sem, sc_stored.after(b, 2))
                link(dve.tensor_tensor(top_t[:], sc[:, 0], sc[:, 1], ALU.max))
                dve.wait_ge(sc_stored.sem, sc_stored.after(b, 3))
                link(dve.tensor_tensor(top_t[:], top_t[:], sc[:, 2], ALU.max))
                dve.wait_ge(sc_stored.sem, sc_stored.after(b, 4))
                dve.tensor_tensor(top_t[:], top_t[:], sc[:, 3], ALU.max).then_inc(tail_max.sem, 1)
                for h in range(1, H0):
                    dve.wait_ge(sc_stored.sem, sc_stored.after(b, NG + h + 1))
                    ins = dve.tensor_tensor(top_m[:], sc[:, NG] if h == 1 else top_m[:], sc[:, NG + h], ALU.max)
                    if h < H0 - 1:
                        link(ins)
                    else:
                        ins.then_inc(top_m_ready.sem, 1)
                    if h in (12, 14):
                        n = h // 2 - 5
                        dve.wait_ge(tail_turned.sem, tail_turned.after(b, n))
                        dve.tensor_tensor(top_t[:], top_t[:], bank[0], ALU.max).then_inc(
                            (tail_max if n == 1 else top_t_ready).sem, 1)
                        if n == 1:
                            dve.wait_ge(tail_max.sem, tail_max.after(b, 2))
                dve.wait_ge(top_m_ready.sem, top_m_ready.after(b, 1))
                for h in DVE_HEADS:
                    dve.tensor_tensor(sc[:, NG + h], sc[:, NG + h], top_m[:], ALU.subtract).then_inc(less_dve.sem, 1)
                dve.wait_ge(less_pool.sem, less_pool.after(b, NG + len(POOL_HEADS)))
                dve.wait_ge(less_dve.sem, less_dve.after(b, len(DVE_HEADS)))
                last = None
                for n, h in enumerate(MIXED):
                    if h in POOL_HEADS:
                        continue
                    if last is None:
                        last = sc[:, NG + h]
                        continue
                    dve.wait_ge(exp_ready.sem, exp_ready.after(b, NG + n + 1))
                    link(dve.tensor_tensor(top_m[:], last, sc[:, NG + h], ALU.add))
                    last = top_m[:]
                    if n == 10:
                        dve.wait_ge(tail_den.sem, tail_den.after(b, 1))
                        dve.reciprocal(top_t[:], bank[1]).then_inc(inv_t_ready.sem, 1)
                dve.wait_ge(pool_sum.sem, pool_sum.after(b, 1))
                link(dve.tensor_tensor(top_m[:], top_m[:], den_p[:], ALU.add))
                dve.reciprocal(top_m[:], top_m[:]).then_inc(inv_m_ready.sem, 1)
                dve.wait_ge(inv_m_ready.sem, inv_m_ready.after(b, 1))
                for h in DVE_HEADS:
                    dve.tensor_tensor(sc[:, NG + h], sc[:, NG + h], top_m[:], ALU.mult).then_inc(attn_dve.sem, 1)
                dve.wait_ge(back_psum.sem, back_psum.after(b, 1))
                link(dve.tensor_tensor(y_rows[:], rows(bank[2]), h_rows[:], ALU.add))
                normalise(y_rows, y_rows, None)
                link(dve.tensor_tensor(y_rows[:], y_rows[:], over_tiles(ln0[:, 0], D), ALU.mult))
                link(dve.tensor_tensor(y_rows[:], y_rows[:], over_tiles(ln0[:, 1], D), ALU.add))
                link(dve.tensor_tensor(x_rows[:], y_rows[:], x_in[:], ALU.add))

                normalise(x_rows, h_rows, 2)
                link(dve.tensor_tensor(y_rows[:], h_rows[:], h_rows[:], ALU.mult))
                link(dve.tensor_reduce(nv[:], y_rows[:], AX.X, ALU.add))
                link(dve.tensor_scalar(nv[:], nv[:], 1e-24, None, ALU.max))
                rsqrt(nv[:], ny[:], nt_[:], nu[:], link)
                dve.wait_ge(logit_psum.sem, logit_psum.after(b, 1))
                link(dve.tensor_tensor(lg[:], bank[1][:, 0:NT * NE].rearrange("p (t e) -> p t e", e=NE),
                                       over_tokens(ny[:], NE), ALU.mult))
                link(dve.tensor_tensor(lg[:], lg[:], over_tiles(gate[:], NE), ALU.subtract))
                best_two(NE)
                dve.tensor_scalar(gated[:], lg[:], 0.0, None, ALU.max)
                link(dve.tensor_scalar(eq[:], lg[:], 0.0, None, ALU.is_gt))
                link(dve.tensor_tensor(s1[:], s1[:], s2[:], ALU.add))
                dve.tensor_reduce(top[:, 0], gated[:], AX.X, ALU.max)
                link(dve.tensor_reduce(col[:, 2], eq[:], AX.X, ALU.max))
                dve.tensor_tensor(gated[:], gated[:], over_tokens(top[:, 0], NE), ALU.subtract).then_inc(gate_arg.sem, 1)
                link(dve.tensor_scalar(col[:, 2], col[:, 2], -1.0, 1.0, ALU.mult, ALU.add))
                link(dve.tensor_tensor(s1[:], s1[:], over_tokens(col[:, 2], NE), ALU.mult))
                link(dve.tensor_tensor(s1[:], s1[:], eq[:], ALU.add))
                dve.wait_ge(gate_exp.sem, gate_exp.after(b, 1))
                link(dve.tensor_tensor(rw[:], gated[:], s1[:], ALU.mult))
                link(dve.tensor_reduce(top[:, 0], rw[:], AX.X, ALU.add))
                link(dve.reciprocal(top[:, 1], top[:, 0]))
                link(dve.tensor_tensor(rw[:], rw[:], over_tokens(top[:, 1], NE), ALU.mult))
                split_weights(NE)

                def weigh(m, src):
                    dve.wait_ge(bc_psum.sem, bc_psum.after(b, m + 1))
                    if m >= 3:
                        dve.wait_ge(rh_used.sem, rh_used.after(b, m - 2))
                    dve.tensor_tensor(rh[:, m % 3], src, bank[BC_BANK[m]], ALU.mult).then_inc(rh_ready.sem, 1)

                for e in range(NE):
                    weigh(e, hT[:])

                def row_max(i):
                    dve.wait_ge(s_psum.sem, s_psum.after(b, i + 1))
                    link(dve.tensor_reduce(col[:, 3, i:i + 1], bank[S_BANK[i]][:, 0:P * (i + 1)], AX.X, ALU.max))
                    dve.tensor_scalar(col[:, 0, i:i + 1], col[:, 3, i:i + 1], -(DH ** -0.5), None, ALU.mult).then_inc(
                        s_max.sem, 1)

                def row_norm(i):
                    dve.wait_ge(p_exp.sem, p_exp.after(b, i + 1))
                    link(dve.reciprocal(col[:, 2, i:i + 1], col[:, 1, i:i + 1]))
                    n = P * (i + 1)
                    dve.tensor_scalar(pa[:, i, 0:n], pa[:, i, 0:n], col[:, 2, i:i + 1], None, ALU.mult).then_inc(
                        p_norm.sem, 1)

                for i in range(3):
                    row_max(i)
                row_norm(0)
                row_max(3)
                for i in range(1, NT):
                    row_norm(i)
                dve.wait_ge(att_stored.sem, att_stored.after(b, 1))
                for n in range(NE // 2):
                    weigh(NE + n, a_T[:])
                dve.wait_ge(back_psum.sem, back_psum.after(b, 2))
                link(dve.tensor_tensor(x_rows[:], x_rows[:], rows(bank[1]), ALU.add))

                normalise(x_rows, h_rows, 3)
                dve.wait_ge(k_hi_ready.sem, k_hi_ready.after(b, 1))
                dve.tensor_tensor(k_lo[:], kv_f[:], k_hi[:], ALU.subtract).then_inc(k_lo_ready.sem, 1)
                for g in range(NG):
                    dve.wait_ge(krep_psum.sem, krep_psum.after(b, g + 1))
                    src = bank[KREP_BANK[g]][0:96, 0:KP]
                    dve.tensor_tensor(ks[0:96, g], src.unsqueeze(1).to_broadcast([96, 4, KP]),
                                      band[0:96].unsqueeze(2).to_broadcast([96, 4, KP]), ALU.mult).then_inc(
                                          ks_ready.sem, 1)
                dve.wait_ge(qf_ready.sem, qf_ready.after(b, 1))
                dve.wait_ge(count_psum.sem, count_psum.after(b, 1))
                dve.scalar_tensor_tensor(qm[:], bank[6], KP - 0.5, qf[:], ALU.is_lt, ALU.mult).then_inc(q_masked.sem, 1)
                dve.wait_ge(q_hi_ready.sem, q_hi_ready.after(b, 1))
                dve.tensor_tensor(q_lo[:], qm[:], q_hi[:], ALU.subtract).then_inc(q_lo_ready.sem, 1)
                for n in range(NT * NG):
                    i, g = divmod(n, NG)
                    dve.wait_ge(smax_psum.sem, smax_psum.after(b, n + 1))
                    dve.tensor_reduce(mx[:, i, 4 * g:4 * g + 4].rearrange("p (w j) -> p w j", w=2),
                                      duo[n % 2][:, :, 0:2 * SK].rearrange("p w (j k) -> p w j k", j=2),
                                      AX.X, ALU.max).then_inc(smax_used.sem, 1)
                dve.wait_ge(smax_used.sem, smax_used.after(b, NT * NG))
                m4 = mx[:].rearrange("p t (g j) -> p t g j", g=NG)
                link(dve.tensor_scalar(nm[:].bitcast(F32R)[:, :, :, 0:4], m4, -1.0, None, ALU.mult))
                dve.scalar_tensor_tensor(nm[:, :, :, 4:8], m4, -1.0, nm[:, :, :, 0:4], ALU.mult,
                                         ALU.subtract).then_inc(nm_ready.sem, 1)
                dve.wait_ge(pm_used.sem, pm_used.after(b, NG + H1))
                dve.reciprocal(rz[0:64], bank[6][64:P])
                link(dve.reciprocal(rz[64:P], bank[7][0:64]))
                dve.tensor_tensor(qf[0:64], bank[6][0:64], rz[0:64], ALU.mult)
                dve.tensor_tensor(qf[64:P], bank[7][64:P], rz[64:P], ALU.mult).then_inc(pv_normed.sem, 1)
                dve.wait_ge(back_psum.sem, back_psum.after(b, 3))
                link(dve.tensor_tensor(x_rows[:], x_rows[:], rows(bank[5]), ALU.add))

                normalise(x_rows, h_rows, 4)
                dve.wait_ge(hT_hi_ready.sem, hT_hi_ready.after(b, 2))
                dve.tensor_tensor(hT_lo[:], bank[4], hT_hi[:], ALU.subtract).then_inc(hT_lo_ready.sem, 1)
                dve.wait_ge(logit_psum.sem, logit_psum.after(b, 2))
                link(dve.tensor_tensor(lg[:, :, 0:NX], bank[5][:, 0:NT * NX].rearrange("p (t e) -> p t e", e=NX),
                                       over_tiles(b_r[:], NX), ALU.add))
                best_two(NX)
                dve.tensor_tensor(col[:, 0], top[:, 1], top[:, 0], ALU.subtract).then_inc(gate_arg.sem, 1)
                dve.wait_ge(gate_exp.sem, gate_exp.after(b, 2))
                link(dve.tensor_scalar(col[:, 2], col[:, 1], 1.0, None, ALU.add))
                link(dve.reciprocal(col[:, 3], col[:, 2]))
                link(dve.tensor_tensor(col[:, 2], col[:, 1], col[:, 3], ALU.mult))
                dve.tensor_tensor(s1[:, :, 0:NX], s1[:, :, 0:NX], over_tokens(col[:, 3], NX), ALU.mult)
                link(dve.tensor_tensor(s2[:, :, 0:NX], s2[:, :, 0:NX], over_tokens(col[:, 2], NX), ALU.mult))
                link(dve.tensor_tensor(rw[:, :, 0:NX], s1[:, :, 0:NX], s2[:, :, 0:NX], ALU.add))
                split_weights(NX)
                dve.wait_ge(acc_begun.sem, acc_begun.after(b, 1))
                for e in range(NX):
                    dve.wait_ge(rwb_stored.sem, rwb_stored.after(b, e + 1))
                    dve.wait_ge(hid_used.sem, hid_used.after(b, FC * (e + 1)))
                    dve.tensor_tensor(part[:], bank[6], rw_b[:, e % 2], ALU.mult).then_inc(ex_used.sem, 1)
                    dve.wait_ge(ex_used.sem, ex_used.after(b, e + 1))
                    ins = dve.tensor_tensor(acc[:], acc[:], part[:], ALU.add)
                    if e < NX - 1:
                        link(ins)
                    else:
                        ins.then_inc(acc_done.sem, 1)
                dve.wait_ge(back_psum.sem, back_psum.after(b, 4))
                link(dve.tensor_tensor(y_rows[:], rows(bank[4]), h_rows[:], ALU.add))
                normalise(y_rows, y_rows, None)
                link(dve.tensor_tensor(y_rows[:], y_rows[:], over_tiles(ln1[:, 0], D), ALU.mult))
                link(dve.tensor_tensor(y_rows[:], y_rows[:], over_tiles(ln1[:, 1], D), ALU.add))
                dve.tensor_tensor(out_rows[:], y_rows[:], x_rows[:], ALU.add).then_inc(out_ready.sem, 1)
                assert steps[0] == DVE_STEPS, steps

            with dve.Fori(0, B) as b:
                batch(b)


_SHAPES = ["x", "ctx_T", "mask", "mask_T", "wq_T", "wk_T", "wv_T", "wo", "gamma0", "beta0", "sim", "gates", "q_proj",
           "k_proj", "v_proj", "o_proj", "w_att", "b_att", "w_r", "b_r", "w1", "b1", "w2", "b2", "gamma1", "beta1"]


def kernel(x, ctx_1024, mask_BxSxS2_if1, L0_xattn_W_Q, L0_xattn_W_K, L0_xattn_W_V, L0_xattn_W_O, L0_xattn_ln_gamma,
           L0_xattn_ln_beta, L0_ffn_sim_matrix, L0_ffn_gates, L0_ffn_q_proj, L0_ffn_k_proj, L0_ffn_v_proj,
           L0_ffn_o_proj, L1_xattn_W0, L1_xattn_b0, L1_xattn_W1, L1_xattn_b1, L1_xattn_W2, L1_xattn_b2, L1_xattn_W3,
           L1_xattn_b3, L1_ffn_Wr, L1_ffn_br, L1_ffn_W1, L1_ffn_b1, L1_ffn_W2, L1_ffn_b2, L1_ffn_gamma, L1_ffn_beta):
    import concourse.bacc as bacc
    from concourse.bass_utils import run_bass_kernel_spmd

    arrays = {
        "x": x,
        "ctx_T": ctx_1024.transpose(0, 2, 1),
        "mask": mask_BxSxS2_if1,
        "mask_T": mask_BxSxS2_if1.transpose(0, 2, 1),
        "wq_T": L0_xattn_W_Q.T, "wk_T": L0_xattn_W_K.T, "wv_T": L0_xattn_W_V.T, "wo": L0_xattn_W_O,
        "gamma0": L0_xattn_ln_gamma, "beta0": L0_xattn_ln_beta,
        "sim": L0_ffn_sim_matrix, "gates": L0_ffn_gates,
        "q_proj": L0_ffn_q_proj, "k_proj": L0_ffn_k_proj, "v_proj": L0_ffn_v_proj, "o_proj": L0_ffn_o_proj,
        "w_att": np.stack([np.asarray(w).T for w in (L1_xattn_W0, L1_xattn_W1, L1_xattn_W2, L1_xattn_W3)], 1),
        "b_att": np.stack([np.asarray(w) for w in (L1_xattn_b0, L1_xattn_b1, L1_xattn_b2, L1_xattn_b3)], 1),
        "w_r": L1_ffn_Wr.T, "b_r": L1_ffn_br,
        "w1": L1_ffn_W1.transpose(2, 0, 1).reshape(D, NX * F),
        "b1": L1_ffn_b1.reshape(NX * FC, P).T,
        "w2": L1_ffn_W2.transpose(0, 2, 1).reshape(NX * FC, P, D).transpose(1, 0, 2),
        "b2": L1_ffn_b2, "gamma1": L1_ffn_gamma, "beta1": L1_ffn_beta,
    }
    arrays.update(constants())
    nc = bacc.Bacc("TRN2", target_bir_lowering=False, num_devices=1)
    sent, aps = {}, {}
    for name, value in arrays.items():
        value = np.ascontiguousarray(value)
        sent[f"in_{name}"] = value
        aps[name] = nc.dram_tensor(f"in_{name}", value.shape, mybir.dt.from_np(value.dtype),
                                   kind="ExternalInput").ap()
    out = nc.dram_tensor("out", (B, S, D), F32, kind="ExternalOutput").ap()
    program(nc, aps, out)
    result = run_bass_kernel_spmd(nc, [sent], core_ids=[0])
    return result.results[0]["out"]
```

```python
from contextlib import ExitStack

import numpy as np

import concourse.bass as bass
from concourse import mybir

ALU = mybir.AluOpType
ACT = mybir.ActivationFunctionType
AX = mybir.AxisListType
F32 = mybir.dt.float32
F32R = mybir.dt.float32r
BF16 = mybir.dt.bfloat16
I32 = mybir.dt.int32

B, S, D, SK = 4, 512, 128, 154
P = 128
NT = S // P
KT = 32
KP = P + KT
TAIL = SK - P
H0, DK0 = 16, 64
NE = 16
DH = 64
H1, DK1 = 16, 8
NG = 4
NX, F = 8, 512
FC = F // P
VZP = P + DK1
VTP = P + 4 * DK1
LN_EPS = 1e-5
NEG = -1e9
HUGE = 1e30
MAGIC = 1597463007.0
SCALE1 = float(DK1) ** -0.5


def constants():
    i = np.arange(P)
    eye = np.eye(P, dtype=np.float32)
    q, r = i // 32, i % 32
    perm64 = (i[:, None] == (i[None, :] + 64) % P)
    perm32 = (i[:, None] == (i[None, :] ^ 32))
    same = r[:, None] == r[None, :]
    after = i[None, :] > i[:, None]
    mats = np.stack([eye, perm64, perm32, same, after], 1).astype(np.float32)
    into = [[0, 2], [1], [0, 1], [2]]
    rep = np.zeros((P, 4, P), np.float32)
    for n, quads in enumerate(into):
        for z in quads:
            rep[i, n, 32 * z + r] = 1
    band = (r[:, None] // DK1 == np.arange(4)[None, :]).astype(np.float32)
    maxrow = np.zeros((32, 4, KP), np.float32)
    for j in range(4):
        maxrow[j, j] = maxrow[4 + j, j] = 1
    pick = np.tile(np.eye(NE, dtype=np.float32), (3, 1))
    pick8 = np.tile(np.eye(NX, dtype=np.float32), (3, 1))
    first = np.zeros((P, NT, NE), np.float32)
    first[:] = NE - np.arange(NE)
    vz = np.zeros((P, H1 * VZP), np.float32)
    vzt = np.zeros((P, NG * VTP), np.float32)
    for h in range(H1):
        at = 64 + DK1 * h if h < 8 else DK1 * (h - 8)
        vz[:, P * h + at:P * h + at + DK1] = 1
        g, j = divmod(h, 4)
        vzt[32 * j:32 * j + TAIL, P * g + at:P * g + at + DK1] = 1
    return {"c_mats": mats, "c_rep": rep, "c_band": band, "c_maxrow": maxrow, "c_pick": pick, 
            "c_pick8": pick8, "c_first": first, "c_vz": vz, "c_vzt": vzt}


DVE_STEPS, FIRST_STEPS, LAST_STEPS, POOL_STEPS = 160, 18, 26, 4


class Signal:

    def __init__(self, sem, per_batch):
        self.sem, self.per_batch = sem, per_batch

    def after(self, b, k):
        assert 1 <= k <= self.per_batch
        return b * self.per_batch + k


def program(nc, a, out):
    ctx = ExitStack()
    with ctx:
        def sb(name, shape, dt=F32):
            return ctx.enter_context(nc.sbuf_tensor(name, shape, dt))

        def sem(name):
            return ctx.enter_context(nc.semaphore(name))

        def sig(name, per_batch):
            return Signal(sem(name), per_batch)

        bank = [ctx.enter_context(nc.psum_tensor(f"bank{n}", [P, 512], F32)) for n in range(4)]
        duo = [ctx.enter_context(nc.psum_tensor(f"duo{n}", [P, 2, 512], F32)) for n in range(2)]
        bank += [duo[0][:, 0], duo[0][:, 1], duo[1][:, 0], duo[1][:, 1]]
        bank = [t[:] if n < 4 else t for n, t in enumerate(bank)]

        mats = sb("mats", [P, 5, P])
        ident, perm64, perm32, same, after_ = (mats[:, n, :] for n in range(5))
        ident_b = sb("ident_b", [P, P], BF16)
        causal_b = sb("causal_b", [P, P], BF16)
        neg_b = sb("neg_b", [P, P], BF16)
        ones_b = sb("ones_b", [P, P], BF16)
        rep = sb("rep", [P, 4, P], F32R)
        band = sb("band", [P, 4])
        pick = sb("pick", [3 * NE, NE], BF16)
        pick8 = sb("pick8", [3 * NX, NX], BF16)
        first = sb("first", [P, NT, NE])
        mq = sb("mq", [P, H0, P])
        mo = sb("mo", [P, H0, P])
        qk_w = sb("qk_w", [P, NE, 2 * DH])
        v_w = sb("v_w", [P, NE, DH])
        o_w = sb("o_w", [P, NE // 2, D])
        sim = sb("sim", [P, NE])
        sim_n = sb("sim_n", [P, NE])
        gate = sb("gate", [P, NE])
        ln0 = sb("ln0", [P, 2, D])
        w_att = sb("w_att", [P, 4, D])
        b_att = sb("b_att", [P, 4])
        bq = sb("bq", [P, 1])
        bo = sb("bo", [P, 1])
        w_r = sb("w_r", [P, NX])
        b_r = sb("b_r", [P, NX])
        w2 = sb("w2", [P, NX * FC, D])
        maxrow = sb("maxrow", [P, 4, KP], BF16)
        w1_hi = sb("w1_hi", [P, NX * F], F32R)
        w1_lo = sb("w1_lo", [P, NX * F], F32R)
        b1 = sb("b1", [P, NX * FC])
        b2 = sb("b2", [3 * NX, D])
        b2_parts = sb("b2_parts", [3 * NX, 3, D], BF16)
        ln1 = sb("ln1", [P, 2, D])
        vz = sb("vz", [P, H1 * VZP])
        vz_t = sb("vz_t", [P, NG * VTP])

        x_in = sb("x_in", [P, NT, D])
        h_rows = sb("h_rows", [P, NT, D])
        y_rows = sb("y_rows", [P, NT, D])
        x_rows = sb("x_rows", [P, NT, D])
        x4_rows = sb("x4_rows", [P, NT, D])
        h4_rows = sb("h4_rows", [P, NT, D])
        h4_hi = sb("h4_hi", [P, S], F32R)
        h4_lo = sb("h4_lo", [P, S], F32R)
        rw4T = sb("rw4T", [3 * NX, S], BF16)
        hid = sb("hid", [P, 3, S])
        rw_b = sb("rw_b", [P, 3, S])
        acc = sb("acc", [P, S])
        ctx_T = sb("ctx_T", [P, KP])

        hT = sb("hT", [P, S])
        hT_hi = sb("hT_hi", [P, S], F32R)
        hT_lo = sb("hT_lo", [P, S], F32R)
        oT = den_p = hT

        stats = sb("stats", [P, NT, 6])
        mv = sb("mv", [P, NT, 2])
        nv = sb("nv", [P, NT])
        ny = sb("ny", [P, NT])
        nt_ = sb("nt_", [P, NT])
        nu = sb("nu", [P, NT])
        lg = sb("lg", [P, NT, NE])
        lg2 = sb("lg2", [P, NT, NE])
        eq = sb("eq", [P, NT, NE])
        pr = sb("pr", [P, NT, NE])
        s1 = sb("s1", [P, NT, NE])
        s2 = sb("s2", [P, NT, NE])
        gated = sb("gated", [P, NT, NE])
        rw = sb("rw", [P, NT, NE])
        top = sb("top", [P, 2, NT])
        col = sb("col", [P, 4, NT])
        rw_parts = sb("rw_parts", [P, NT, 3 * NE], BF16)
        rw_rest = sb("rw_rest", [P, 2, NT, NE])
        rwT = sb("rwT", [3 * NE, S], BF16)

        def arena(*specs):
            with ExitStack() as own:
                return [own.enter_context(nc.sbuf_tensor(n, sh, dt)) for n, sh, dt in specs]

        cst, wq_T, wk_T, wv_T, wo_n, w1_raw = arena(
            ("cst", [P, 40 * P], F32), ("wq_T", [P, H0 // 2, D], F32), ("wk_T", [P, H0 // 2, D], F32),
            ("wv_T", [P, H0 // 2, D], F32), ("wo_n", [P, H0 // 2, D], F32), ("w1_raw", [P, NX * F], F32))
        rep_raw = cst[:, 0:4 * P].rearrange("p (n c) -> p n c", n=4)
        pick_raw = cst[0:3 * NE, 4 * P:4 * P + NE]
        pick8_raw = cst[0:3 * NX, 5 * P:5 * P + NX]
        maxrow_raw = cst[96:P, 28 * P:28 * P + 4 * KP].rearrange("p (j k) -> p j k", j=4)
        ones_f = cst[:, 36 * P:37 * P]
        sim_sq = cst[:, 37 * P:37 * P + NE]
        sim_ss = cst[:, 37 * P + 16:37 * P + 32]
        sim_t = cst[:, 37 * P + 32:37 * P + 48]
        sim_u = cst[:, 37 * P + 48:37 * P + 64]
        sim_r = cst[:, 37 * P + 64:37 * P + 80]
        b2_rest = cst[0:3 * NX, 38 * P:40 * P].rearrange("p (n c) -> p n c", n=2)
        g_hi, g_lo, sc, top_m = arena(
            ("g_hi", [P, H0 * KP], F32R), ("g_lo", [P, H0 * KP], F32R), ("sc", [P, NG + H0, S], F32),
            ("top_m", [P, S], F32))
        top_t = y_rows[:].rearrange("p t c -> p (t c)")
        u_main, u_tail = arena(("u_main", [P, H0, D], F32), ("u_tail", [P, NG, D], F32))
        rh, q_T, k_T, v_T, v_dup, pa, p_T, a_T = arena(
            ("rh", [P, 3, S], F32), ("q_T", [DH, S], F32), ("k_T", [DH, S], F32), ("v_T", [DH, S], F32),
            ("v_dup", [P, NT, 2, DH], F32), ("pa", [P, NT, S], F32), ("p_T", [P, NT, S], F32),
            ("a_T", [P, S], F32))
        ks_t, qm, q_hi, q_lo, pm, mz, mz_T, mx = arena(
            ("ks_t", [P, NG, P], F32R), ("qm", [P, S], F32),
            ("q_hi", [P, S], F32R), ("q_lo", [P, S], F32R), ("pm", [P, 4, S], F32),
            ("mz", [P, NT, SK], BF16), ("mz_T", [P, 2, S], BF16), ("mx", [P, NT, H1], F32))
        _, qf, rz = arena(("folded_keys", [P, 2 * H0 * KP], F32), ("qf", [P, S], F32), ("rz", [P, S], F32))
        _, g_f = arena(("first_scores", [P, 2 * H0 * KP + (NG + 10) * S], F32), ("g_f", [P, 6, 3 * KP], F32))
        _, ks, qs, nm, mask_i, maskT_i, kv_f, k_hi, k_lo = arena(
            ("gated_buffers", [P, 16 * S], F32), ("ks", [P, NG, 4, KP], F32R), ("qs", [P, NG, S], F32R),
            ("nm", [P, NT, NG, 32], F32), ("mask_i", [P, NT, SK], I32), ("maskT_i", [P, 2, S], I32),
            ("kv_f", [P, KP], F32), ("k_hi", [P, KP], F32R), ("k_lo", [P, KP], F32R))

        passed = sem("passed")
        mats_loaded, fold_loaded, tables_loaded, direct_loaded = (
            sem(n) for n in ("mats_loaded", "fold_loaded", "tables_loaded", "direct_loaded"))
        gated_loaded, experts_loaded, pads_zeroed = (
            sem(n) for n in ("gated_loaded", "experts_loaded", "pads_zeroed"))
        x_loaded, ctx_loaded, mask_loaded = sig("x_loaded", 16), sig("ctx_loaded", 16), sig("mask_loaded", 16 * 6)
        w2_loaded, out_ready, out_stored = sem("w2_loaded"), sig("out_ready", 1), sig("out_stored", 16)
        set_step, fold_ready, fold_stored, set_ready, set_act, set_pe, set_dve = (
            sem(n) for n in ("set_step", "fold_ready", "fold_stored", "set_ready", "set_act", "set_pe", "set_dve"))
        dve_step, first_step, last_step = (
            sig("dve_step", DVE_STEPS), sig("first_step", FIRST_STEPS), sig("last_step", LAST_STEPS))
        pool_step = sig("pool_step", POOL_STEPS)
        h1_ready, h1T_psum, h1T_hi_ready, h1T_lo_ready = (
            sig("h1_ready", 4), sig("h1T_psum", 1), sig("h1T_hi_ready", 1), sig("h1T_lo_ready", 1))
        h_ready, hT_psum, hT_full, h4T_hi_ready, h4T_lo_ready = (
            sig("h_ready", 12), sig("hT_psum", 3), sig("hT_full", 3), sig("h4T_hi_ready", 1), sig("h4T_lo_ready", 1))
        o_psum, oT_stored, back_psum = sig("o_psum", 3), sig("oT_stored", 3), sig("back_psum", 3)
        g_psum, g_stored, g_lo_ready = sig("g_psum", 6), sig("g_stored", 6), sig("g_lo_ready", 6)
        u_psum, u_stored = sig("u_psum", 5), sig("u_stored", 5)
        sc_psum, sc_stored = sig("sc_psum", 20), sig("sc_stored", 20)
        tail_max, tail_turned = sig("tail_max", 2), sig("tail_turned", 2)
        top_t_ready, top_m_ready = sig("top_t_ready", 1), sig("top_m_ready", 1)
        less_dve, less_pool, exp_ready = sig("less_dve", 12), sig("less_pool", 8), sig("exp_ready", 20)
        tail_sum, pool_sum, tail_den = sig("tail_sum", 1), sig("pool_sum", 1), sig("tail_den", 1)
        inv_t_ready, inv_m_ready = sig("inv_t_ready", 1), sig("inv_m_ready", 1)
        attn_dve, attn_pool = sig("attn_dve", 12), sig("attn_pool", 8)
        logit_psum, gate_arg, gate_exp = sig("logit_psum", 2), sig("gate_arg", 2), sig("gate_exp", 2)
        rw_ready, rwT_psum, rwT_stored = sig("rw_ready", 2), sig("rwT_psum", 2), sig("rwT_stored", 2)
        bc_psum, rh_ready, rh_used = sig("bc_psum", 24), sig("rh_ready", 24), sig("rh_used", 23)
        qkv_stored, v_psum, v_stored = (
            sig("qkv_stored", 1), sig("v_psum", 1), sig("v_stored", 1))
        s_psum, s_max, p_exp, p_norm = sig("s_psum", 4), sig("s_max", 4), sig("p_exp", 4), sig("p_norm", 4)
        pT_psum, pT_stored, att_psum, att_stored = (
            sig("pT_psum", 4), sig("pT_stored", 4), sig("att_psum", 1), sig("att_stored", 1))
        mz_ready, k_psum, k_full, k_hi_ready, k_lo_ready = (
            sig("mz_ready", 2), sig("k_psum", 1), sig("k_full", 1), sig("k_hi_ready", 1), sig("k_lo_ready", 1))
        mask_padded, fixed_ready = sig("mask_padded", 1), sig("fixed_ready", 3)
        krep_psum, ks_ready, kst_ready, v8_psum, v8_stored = (
            sig("krep_psum", 4), sig("ks_ready", 4), sig("kst_ready", 1), sig("v8_psum", 1), sig("v8_stored", 1))
        q_psum, qf_ready, count_psum, q_masked, q_hi_ready, q_lo_ready = (
            sig("q_psum", 1), sig("qf_ready", 1), sig("count_psum", 1), sig("q_masked", 1), sig("q_hi_ready", 1),
            sig("q_lo_ready", 1))
        qrep_psum, qs_ready, smax_psum, smax_used = (
            sig("qrep_psum", 4), sig("qs_ready", 4), sig("smax_psum", 16), sig("smax_used", 16))
        nm_ready, nmT_psum, nm_stored = sig("nm_ready", 1), sig("nmT_psum", 1), sig("nm_stored", 1)
        st_psum, pm_ready, pm_used = sig("st_psum", 20), sig("pm_ready", 20), sig("pm_used", 20)
        pv_normed = sig("pv_normed", 1)
        item_psum, item_stored = sig("item_psum", NX + NX * FC), sig("item_stored", NX + NX * FC)
        hid_used, ex_added = sig("hid_used", NX * FC), sig("ex_added", NX)
        b2_psum, acc_begun, back4_psum = sig("b2_psum", 1), sig("acc_begun", 1), sig("back4_psum", 1)

        POOL_HEADS = [12, 13, 14, 15]
        DVE_HEADS = [h for h in range(H0) if h not in POOL_HEADS]
        MIXED = [0, 1, 12, 2, 3, 13, 4, 5, 14, 6, 7, 15, 8, 9, 10, 11]

        EARLY_MAX = 3
        FRONT_BANK = [5, 1, 2]
        FOLD_HEADS = [0, 1, 8, 9]
        S_BANK, PT_BANK = [1, 2, 3, 1], [0, 2, 3, 0]
        BC_BANK = [0, 1] * (NE // 2) + [0, 2] * (NE // 4)
        KREP_BANK = [2, 0, 1, 3]
        ST_TILES = [(0, None), (1, None)] + [(h // 4, h % 4) for h in range(8)] + \
            [(2, None), (3, None)] + [(h // 4, h % 4) for h in range(8, H1)]
        v_bank = bank[0][:, 0:NT * DH].rearrange("p (i d) -> p i d", d=DH)
        vzt_own = vz_t[:].rearrange("p (g c) -> p g c", c=VTP)

        def weight_item(e):
            return (FC + 1) * e

        def hidden_item(c):
            return c + c // FC + 1

        def rwT_bank(n, rows_):
            return bank[n].bitcast(BF16)[0:rows_, 0:S]

        def apart(eng):
            eng.sem_inc(passed, 1)

        def one(table, e, n=P):
            return table[:, e:e + 1].to_broadcast([table.shape[0], n])

        def g_main(t, h, k):
            return t[:, h * P:(h + k) * P].rearrange("p (h c) -> p h c", c=P)

        def g_tail(t, h, k):
            at = H0 * P + h * KT
            return t[:, at:at + k * KT].rearrange("p (h c) -> p h c", c=KT)

        def rows(t):
            return t.rearrange("p (t c) -> p t c", c=D)

        block = ctx.enter_context(nc.Block())

        @block.sync
        def _(sp):
            def load_x(b):
                sp.dma_start(x_in[:], a["x"][b].rearrange("(t p) c -> p t c", p=P)).then_inc(x_loaded.sem, 16)

            def load_ctx(b):
                sp.dma_start(ctx_T[:, 0:SK], a["ctx_T"][b]).then_inc(ctx_loaded.sem, 16)

            def load_masks(b):
                sp.dma_start(mask_i[:], a["mask"][b].rearrange("(t p) k -> p t k", p=P)).then_inc(mask_loaded.sem, 16)
                sp.dma_start(maskT_i[:, 0, :], a["mask_T"][b][0:P, :]).then_inc(mask_loaded.sem, 16)
                for j in range(4):
                    sp.dma_start(maskT_i[32 * j:32 * j + TAIL, 1, :], a["mask_T"][b][P:SK, :]).then_inc(
                        mask_loaded.sem, 16)

            sp.dma_start(mats[:], a["c_mats"]).then_inc(mats_loaded, 16)
            for dst, name in ((wk_T, "wk_T"), (wq_T, "wq_T"), (wv_T, "wv_T"), (wo_n, "wo")):
                sp.dma_start(dst[:], a[name].rearrange("(n p) c -> p n c", p=P)).then_inc(fold_loaded, 16)
            load_ctx(0)
            load_x(0)
            for dst, name in ((rep_raw, "c_rep"), (band[:], "c_band"), (maxrow_raw, "c_maxrow"),
                              (pick_raw, "c_pick"), (pick8_raw, "c_pick8"),
                              (first[:], "c_first")):
                sp.dma_start(dst, a[name]).then_inc(tables_loaded, 16)
            for dst, src in ((sim[:], a["sim"]), (gate[:], a["gates"].partition_broadcast(P)),
                             (ln0[:, 0], a["gamma0"].partition_broadcast(P)),
                             (ln0[:, 1], a["beta0"].partition_broadcast(P)),
                             (ln1[:, 0], a["gamma1"].partition_broadcast(P)),
                             (ln1[:, 1], a["beta1"].partition_broadcast(P)),
                             (w_att[:], a["w_att"]), (b_att[:], a["b_att"]), (w_r[:], a["w_r"]),
                             (b_r[:], a["b_r"].partition_broadcast(P)), (b1[:], a["b1"]),
                             (b2[0:NX], a["b2"]), (b2[NX:2 * NX], a["b2"]), (b2[2 * NX:3 * NX], a["b2"]),
                             (vz[:], a["c_vz"]), (vz_t[:], a["c_vzt"])):
                sp.dma_start(dst, src).then_inc(direct_loaded, 16)
            sp.dma_start(w1_raw[:], a["w1"]).then_inc(experts_loaded, 16)
            sp.dma_start(qk_w[:, :, 0:DH], a["q_proj"].rearrange("e c d -> c e d")).then_inc(gated_loaded, 16)
            sp.dma_start(qk_w[:, :, DH:], a["k_proj"].rearrange("e c d -> c e d")).then_inc(gated_loaded, 16)
            sp.dma_start(v_w[:], a["v_proj"].rearrange("e c d -> c e d")).then_inc(gated_loaded, 16)
            sp.dma_start(o_w[:], a["o_proj"].rearrange("(n w) d c -> (w d) n c", w=2)).then_inc(gated_loaded, 16)
            sp.dma_start(w2[:], a["w2"]).then_inc(w2_loaded, 16)

            def batch(b, more):
                sp.wait_ge(mask_padded.sem, mask_padded.after(b, 1))
                apart(sp)
                load_masks(b)
                if more:
                    sp.wait_ge(h_ready.sem, h_ready.after(b, 4))
                    apart(sp)
                    load_x(b + 1)
                    sp.wait_ge(v8_stored.sem, v8_stored.after(b, 1))
                    sp.wait_ge(k_full.sem, k_full.after(b, 1))
                    apart(sp)
                    load_ctx(b + 1)

            def store(b):
                sp.wait_ge(out_ready.sem, out_ready.after(b, 1))
                apart(sp)
                sp.dma_start(out[b].rearrange("(t p) c -> p t c", p=P), x4_rows[:]).then_inc(out_stored.sem, 16)
                sp.wait_ge(out_stored.sem, out_stored.after(b, 16))
                apart(sp)

            batch(0, True)
            with sp.Fori(1, B - 1) as b:
                batch(b, True)
                store(b - 1)
            batch(B - 1, False)
            store(B - 2)
            store(B - 1)

        @block.gpsimd
        def _(pool):
            pool.memset(ctx_T[:, SK:KP], 0.0).then_inc(pads_zeroed, 1)

            def batch(b):
                steps = [0]

                def link(ins):
                    steps[0] += 1
                    ins.then_inc(pool_step.sem, 1)
                    pool.wait_ge(pool_step.sem, pool_step.after(b, steps[0]))

                pool.wait_ge(top_t_ready.sem, top_t_ready.after(b, 1))
                for g in range(NG):
                    pool.tensor_tensor(sc[:, g], sc[:, g], top_t[:], ALU.subtract).then_inc(less_pool.sem, 1)
                pool.wait_ge(top_m_ready.sem, top_m_ready.after(b, 1))
                for h in POOL_HEADS:
                    pool.tensor_tensor(sc[:, NG + h], sc[:, NG + h], top_m[:], ALU.subtract).then_inc(less_pool.sem, 1)
                pool.wait_ge(exp_ready.sem, exp_ready.after(b, NG))
                link(pool.tensor_tensor(top_t[:], sc[:, 0], sc[:, 1], ALU.add))
                link(pool.tensor_tensor(top_t[:], top_t[:], sc[:, 2], ALU.add))
                pool.tensor_tensor(top_t[:], top_t[:], sc[:, 3], ALU.add).then_inc(tail_sum.sem, 1)
                p0, p1, p2, p3 = (sc[:, NG + h] for h in POOL_HEADS)
                p_ready = [NG + MIXED.index(h) + 1 for h in POOL_HEADS]
                pool.wait_ge(exp_ready.sem, exp_ready.after(b, p_ready[1]))
                link(pool.tensor_tensor(den_p[:], p0, p1, ALU.add))
                pool.wait_ge(exp_ready.sem, exp_ready.after(b, p_ready[2]))
                link(pool.tensor_tensor(den_p[:], den_p[:], p2, ALU.add))
                pool.wait_ge(exp_ready.sem, exp_ready.after(b, p_ready[3]))
                pool.tensor_tensor(den_p[:], den_p[:], p3, ALU.add).then_inc(pool_sum.sem, 1)
                pool.wait_ge(inv_m_ready.sem, inv_m_ready.after(b, 1))
                for h in POOL_HEADS:
                    pool.tensor_tensor(sc[:, NG + h], sc[:, NG + h], top_m[:], ALU.mult).then_inc(attn_pool.sem, 1)
                pool.wait_ge(inv_t_ready.sem, inv_t_ready.after(b, 1))
                for g in range(NG):
                    pool.tensor_tensor(sc[:, g], sc[:, g], top_t[:], ALU.mult).then_inc(attn_pool.sem, 1)
                pool.wait_ge(h_ready.sem, h_ready.after(b, 4))
                apart(pool)
                pool.memset(maskT_i[:, 1, :], 0).then_inc(mask_padded.sem, 1)
                pool.wait_ge(mask_padded.sem, mask_padded.after(b, 1))
                apart(pool)
                pool.memset(nm[:], 0.0).then_inc(fixed_ready.sem, 1)
                pool.wait_ge(fixed_ready.sem, fixed_ready.after(b, 1))
                apart(pool)
                pool.memset(qs[96:P].bitcast(F32), 0.0).then_inc(fixed_ready.sem, 1)
                pool.wait_ge(fixed_ready.sem, fixed_ready.after(b, 2))
                apart(pool)
                pool.tensor_copy(ks[96:P], maxrow[96:P].unsqueeze(1).to_broadcast([32, NG, 4, KP])).then_inc(
                    fixed_ready.sem, 1)
                pool.wait_ge(fixed_ready.sem, fixed_ready.after(b, 3))
                pool.wait_ge(mask_loaded.sem, mask_loaded.after(b, 96))
                pool.wait_ge(h_ready.sem, h_ready.after(b, 8))
                apart(pool)
                pool.tensor_scalar(mz[:], mask_i[:], 0.0, None, ALU.is_equal).then_inc(mz_ready.sem, 1)
                pool.tensor_scalar(mz_T[:], maskT_i[:], 0.0, None, ALU.is_equal).then_inc(mz_ready.sem, 1)
                assert steps[0] == POOL_STEPS

            def low_keys(b):
                for n in range(6):
                    k = min(3, H0 - 3 * n)
                    pool.wait_ge(g_stored.sem, g_stored.after(b, n + 1))
                    src = g_f[:, n, 0:KP * k].rearrange("p (h c) -> p h c", c=KP)
                    pool.tensor_tensor(g_main(g_lo, 3 * n, k), src[:, :, 0:P], g_main(g_hi, 3 * n, k), ALU.subtract)
                    pool.tensor_tensor(g_tail(g_lo, 3 * n, k), src[:, :, P:KP], g_tail(g_hi, 3 * n, k),
                                       ALU.subtract).then_inc(g_lo_ready.sem, 1)

            low_keys(0)
            with pool.Fori(0, B - 1) as b:
                batch(b)
                low_keys(b + 1)
            batch(B - 1)

        @block.scalar
        def _(act):
            for n in range(8):
                act.wait_ge(fold_ready, n + 1)
                dst, scale = (mq, DK0 ** -0.5) if n < 4 else (mo, 1.0)
                h = FOLD_HEADS[n % 4]
                act.activation(dst[:, h:h + 7:2], bank[n].rearrange("p (h c) -> p h c", c=D), ACT.Copy,
                               scale=scale).then_inc(fold_stored, 1)
            act.wait_ge(direct_loaded, 16 * 16)
            act.activation(gate[:], gate[:], ACT.Exp, scale=-1.0).then_inc(set_act, 1)
            act.wait_ge(experts_loaded, 16)
            for n in range(4):
                act.activation(w1_hi[:, bass.ts(n, 1024)], w1_raw[:, bass.ts(n, 1024)], ACT.Copy).then_inc(set_act, 1)
            act.wait_ge(set_dve, 1)

            def expert_items(b, c0, c1):
                for c in range(c0, c1):
                    e, j = divmod(c, FC)
                    if j == 0:
                        act.wait_ge(item_psum.sem, item_psum.after(b, weight_item(e) + 1))
                        if e >= 3:
                            act.wait_ge(ex_added.sem, ex_added.after(b, e - 2))
                        act.activation(rw_b[:, e % 3], bank[4 + weight_item(e) % 2], ACT.Copy).then_inc(
                            item_stored.sem, 1)
                    act.wait_ge(item_psum.sem, item_psum.after(b, hidden_item(c) + 1))
                    if c >= 3:
                        act.wait_ge(hid_used.sem, hid_used.after(b, c - 2))
                    act.activation(hid[:, c % 3], bank[4 + hidden_item(c) % 2], ACT.Relu, bias=b1[:, c:c + 1]).then_inc(
                        item_stored.sem, 1)

            def store_h1T(b):
                act.wait_ge(h1T_psum.sem, h1T_psum.after(b, 1))
                act.activation(hT_hi[:], bank[4], ACT.Copy).then_inc(h1T_hi_ready.sem, 1)

            def store_keys(b, *jobs):
                for n in jobs:
                    k = min(3, H0 - 3 * n)
                    act.wait_ge(g_psum.sem, g_psum.after(b, n + 1))
                    src = bank[FRONT_BANK[n % 3]][:, 0:KP * k]
                    own = src.rearrange("p (h c) -> p h c", c=KP)
                    act.activation(g_main(g_hi, 3 * n, k), own[:, :, 0:P], ACT.Copy)
                    act.activation(g_tail(g_hi, 3 * n, k), own[:, :, P:KP], ACT.Copy)
                    act.activation(g_f[:, n, 0:KP * k], src, ACT.Copy).then_inc(g_stored.sem, 1)

            def store_scores(b, t0, t1):
                for t in range(t0, t1):
                    act.wait_ge(sc_psum.sem, sc_psum.after(b, t + 1))
                    act.activation(sc[:, t], bank[FRONT_BANK[t % 3]], ACT.Copy).then_inc(sc_stored.sem, 1)

            def batch(b, behind=True, more=True):
                def items(c0, c1):
                    if behind:
                        expert_items(b - 1, c0, c1)

                items(0, 2)

                def store_values(n):
                    act.wait_ge(u_psum.sem, u_psum.after(b, n + 1))
                    dst = u_main[:, 4 * n:4 * n + 4] if n < 4 else u_tail[:]
                    act.activation(dst.rearrange("p h c -> p (h c)"), bank[1 + n % 3], ACT.Copy).then_inc(u_stored.sem, 1)

                for n in range(5):
                    store_values(n)
                for g in range(NG):
                    act.wait_ge(less_pool.sem, less_pool.after(b, g + 1))
                    act.activation(sc[:, g], sc[:, g], ACT.Exp).then_inc(exp_ready.sem, 1)
                for n, h in enumerate(MIXED):
                    if h in POOL_HEADS:
                        act.wait_ge(less_pool.sem, less_pool.after(b, NG + POOL_HEADS.index(h) + 1))
                    else:
                        act.wait_ge(less_dve.sem, less_dve.after(b, DVE_HEADS.index(h) + 1))
                    act.activation(sc[:, NG + h], sc[:, NG + h], ACT.Exp).then_inc(exp_ready.sem, 1)
                    if n % 3 == 2:
                        items(2 + n // 3, 3 + n // 3)
                items(7, 12)
                act.wait_ge(o_psum.sem, o_psum.after(b, 1))
                act.activation(oT[:], bank[0], ACT.Copy).then_inc(oT_stored.sem, 1)
                items(12, 20)

                act.wait_ge(hT_psum.sem, hT_psum.after(b, 1))
                act.activation(hT[:], bank[0], ACT.Copy).then_inc(hT_full.sem, 1)
                items(20, 23)
                act.wait_ge(gate_arg.sem, gate_arg.after(b, 1))
                act.activation(gated[:], gated[:], ACT.Exp).then_inc(gate_exp.sem, 1)
                items(23, 26)
                act.wait_ge(rwT_psum.sem, rwT_psum.after(b, 1))
                act.activation(rwT[:], rwT_bank(2, 3 * NE), ACT.Copy).then_inc(rwT_stored.sem, 1)
                act.wait_ge(rh_used.sem, rh_used.after(b, NE))
                act.activation(q_T[:], bank[2][0:DH], ACT.Copy)
                act.activation(k_T[:], bank[2][DH:P], ACT.Copy)
                act.activation(v_T[:], bank[3][0:DH], ACT.Copy).then_inc(qkv_stored.sem, 1)
                act.wait_ge(v_psum.sem, v_psum.after(b, 1))
                act.activation(v_dup[:, :, 0], v_bank, ACT.Copy)
                act.activation(v_dup[:, :, 1], v_bank, ACT.Copy).then_inc(v_stored.sem, 1)
                items(26, 27)
                for i in range(NT):
                    n = P * (i + 1)
                    act.wait_ge(s_max.sem, s_max.after(b, i + 1))
                    act.activation(pa[:, i, 0:n], bank[S_BANK[i]][:, 0:n], ACT.Exp, bias=col[:, 0, i:i + 1],
                                   scale=DH ** -0.5, accum_out=col[:, 1, i:i + 1]).then_inc(p_exp.sem, 1)
                items(27, 28)
                for i in range(NT):
                    act.wait_ge(pT_psum.sem, pT_psum.after(b, i + 1))
                    act.activation(p_T[:, 0:i + 1, bass.ts(i, P)],
                                   bank[PT_BANK[i]][:, 0:P * (i + 1)].rearrange("p (j q) -> p j q", q=P),
                                   ACT.Copy).then_inc(pT_stored.sem, 1)
                act.wait_ge(att_psum.sem, att_psum.after(b, 1))
                act.activation(a_T[:], bank[1], ACT.Copy).then_inc(att_stored.sem, 1)
                act.wait_ge(o_psum.sem, o_psum.after(b, 2))
                act.activation(oT[:], bank[3], ACT.Copy).then_inc(oT_stored.sem, 1)

                act.wait_ge(k_psum.sem, k_psum.after(b, 1))
                act.activation(kv_f[:], bank[2][:, 0:KP], ACT.Identity, bias=b_att[:, 1:2]).then_inc(k_full.sem, 1)
                act.wait_ge(k_full.sem, k_full.after(b, 1))
                act.activation(k_hi[:], kv_f[:], ACT.Copy).then_inc(k_hi_ready.sem, 1)
                act.wait_ge(v8_psum.sem, v8_psum.after(b, 1))
                act.activation(vz[:].rearrange("p (h c) -> p h c", c=VZP)[:, :, 0:DK1],
                               bank[0][:, 0:P].rearrange("p (h d) -> p h d", d=DK1), ACT.Copy)
                for j in range(4):
                    q = slice(32 * j, 32 * j + 32)
                    ins = act.activation(vzt_own[q, :, DK1 * j:DK1 * j + DK1],
                                         bank[0][q, P:2 * P].rearrange("p (g c) -> p g c", g=NG)[
                                             :, :, DK1 * j:DK1 * j + DK1], ACT.Copy)
                ins.then_inc(v8_stored.sem, 1)
                items(28, 31)
                act.wait_ge(hT_psum.sem, hT_psum.after(b, 2))
                act.activation(hT[:], bank[3], ACT.Copy).then_inc(hT_full.sem, 1)
                items(31, 32)
                act.wait_ge(q_psum.sem, q_psum.after(b, 1))
                act.activation(qf[:], bank[1], ACT.Identity, bias=bq[:], scale=SCALE1).then_inc(qf_ready.sem, 1)
                act.wait_ge(ks_ready.sem, ks_ready.after(b, 4))
                act.wait_ge(fixed_ready.sem, fixed_ready.after(b, 3))
                act.activation(ks_t[:].rearrange("p g (j k) -> p g j k", j=4), ks[:, :, :, P:KP], ACT.Copy).then_inc(
                    kst_ready.sem, 1)
                act.wait_ge(q_masked.sem, q_masked.after(b, 1))
                act.activation(q_hi[:], qm[:], ACT.Copy).then_inc(q_hi_ready.sem, 1)
                for g in range(NG):
                    act.wait_ge(qrep_psum.sem, qrep_psum.after(b, g + 1))
                    act.activation(qs[0:96, g], bank[g][0:96], ACT.Copy).then_inc(qs_ready.sem, 1)
                act.wait_ge(nmT_psum.sem, nmT_psum.after(b, 1))
                for g in range(NG):
                    ins = act.activation(qs[96:104, g], bank[0][32 * g:32 * g + 8], ACT.Copy)
                ins.then_inc(nm_stored.sem, 1)
                for t in range(NG + H1):
                    act.wait_ge(st_psum.sem, st_psum.after(b, t + 1))
                    if t >= 4:
                        act.wait_ge(pm_used.sem, pm_used.after(b, t - 3))
                    act.activation(pm[:, t % 4], bank[4 + t % 2], ACT.Exp).then_inc(pm_ready.sem, 1)
                if more:
                    store_h1T(b + 1)
                    store_keys(b + 1, 0, 1, 2)
                act.wait_ge(o_psum.sem, o_psum.after(b, 3))
                act.activation(oT[:], bank[0], ACT.Identity, bias=bo[:]).then_inc(oT_stored.sem, 1)
                if more:
                    store_keys(b + 1, 3, 4, 5)
                    store_scores(b + 1, 0, 8)

                act.wait_ge(hT_psum.sem, hT_psum.after(b, 3))
                act.activation(hT[:], bank[0], ACT.Copy).then_inc(hT_full.sem, 1)
                act.activation(h4_hi[:], bank[0], ACT.Copy).then_inc(h4T_hi_ready.sem, 1)
                if more:
                    store_scores(b + 1, 8, 16)
                act.wait_ge(gate_arg.sem, gate_arg.after(b, 2))
                act.activation(col[:, 1], col[:, 0], ACT.Exp).then_inc(gate_exp.sem, 1)
                if more:
                    store_scores(b + 1, 16, 18)
                act.wait_ge(rwT_psum.sem, rwT_psum.after(b, 2))
                act.activation(rw4T[:], rwT_bank(3, 3 * NX), ACT.Copy).then_inc(rwT_stored.sem, 1)
                if more:
                    store_scores(b + 1, 18, 19)
                act.wait_ge(b2_psum.sem, b2_psum.after(b, 1))
                act.activation(acc[:], bank[3], ACT.Copy).then_inc(acc_begun.sem, 1)
                if more:
                    store_scores(b + 1, 19, NG + H0)

            store_h1T(0)
            store_keys(0, *range(6))
            store_scores(0, 0, NG + H0)
            batch(0, behind=False)
            with act.Fori(1, B - 1) as b:
                batch(b)
            batch(B - 1, more=False)
            expert_items(B - 1, 0, NX * FC)

        @block.tensor
        def _(pe):
            pe.wait_ge(fold_loaded, 64)
            for n in range(8):
                for i in range(4):
                    h = FOLD_HEADS[n % 4] + 2 * i
                    q = slice(DK0 * (h % 2), DK0 * (h % 2) + DK0)
                    l, r = (wk_T, wq_T) if n < 4 else (wv_T, wo_n)
                    mm = pe.matmul(bank[n][:, bass.ts(i, P)], l[q, h // 2], r[q, h // 2], start=True, stop=True)
                mm.then_inc(fold_ready, 1)
            pe.wait_ge(fold_stored, 8)
            pe.wait_ge(set_ready, 1)
            pe.matmul(bank[0][:, 0:NE], ones_f, sim_sq, start=True, stop=True).then_inc(set_pe, 1)
            pe.matmul(bank[1][:, 0:1], w_att[:, 3], b_att[:, 2:3], start=True, stop=True).then_inc(set_pe, 1)
            pe.wait_ge(set_dve, 1)
            pe.wait_ge(pads_zeroed, 1)
            pe.wait_ge(gated_loaded, 64)
            pe.wait_ge(w2_loaded, 16)

            def turn_in(h, dst, done=hT_psum):
                for i in range(NT):
                    mm = pe.transpose(dst[:, bass.ts(i, P)], h[:, i], ident)
                mm.then_inc(done.sem, 1)

            def turn_back(src, dst, done):
                for i in range(NT):
                    mm = pe.transpose(dst[:, bass.ts(i, P)], src[:, bass.ts(i, P)], ident)
                mm.then_inc(done.sem, 1)

            def split3(dst, hi, lo, m_hi, m_lo):
                pe.matmul(dst, hi, m_hi, start=True, stop=False)
                pe.matmul(dst, hi, m_lo, start=False, stop=False)
                return pe.matmul(dst, lo, m_hi, start=False, stop=True)

            def logits(dst, w, n):
                for i in range(NT):
                    mm = pe.matmul(dst[:, n * i:n * i + n], hT[:, bass.ts(i, P)], w, start=True, stop=True)
                mm.then_inc(logit_psum.sem, 1)

            def turn_weights(b, k, n, dst_rw):
                pe.wait_ge(rw_ready.sem, rw_ready.after(b, k))
                apart(pe)
                for i in range(NT):
                    mm = pe.transpose(dst_rw[:, bass.ts(i, P)], rw_parts[:, i, 0:3 * n], ident_b[:])
                mm.then_inc(rwT_psum.sem, 1)

            def expert_weights(b, e):
                i = weight_item(e)
                if i >= 2:
                    pe.wait_ge(item_stored.sem, item_stored.after(b, i - 1))
                pe.matmul(bank[4 + i % 2], one(pick8, e), rw4T[:], start=True, stop=True).then_inc(item_psum.sem, 1)

            def layer1(b, c):
                if c % FC == 0:
                    expert_weights(b, c // FC)
                i = hidden_item(c)
                if i >= 2:
                    pe.wait_ge(item_stored.sem, item_stored.after(b, i - 1))
                w = bass.ts(c, P)
                split3(bank[4 + i % 2], w1_hi[:, w], w1_lo[:, w], h4_hi[:], h4_lo[:]).then_inc(item_psum.sem, 1)

            def expert_steps(b, c0, c1):
                for c in range(c0, c1):
                    e, j = divmod(c, FC)
                    if j == 0 and e >= 2:
                        pe.wait_ge(ex_added.sem, ex_added.after(b, e - 1))
                    pe.wait_ge(item_stored.sem, item_stored.after(b, hidden_item(c) + 1))
                    pe.matmul(bank[6 + e % 2], w2[:, c], hid[:, c % 3], start=(j == 0), stop=(j == FC - 1)).then_inc(
                        hid_used.sem, 1)
                    if c + 2 < NX * FC:
                        layer1(b, c + 2)

            def turn_h1(b):
                pe.wait_ge(h1_ready.sem, h1_ready.after(b, 4))
                turn_in(h_rows, bank[4], h1T_psum)

            def folded_keys(b, *jobs):
                for n in jobs:
                    if n == 0:
                        pe.wait_ge(ctx_loaded.sem, ctx_loaded.after(b, 16))
                    if n >= 3:
                        pe.wait_ge(g_stored.sem, g_stored.after(b, n - 2))
                    for i in range(min(3, H0 - 3 * n)):
                        mm = pe.matmul(bank[FRONT_BANK[n % 3]][:, KP * i:KP * i + KP], mq[:, 3 * n + i], ctx_T[:],
                                       start=True, stop=True)
                    mm.then_inc(g_psum.sem, 1)

            def scores(b, t0, t1):
                for t in range(t0, t1):
                    if t == 0:
                        pe.wait_ge(h1T_lo_ready.sem, h1T_lo_ready.after(b, 1))
                    if t < NG:
                        pe.wait_ge(g_lo_ready.sem, g_lo_ready.after(b, (4 * t + 3) // 3 + 1))
                        pe.wait_ge(g_stored.sem, g_stored.after(b, min(6, t + 4)))
                    if t >= 3:
                        pe.wait_ge(sc_stored.sem, sc_stored.after(b, t - 2))
                    at = H0 * P + t * P if t < NG else (t - NG) * P
                    hi, lo = (g[:, at:at + P] for g in (g_hi, g_lo))
                    split3(bank[FRONT_BANK[t % 3]], hi, lo, hT_hi[:], hT_lo[:]).then_inc(sc_psum.sem, 1)

            def turn_tails(b, n):
                pe.wait_ge(tail_max.sem, tail_max.after(b, n))
                pe.matmul(bank[0], (perm64, perm32)[n - 1], top_t[:], start=True, stop=True).then_inc(tail_turned.sem, 1)

            def batch(b, behind=True, more=True):
                def steps(c0, c1):
                    if behind:
                        expert_steps(b - 1, c0, c1)

                pe.wait_ge(sc_stored.sem, sc_stored.after(b, NG + H0))
                if behind:
                    layer1(b - 1, 0)
                    layer1(b - 1, 1)
                for n in range(5):
                    if n < 3:
                        pe.wait_ge(sc_stored.sem, sc_stored.after(b, NG + H0))
                    else:
                        pe.wait_ge(u_stored.sem, u_stored.after(b, n - 2))
                    dst = bank[1 + n % 3]
                    if n < 4:
                        mm = pe.matmul(dst, ctx_T[:, 0:P], mo[:, 4 * n:4 * n + 4].rearrange("p h c -> p (h c)"),
                                       start=True, stop=True)
                    else:
                        for j in range(4):
                            mm = pe.matmul(dst[32 * j:32 * j + 32].rearrange("p (g c) -> p g c", g=NG),
                                           ctx_T[:, P:KP], mo[:].rearrange("p (g j) c -> p j g c", j=4)[:, j],
                                           start=True, stop=True, tile_position=(0, 32 * j))
                    mm.then_inc(u_psum.sem, 1)
                steps(0, 4)
                pe.wait_ge(tail_sum.sem, tail_sum.after(b, 1))
                pe.wait_ge(u_stored.sem, u_stored.after(b, 5))
                pe.matmul(bank[1], same, top_t[:], start=True, stop=True).then_inc(tail_den.sem, 1)
                steps(4, 11)
                for n, h in enumerate(MIXED):
                    if h in POOL_HEADS:
                        pe.wait_ge(attn_pool.sem, attn_pool.after(b, POOL_HEADS.index(h) + 1))
                    else:
                        pe.wait_ge(attn_dve.sem, attn_dve.after(b, DVE_HEADS.index(h) + 1))
                    pe.matmul(bank[0], u_main[:, h], sc[:, NG + h], start=(n == 0), stop=False)
                for g in range(NG):
                    pe.wait_ge(attn_pool.sem, attn_pool.after(b, len(POOL_HEADS) + g + 1))
                    mm = pe.matmul(bank[0], u_tail[:, g], sc[:, g], start=False, stop=(g == NG - 1))
                mm.then_inc(o_psum.sem, 1)
                pe.wait_ge(oT_stored.sem, oT_stored.after(b, 1))
                turn_back(oT, bank[2], back_psum)
                steps(11, 18)

                pe.wait_ge(h_ready.sem, h_ready.after(b, 4))
                turn_in(h_rows, bank[0])
                pe.wait_ge(hT_full.sem, hT_full.after(b, 1))
                logits(bank[1], sim_n[:], NE)
                steps(18, 24)
                turn_weights(b, 1, NE, rwT_bank(2, 3 * NE))
                pe.wait_ge(rwT_stored.sem, rwT_stored.after(b, 1))

                def spread(table, n):
                    pe.matmul(bank[BC_BANK[n]], table, rwT[:], start=True, stop=True).then_inc(bc_psum.sem, 1)

                def spread_pair(n):
                    m = NE + n
                    pe.matmul(bank[BC_BANK[m]][0:DH], one(pick, 2 * n, DH), rwT[:], start=True, stop=True)
                    pe.matmul(bank[BC_BANK[m]][DH:P], one(pick, 2 * n + 1, DH), rwT[:], start=True,
                              stop=True).then_inc(bc_psum.sem, 1)

                spread(one(pick, 0), 0)
                spread(one(pick, 1), 1)
                for e in range(NE):
                    pe.wait_ge(rh_ready.sem, rh_ready.after(b, e + 1))
                    pe.matmul(bank[2], qk_w[:, e], rh[:, e % 3], start=(e == 0), stop=(e == NE - 1))
                    mm = pe.matmul(bank[3][0:DH], v_w[:, e], rh[:, e % 3], start=(e == 0), stop=(e == NE - 1))
                    mm.then_inc(rh_used.sem, 1)
                    if e + 2 < NE:
                        spread(one(pick, e + 2), e + 2)
                steps(24, 25)
                pe.wait_ge(qkv_stored.sem, qkv_stored.after(b, 1))
                apart(pe)
                for i in range(NT):
                    mm = pe.transpose(v_bank[:, i], v_T[:, bass.ts(i, P)], ident[0:DH, 0:DH])
                mm.then_inc(v_psum.sem, 1)
                for i in range(NT):
                    if i == 3:
                        pe.wait_ge(p_exp.sem, p_exp.after(b, 1))
                    dst = bank[S_BANK[i]]
                    pe.matmul(dst[:, 0:P * (i + 1)], q_T[:, bass.ts(i, P)], k_T[:, 0:P * (i + 1)], start=True,
                              stop=False)
                    pe.matmul(dst[:, bass.ts(i, P)], ident_b[:], causal_b[:], start=False, stop=True).then_inc(
                        s_psum.sem, 1)
                pe.wait_ge(v_stored.sem, v_stored.after(b, 1))
                steps(25, 26)
                for i in range(NT):
                    pe.wait_ge(p_norm.sem, p_norm.after(b, i + 1))
                    if i == 3:
                        pe.wait_ge(pT_stored.sem, pT_stored.after(b, 1))
                    for j in range(i + 1):
                        mm = pe.transpose(bank[PT_BANK[i]][:, bass.ts(j, P)], pa[:, i, bass.ts(j, P)], ident)
                    mm.then_inc(pT_psum.sem, 1)
                pe.wait_ge(pT_stored.sem, pT_stored.after(b, 4))
                for j in range(NT):
                    mm = pe.matmul(bank[1][:, P * j:S], v_dup[:, j].rearrange("p a d -> p (a d)"),
                                   p_T[:, j, P * j:S], start=(j == 0), stop=(j == NT - 1))
                mm.then_inc(att_psum.sem, 1)
                spread_pair(0)
                spread_pair(1)
                for n in range(NE // 2):
                    pe.wait_ge(rh_ready.sem, rh_ready.after(b, NE + n + 1))
                    mm = pe.matmul(bank[3], o_w[:, n], rh[:, (NE + n) % 3], start=(n == 0), stop=(n == NE // 2 - 1))
                    if n < NE // 2 - 1:
                        mm.then_inc(rh_used.sem, 1)
                    else:
                        mm.then_inc(o_psum.sem, 1)
                    if n + 2 < NE // 2:
                        spread_pair(n + 2)
                pe.matmul(bank[2][:, 0:KP], w_att[:, 1], ctx_T[:], start=True, stop=True).then_inc(k_psum.sem, 1)
                pe.matmul(bank[0][:, 0:P], ctx_T[:, 0:P], w_att[:, 2], start=True, stop=True)
                for j in range(4):
                    mm = pe.matmul(bank[0][32 * j:32 * j + 32, P:2 * P], ctx_T[:, P:KP], w_att[:, 2], start=True,
                                   stop=True, tile_position=(0, 32 * j))
                mm.then_inc(v8_psum.sem, 1)
                pe.wait_ge(oT_stored.sem, oT_stored.after(b, 2))
                turn_back(oT, bank[1], back_psum)
                steps(26, 29)

                def keys(g):
                    q = slice(32 * g, 32 * g + 32)
                    dst = bank[KREP_BANK[g]][:, 0:KP]
                    pe.matmul(dst, rep[q, 0], k_hi[q], start=True, stop=False)
                    pe.matmul(dst, rep[q, 1], k_lo[q], start=False, stop=True).then_inc(krep_psum.sem, 1)

                pe.wait_ge(k_lo_ready.sem, k_lo_ready.after(b, 1))
                keys(0)
                pe.wait_ge(v8_stored.sem, v8_stored.after(b, 1))
                keys(1)

                pe.wait_ge(h_ready.sem, h_ready.after(b, 8))
                turn_in(h_rows, bank[3])
                keys(2)
                steps(29, 30)
                pe.wait_ge(hT_full.sem, hT_full.after(b, 2))
                keys(3)
                pe.wait_ge(ks_ready.sem, ks_ready.after(b, 3))
                pe.matmul(bank[1], w_att[:, 0], hT[:], start=True, stop=True).then_inc(q_psum.sem, 1)
                pe.wait_ge(mz_ready.sem, mz_ready.after(b, 2))
                pe.matmul(bank[2], ones_b[:], mz_T[:, 0], start=True, stop=False)
                pe.matmul(bank[2], ones_b[0:32], mz_T[0:32, 1], start=False, stop=True).then_inc(count_psum.sem, 1)
                steps(30, 31)
                pe.wait_ge(q_lo_ready.sem, q_lo_ready.after(b, 1))
                pe.wait_ge(v8_stored.sem, v8_stored.after(b, 1))
                for g in range(NG):
                    q = slice(32 * g, 32 * g + 32)
                    pe.matmul(bank[g], rep[q, 2], q_hi[q], start=True, stop=False)
                    pe.matmul(bank[g], rep[q, 3], q_lo[q], start=False, stop=True).then_inc(qrep_psum.sem, 1)
                steps(31, 32)
                if behind:
                    pe.wait_ge(ex_added.sem, ex_added.after(b - 1, NX))
                pe.wait_ge(qs_ready.sem, qs_ready.after(b, 4))
                for i in range(NT):
                    for g in range(NG):
                        n = NG * i + g
                        if n >= 2:
                            pe.wait_ge(smax_used.sem, smax_used.after(b, n - 1))
                        for w in range(2):
                            dst = duo[n % 2][:, w, 0:2 * SK].rearrange("p (j k) -> p j k", j=2)
                            pe.matmul(dst, qs[0:96, g, bass.ts(i, P)], ks[0:96, g, 2 * w:2 * w + 2, 0:SK], start=True,
                                      stop=False)
                            mm = pe.matmul(dst, neg_b[:], mz[:, i].unsqueeze(1).to_broadcast([P, 2, SK]),
                                           start=False, stop=True)
                        mm.then_inc(smax_psum.sem, 1)
                if behind:
                    turn_back(acc, bank[1], back4_psum)
                pe.wait_ge(fixed_ready.sem, fixed_ready.after(b, 3))
                pe.wait_ge(nm_ready.sem, nm_ready.after(b, 1))
                for i in range(NT):
                    mm = pe.transpose(bank[0][:, bass.ts(i, P)], nm[:, i].rearrange("p g c -> p (g c)"), ident)
                mm.then_inc(nmT_psum.sem, 1)
                pe.wait_ge(nm_stored.sem, nm_stored.after(b, 1))

                def scores_T(t):
                    g, j = ST_TILES[t]
                    if t >= 2:
                        pe.wait_ge(pm_ready.sem, pm_ready.after(b, t - 1))
                    keys = ks_t[:, g] if j is None else ks[:, g, j, 0:P]
                    pe.matmul(bank[4 + t % 2], keys, qs[:, g], start=True, stop=False)
                    pe.matmul(bank[4 + t % 2], neg_b[:], mz_T[:, int(j is None)], start=False, stop=True).then_inc(
                        st_psum.sem, 1)

                scores_T(0)
                scores_T(1)
                for t, (g, j) in enumerate(ST_TILES):
                    pe.wait_ge(pm_ready.sem, pm_ready.after(b, t + 1))
                    w = vz_t[:, P * g:P * g + P] if j is None else vz[:, P * (4 * g + j):P * (4 * g + j) + P]
                    mm = pe.matmul(bank[6 + g // 2], w, pm[:, t % 4], start=(t % 10 == 0), stop=(t % 10 == 9))
                    mm.then_inc(pm_used.sem, 1)
                    if t + 2 < NG + H1:
                        scores_T(t + 2)
                if more:
                    turn_h1(b + 1)
                    folded_keys(b + 1, 0, 1, 2)
                pe.wait_ge(pv_normed.sem, pv_normed.after(b, 1))
                pe.matmul(bank[0], w_att[:, 3], qf[:], start=True, stop=True).then_inc(o_psum.sem, 1)
                if more:
                    folded_keys(b + 1, 3, 4)
                pe.wait_ge(oT_stored.sem, oT_stored.after(b, 3))
                turn_back(oT, bank[3], back_psum)
                if more:
                    folded_keys(b + 1, 5)
                    scores(b + 1, 0, 8)

                pe.wait_ge(h_ready.sem, h_ready.after(b, 12))
                turn_in(h4_rows, bank[0])
                if more:
                    scores(b + 1, 8, 10)
                pe.wait_ge(hT_full.sem, hT_full.after(b, 3))
                logits(bank[3], w_r[:], NX)
                if more:
                    scores(b + 1, 10, 14)
                    pe.wait_ge(h4T_lo_ready.sem, h4T_lo_ready.after(b, 1))
                    turn_tails(b + 1, 1)
                    scores(b + 1, 14, 18)
                turn_weights(b, 2, NX, rwT_bank(3, 3 * NX))
                if more:
                    scores(b + 1, 18, 19)
                pe.wait_ge(rwT_stored.sem, rwT_stored.after(b, 2))
                for n in range(3):
                    mm = pe.matmul(bank[3], b2_parts[:, n], rw4T[:], start=(n == 0), stop=(n == 2))
                mm.then_inc(b2_psum.sem, 1)
                if more:
                    turn_tails(b + 1, 2)
                    scores(b + 1, 19, NG + H0)
                pe.wait_ge(h4T_lo_ready.sem, h4T_lo_ready.after(b, 1))
                pe.wait_ge(acc_begun.sem, acc_begun.after(b, 1))

            turn_h1(0)
            folded_keys(0, *range(6))
            scores(0, 0, NG + H0)
            turn_tails(0, 1)
            turn_tails(0, 2)
            batch(0, behind=False)
            with pe.Fori(1, B - 1) as b:
                batch(b)
            batch(B - 1, more=False)
            layer1(B - 1, 0)
            layer1(B - 1, 1)
            expert_steps(B - 1, 0, NX * FC)
            pe.wait_ge(ex_added.sem, ex_added.after(B - 1, NX))
            turn_back(acc, bank[1], back4_psum)

        @block.vector
        def _(dve):
            def rsqrt(v, y, t, u, link):
                link(dve.tensor_scalar(t.bitcast(I32), v.bitcast(I32), 1, None, ALU.arith_shift_right))
                link(dve.tensor_scalar(y.bitcast(I32), t.bitcast(I32), -1.0, MAGIC, ALU.mult, ALU.add))
                for _ in range(3):
                    link(dve.scalar_tensor_tensor(t, y, -0.5, v, ALU.mult, ALU.mult))
                    link(dve.tensor_tensor(u, t, y, ALU.mult))
                    link(dve.scalar_tensor_tensor(y, u, 1.5, y, ALU.add, ALU.mult))

            done = [0]

            def set_link(ins):
                done[0] += 1
                ins.then_inc(set_step, 1)
                dve.wait_ge(set_step, done[0])

            dve.memset(ones_b[:], 1.0)
            dve.memset(ones_f, 1.0)

            dve.wait_ge(mats_loaded, 16)
            dve.tensor_copy(ident_b[:], ident)
            dve.tensor_scalar(causal_b[:], after_, -HUGE, None, ALU.mult)
            dve.tensor_scalar(neg_b[:], ident, NEG, None, ALU.mult)
            dve.wait_ge(tables_loaded, 16 * 6)
            dve.tensor_copy(rep[:], rep_raw)
            dve.tensor_copy(pick[:], pick_raw)
            dve.tensor_copy(pick8[:], pick8_raw)
            dve.tensor_copy(maxrow[96:P], maxrow_raw)
            dve.wait_ge(direct_loaded, 16 * 16)
            dve.tensor_scalar(bq[:], b_att[:, 0:1], SCALE1, None, ALU.mult)
            set_link(dve.tensor_copy(b2_parts[:, 0], b2[:]))
            set_link(dve.tensor_tensor(b2_rest[:, 0], b2[:], b2_parts[:, 0], ALU.subtract))
            set_link(dve.tensor_copy(b2_parts[:, 1], b2_rest[:, 0]))
            set_link(dve.tensor_tensor(b2_rest[:, 1], b2_rest[:, 0], b2_parts[:, 1], ALU.subtract))
            dve.tensor_copy(b2_parts[:, 2], b2_rest[:, 1])
            dve.tensor_tensor(sim_sq, sim[:], sim[:], ALU.mult).then_inc(set_ready, 1)
            dve.wait_ge(set_pe, 2)
            dve.tensor_tensor(bo[:], bank[1][:, 0:1], b_att[:, 3:4], ALU.add)
            set_link(dve.tensor_scalar(sim_ss, bank[0][:, 0:NE], 1e-24, None, ALU.max))
            rsqrt(sim_ss, sim_r, sim_t, sim_u, set_link)
            dve.tensor_tensor(sim_n[:], sim[:], sim_r, ALU.mult)
            dve.wait_ge(set_act, 1)
            set_link(dve.tensor_scalar(gate[:], gate[:], 1.0, None, ALU.add))
            dve.reciprocal(gate[:], gate[:])
            for n in range(4):
                w = bass.ts(n, 1024)
                dve.wait_ge(set_act, n + 2)
                ins = dve.tensor_tensor(w1_lo[:, w], w1_raw[:, w], w1_hi[:, w], ALU.subtract)
            ins.then_inc(set_dve, 1)

            def over_tokens(v, n):
                return v.unsqueeze(2).to_broadcast([P, NT, n])

            def over_tiles(v, n):
                return v.unsqueeze(1).to_broadcast([P, NT, n])

            def normalise(src, dst, link, ready=None):
                for t in range(NT):
                    ins = dve.bn_stats(stats[:, t], src[:, t])
                link(ins)
                apart(dve)
                for t in range(NT):
                    ins = dve.bn_aggr(mv[:, t], stats[:, t])
                link(ins)
                link(dve.tensor_scalar(nv[:], mv[:, :, 1], LN_EPS, None, ALU.add))
                rsqrt(nv[:], ny[:], nt_[:], nu[:], link)
                for t in range(NT):
                    ins = dve.tensor_scalar(dst[:, t], src[:, t], mv[:, t, 0:1], ny[:, t:t + 1], ALU.subtract,
                                            ALU.mult)
                    if ready is not None:
                        ins.then_inc(ready[0].sem, 1)
                if ready is None:
                    link(ins)
                else:
                    dve.wait_ge(ready[0].sem, ready[1])

            def first_chain(b, done):
                count = [done]

                def link(ins):
                    count[0] += 1
                    ins.then_inc(first_step.sem, 1)
                    dve.wait_ge(first_step.sem, first_step.after(b, count[0]))

                return link, count

            def first_norm(b):
                link, count = first_chain(b, 0)
                dve.wait_ge(x_loaded.sem, x_loaded.after(b, 16))
                normalise(x_in, h_rows, link, (h1_ready, h1_ready.after(b, 4)))
                assert count[0] == FIRST_STEPS - EARLY_MAX - 1, count

            def split_h1(b):
                dve.wait_ge(h1T_hi_ready.sem, h1T_hi_ready.after(b, 1))
                dve.tensor_tensor(hT_lo[:], bank[4], hT_hi[:], ALU.subtract).then_inc(h1T_lo_ready.sem, 1)

            def early_maxima(b):
                link, count = first_chain(b, FIRST_STEPS - EARLY_MAX - 1)
                dve.wait_ge(sc_stored.sem, sc_stored.after(b, 4))
                link(dve.tensor_tensor(top_t[:], sc[:, 0], sc[:, 1], ALU.max))
                link(dve.tensor_tensor(top_t[:], top_t[:], sc[:, 2], ALU.max))
                dve.tensor_tensor(top_t[:], top_t[:], sc[:, 3], ALU.max).then_inc(tail_max.sem, 1)
                for h in range(1, EARLY_MAX):
                    dve.wait_ge(sc_stored.sem, sc_stored.after(b, NG + h + 1))
                    link(dve.tensor_tensor(top_m[:], sc[:, NG] if h == 1 else top_m[:], sc[:, NG + h], ALU.max))
                assert count[0] == FIRST_STEPS, count

            def turned_tails(b, n):
                dve.wait_ge(tail_turned.sem, tail_turned.after(b, n))
                dve.wait_ge(tail_max.sem, tail_max.after(b, n))
                dve.tensor_tensor(top_t[:], top_t[:], bank[0], ALU.max).then_inc(
                    (tail_max if n == 1 else top_t_ready).sem, 1)

            def add_expert(b, e):
                if e == 0:
                    dve.wait_ge(acc_begun.sem, acc_begun.after(b, 1))
                dve.wait_ge(item_stored.sem, item_stored.after(b, weight_item(e) + 1))
                dve.wait_ge(hid_used.sem, hid_used.after(b, FC * (e + 1)))
                dve.tensor_tensor(rw_b[:, e % 3], bank[6 + e % 2], rw_b[:, e % 3], ALU.mult).then_inc(last_step.sem, 1)
                dve.wait_ge(last_step.sem, last_step.after(b, e + 1))
                dve.tensor_tensor(acc[:], acc[:], rw_b[:, e % 3], ALU.add).then_inc(ex_added.sem, 1)
                dve.wait_ge(ex_added.sem, ex_added.after(b, e + 1))

            def last_norm(b):
                count = [NX]

                def link(ins):
                    count[0] += 1
                    ins.then_inc(last_step.sem, 1)
                    dve.wait_ge(last_step.sem, last_step.after(b, count[0]))

                dve.wait_ge(back4_psum.sem, back4_psum.after(b, 1))
                link(dve.tensor_tensor(y_rows[:], rows(bank[1]), h4_rows[:], ALU.add))
                normalise(y_rows, y_rows, link)
                link(dve.tensor_tensor(y_rows[:], y_rows[:], over_tiles(ln1[:, 0], D), ALU.mult))
                link(dve.tensor_tensor(y_rows[:], y_rows[:], over_tiles(ln1[:, 1], D), ALU.add))
                dve.tensor_tensor(x4_rows[:], y_rows[:], x4_rows[:], ALU.add).then_inc(out_ready.sem, 1)
                assert count[0] == LAST_STEPS, count

            def batch(b, behind=True, more=True):
                steps = [0]

                def link(ins):
                    steps[0] += 1
                    ins.then_inc(dve_step.sem, 1)
                    dve.wait_ge(dve_step.sem, dve_step.after(b, steps[0]))

                def add_experts(*experts):
                    if behind:
                        for e in experts:
                            add_expert(b - 1, e)

                def first_best(src, n, best, sel):
                    link(dve.tensor_reduce(best, src, AX.X, ALU.max))
                    link(dve.tensor_tensor(eq[:, :, 0:n], src, over_tokens(best, n), ALU.is_equal))
                    link(dve.tensor_tensor(pr[:, :, 0:n], eq[:, :, 0:n], first[:, :, 0:n], ALU.mult))
                    link(dve.tensor_reduce(col[:, 3], pr[:, :, 0:n], AX.X, ALU.max))
                    link(dve.tensor_tensor(sel, pr[:, :, 0:n], over_tokens(col[:, 3], n), ALU.is_equal))

                def best_two(n):
                    v, v2 = lg[:, :, 0:n], lg2[:, :, 0:n]
                    first_best(v, n, top[:, 0], s1[:, :, 0:n])
                    link(dve.scalar_tensor_tensor(v2, s1[:, :, 0:n], -HUGE, v, ALU.mult, ALU.add))
                    first_best(v2, n, top[:, 1], s2[:, :, 0:n])

                def split_weights(n):
                    w, rest = rw[:, :, 0:n], [rw_rest[:, k, :, 0:n] for k in range(2)]
                    part_of = [rw_parts[:, :, n * k:n * k + n] for k in range(3)]
                    link(dve.tensor_copy(part_of[0], w))
                    link(dve.tensor_tensor(rest[0], w, part_of[0], ALU.subtract))
                    link(dve.tensor_copy(part_of[1], rest[0]))
                    link(dve.tensor_tensor(rest[1], rest[0], part_of[1], ALU.subtract))
                    dve.tensor_copy(part_of[2], rest[1]).then_inc(rw_ready.sem, 1)

                for h in range(EARLY_MAX, H0):
                    dve.wait_ge(sc_stored.sem, sc_stored.after(b, NG + h + 1))
                    ins = dve.tensor_tensor(top_m[:], top_m[:], sc[:, NG + h], ALU.max)
                    if h < H0 - 1:
                        link(ins)
                    else:
                        ins.then_inc(top_m_ready.sem, 1)
                    if h == EARLY_MAX + 3:
                        turned_tails(b, 2)
                dve.wait_ge(top_m_ready.sem, top_m_ready.after(b, 1))
                for h in DVE_HEADS:
                    dve.tensor_tensor(sc[:, NG + h], sc[:, NG + h], top_m[:], ALU.subtract).then_inc(less_dve.sem, 1)
                add_experts(0)
                dve.wait_ge(less_pool.sem, less_pool.after(b, NG + len(POOL_HEADS)))
                dve.wait_ge(less_dve.sem, less_dve.after(b, len(DVE_HEADS)))
                last = None
                for n, h in enumerate(MIXED):
                    if h in POOL_HEADS:
                        continue
                    if last is None:
                        last = sc[:, NG + h]
                        continue
                    dve.wait_ge(exp_ready.sem, exp_ready.after(b, NG + n + 1))
                    link(dve.tensor_tensor(top_m[:], last, sc[:, NG + h], ALU.add))
                    last = top_m[:]
                dve.wait_ge(pool_sum.sem, pool_sum.after(b, 1))
                link(dve.tensor_tensor(top_m[:], top_m[:], den_p[:], ALU.add))
                dve.reciprocal(top_m[:], top_m[:]).then_inc(inv_m_ready.sem, 1)
                dve.wait_ge(inv_m_ready.sem, inv_m_ready.after(b, 1))
                for h in DVE_HEADS:
                    dve.tensor_tensor(sc[:, NG + h], sc[:, NG + h], top_m[:], ALU.mult).then_inc(attn_dve.sem, 1)
                    if h == 7:
                        dve.wait_ge(tail_den.sem, tail_den.after(b, 1))
                        dve.reciprocal(top_t[:], bank[1]).then_inc(inv_t_ready.sem, 1)
                add_experts(1)
                dve.wait_ge(back_psum.sem, back_psum.after(b, 1))
                link(dve.tensor_tensor(y_rows[:], rows(bank[2]), h_rows[:], ALU.add))
                normalise(y_rows, y_rows, link)
                link(dve.tensor_tensor(y_rows[:], y_rows[:], over_tiles(ln0[:, 0], D), ALU.mult))
                link(dve.tensor_tensor(y_rows[:], y_rows[:], over_tiles(ln0[:, 1], D), ALU.add))
                link(dve.tensor_tensor(x_rows[:], y_rows[:], x_in[:], ALU.add))
                add_experts(2)

                normalise(x_rows, h_rows, link, (h_ready, h_ready.after(b, 4)))
                add_experts(3)
                link(dve.tensor_tensor(y_rows[:], h_rows[:], h_rows[:], ALU.mult))
                link(dve.tensor_reduce(nv[:], y_rows[:], AX.X, ALU.add))
                link(dve.tensor_scalar(nv[:], nv[:], 1e-24, None, ALU.max))
                rsqrt(nv[:], ny[:], nt_[:], nu[:], link)
                dve.wait_ge(logit_psum.sem, logit_psum.after(b, 1))
                link(dve.tensor_tensor(lg[:], bank[1][:, 0:NT * NE].rearrange("p (t e) -> p t e", e=NE),
                                       over_tokens(ny[:], NE), ALU.mult))
                link(dve.tensor_tensor(lg[:], lg[:], over_tiles(gate[:], NE), ALU.subtract))
                best_two(NE)
                dve.tensor_scalar(gated[:], lg[:], 0.0, None, ALU.max)
                link(dve.tensor_scalar(eq[:], lg[:], 0.0, None, ALU.is_gt))
                link(dve.tensor_tensor(s1[:], s1[:], s2[:], ALU.add))
                dve.tensor_reduce(top[:, 0], gated[:], AX.X, ALU.max)
                link(dve.tensor_reduce(col[:, 2], eq[:], AX.X, ALU.max))
                dve.tensor_tensor(gated[:], gated[:], over_tokens(top[:, 0], NE), ALU.subtract).then_inc(gate_arg.sem, 1)
                link(dve.tensor_scalar(col[:, 2], col[:, 2], -1.0, 1.0, ALU.mult, ALU.add))
                link(dve.tensor_tensor(s1[:], s1[:], over_tokens(col[:, 2], NE), ALU.mult))
                link(dve.tensor_tensor(s1[:], s1[:], eq[:], ALU.add))
                dve.wait_ge(gate_exp.sem, gate_exp.after(b, 1))
                link(dve.tensor_tensor(rw[:], gated[:], s1[:], ALU.mult))
                link(dve.tensor_reduce(top[:, 0], rw[:], AX.X, ALU.add))
                link(dve.reciprocal(top[:, 1], top[:, 0]))
                link(dve.tensor_tensor(rw[:], rw[:], over_tokens(top[:, 1], NE), ALU.mult))
                split_weights(NE)
                add_experts(4, 5)
                def weigh(m, src):
                    dve.wait_ge(bc_psum.sem, bc_psum.after(b, m + 1))
                    if m >= 3:
                        dve.wait_ge(rh_used.sem, rh_used.after(b, m - 2))
                    dve.tensor_tensor(rh[:, m % 3], src, bank[BC_BANK[m]], ALU.mult).then_inc(rh_ready.sem, 1)

                for e in range(NE):
                    weigh(e, hT[:])

                def row_max(i):
                    dve.wait_ge(s_psum.sem, s_psum.after(b, i + 1))
                    link(dve.tensor_reduce(col[:, 3, i:i + 1], bank[S_BANK[i]][:, 0:P * (i + 1)], AX.X, ALU.max))
                    dve.tensor_scalar(col[:, 0, i:i + 1], col[:, 3, i:i + 1], -(DH ** -0.5), None, ALU.mult).then_inc(
                        s_max.sem, 1)

                def row_norm(i):
                    dve.wait_ge(p_exp.sem, p_exp.after(b, i + 1))
                    link(dve.reciprocal(col[:, 2, i:i + 1], col[:, 1, i:i + 1]))
                    n = P * (i + 1)
                    dve.tensor_scalar(pa[:, i, 0:n], pa[:, i, 0:n], col[:, 2, i:i + 1], None, ALU.mult).then_inc(
                        p_norm.sem, 1)

                for i in range(3):
                    row_max(i)
                row_norm(0)
                row_max(3)
                for i in range(1, NT):
                    row_norm(i)
                dve.wait_ge(att_stored.sem, att_stored.after(b, 1))
                for n in range(NE // 2):
                    weigh(NE + n, a_T[:])
                dve.wait_ge(k_hi_ready.sem, k_hi_ready.after(b, 1))
                dve.tensor_tensor(k_lo[:], kv_f[:], k_hi[:], ALU.subtract).then_inc(k_lo_ready.sem, 1)
                dve.wait_ge(back_psum.sem, back_psum.after(b, 2))
                link(dve.tensor_tensor(x_rows[:], x_rows[:], rows(bank[1]), ALU.add))

                normalise(x_rows, h_rows, link, (h_ready, h_ready.after(b, 8)))
                add_experts(6)
                for g in range(NG):
                    dve.wait_ge(krep_psum.sem, krep_psum.after(b, g + 1))
                    src = bank[KREP_BANK[g]][0:96, 0:KP]
                    dve.tensor_tensor(ks[0:96, g], src.unsqueeze(1).to_broadcast([96, 4, KP]),
                                      band[0:96].unsqueeze(2).to_broadcast([96, 4, KP]), ALU.mult).then_inc(
                                          ks_ready.sem, 1)
                dve.wait_ge(qf_ready.sem, qf_ready.after(b, 1))
                dve.wait_ge(count_psum.sem, count_psum.after(b, 1))
                dve.scalar_tensor_tensor(qm[:], bank[2], KP - 0.5, qf[:], ALU.is_lt, ALU.mult).then_inc(q_masked.sem, 1)
                dve.wait_ge(q_hi_ready.sem, q_hi_ready.after(b, 1))
                dve.tensor_tensor(q_lo[:], qm[:], q_hi[:], ALU.subtract).then_inc(q_lo_ready.sem, 1)
                add_experts(7)
                for n in range(NT * NG):
                    i, g = divmod(n, NG)
                    dve.wait_ge(smax_psum.sem, smax_psum.after(b, n + 1))
                    dve.tensor_reduce(mx[:, i, 4 * g:4 * g + 4].rearrange("p (w j) -> p w j", w=2),
                                      duo[n % 2][:, :, 0:2 * SK].rearrange("p w (j k) -> p w j k", j=2),
                                      AX.X, ALU.max).then_inc(smax_used.sem, 1)
                dve.wait_ge(smax_used.sem, smax_used.after(b, NT * NG))
                dve.wait_ge(fixed_ready.sem, fixed_ready.after(b, 3))
                m4 = mx[:].rearrange("p t (g j) -> p t g j", g=NG)
                link(dve.tensor_scalar(nm[:].bitcast(F32R)[:, :, :, 0:4], m4, -1.0, None, ALU.mult))
                dve.scalar_tensor_tensor(nm[:, :, :, 4:8], m4, -1.0, nm[:, :, :, 0:4], ALU.mult,
                                         ALU.subtract).then_inc(nm_ready.sem, 1)
                if behind:
                    last_norm(b - 1)
                dve.wait_ge(pm_used.sem, pm_used.after(b, (NG + H1) // 2))
                link(dve.reciprocal(rz[0:64], bank[6][64:P]))
                dve.tensor_tensor(qf[0:64], bank[6][0:64], rz[0:64], ALU.mult)
                if more:
                    first_norm(b + 1)
                dve.wait_ge(pm_used.sem, pm_used.after(b, NG + H1))
                link(dve.reciprocal(rz[64:P], bank[7][0:64]))
                dve.tensor_tensor(qf[64:P], bank[7][64:P], rz[64:P], ALU.mult).then_inc(pv_normed.sem, 1)
                if more:
                    split_h1(b + 1)
                if behind:
                    dve.wait_ge(out_stored.sem, out_stored.after(b - 1, 16))
                dve.wait_ge(back_psum.sem, back_psum.after(b, 3))
                link(dve.tensor_tensor(x4_rows[:], x_rows[:], rows(bank[3]), ALU.add))

                normalise(x4_rows, h4_rows, link, (h_ready, h_ready.after(b, 12)))
                if more:
                    early_maxima(b + 1)
                dve.wait_ge(h4T_hi_ready.sem, h4T_hi_ready.after(b, 1))
                dve.tensor_tensor(h4_lo[:], bank[0], h4_hi[:], ALU.subtract).then_inc(h4T_lo_ready.sem, 1)
                dve.wait_ge(logit_psum.sem, logit_psum.after(b, 2))
                link(dve.tensor_tensor(lg[:, :, 0:NX], bank[3][:, 0:NT * NX].rearrange("p (t e) -> p t e", e=NX),
                                       over_tiles(b_r[:], NX), ALU.add))
                best_two(NX)
                dve.tensor_tensor(col[:, 0], top[:, 1], top[:, 0], ALU.subtract).then_inc(gate_arg.sem, 1)
                if more:
                    turned_tails(b + 1, 1)
                dve.wait_ge(gate_exp.sem, gate_exp.after(b, 2))
                link(dve.tensor_scalar(col[:, 2], col[:, 1], 1.0, None, ALU.add))
                link(dve.reciprocal(col[:, 3], col[:, 2]))
                link(dve.tensor_tensor(col[:, 2], col[:, 1], col[:, 3], ALU.mult))
                dve.tensor_tensor(s1[:, :, 0:NX], s1[:, :, 0:NX], over_tokens(col[:, 3], NX), ALU.mult)
                link(dve.tensor_tensor(s2[:, :, 0:NX], s2[:, :, 0:NX], over_tokens(col[:, 2], NX), ALU.mult))
                link(dve.tensor_tensor(rw[:, :, 0:NX], s1[:, :, 0:NX], s2[:, :, 0:NX], ALU.add))
                split_weights(NX)
                assert steps[0] == DVE_STEPS, steps

            first_norm(0)
            split_h1(0)
            early_maxima(0)
            turned_tails(0, 1)
            batch(0, behind=False)
            with dve.Fori(1, B - 1) as b:
                batch(b)
            batch(B - 1, more=False)
            for e in range(NX):
                add_expert(B - 1, e)
            last_norm(B - 1)


_SHAPES = ["x", "ctx_T", "mask", "mask_T", "wq_T", "wk_T", "wv_T", "wo", "gamma0", "beta0", "sim", "gates", "q_proj",
           "k_proj", "v_proj", "o_proj", "w_att", "b_att", "w_r", "b_r", "w1", "b1", "w2", "b2", "gamma1", "beta1"]


def kernel(x, ctx_1024, mask_BxSxS2_if1, L0_xattn_W_Q, L0_xattn_W_K, L0_xattn_W_V, L0_xattn_W_O, L0_xattn_ln_gamma,
           L0_xattn_ln_beta, L0_ffn_sim_matrix, L0_ffn_gates, L0_ffn_q_proj, L0_ffn_k_proj, L0_ffn_v_proj,
           L0_ffn_o_proj, L1_xattn_W0, L1_xattn_b0, L1_xattn_W1, L1_xattn_b1, L1_xattn_W2, L1_xattn_b2, L1_xattn_W3,
           L1_xattn_b3, L1_ffn_Wr, L1_ffn_br, L1_ffn_W1, L1_ffn_b1, L1_ffn_W2, L1_ffn_b2, L1_ffn_gamma, L1_ffn_beta):
    import concourse.bacc as bacc
    from concourse.bass_utils import run_bass_kernel_spmd

    arrays = {
        "x": x,
        "ctx_T": ctx_1024.transpose(0, 2, 1),
        "mask": mask_BxSxS2_if1,
        "mask_T": mask_BxSxS2_if1.transpose(0, 2, 1),
        "wq_T": L0_xattn_W_Q.T, "wk_T": L0_xattn_W_K.T, "wv_T": L0_xattn_W_V.T, "wo": L0_xattn_W_O,
        "gamma0": L0_xattn_ln_gamma, "beta0": L0_xattn_ln_beta,
        "sim": L0_ffn_sim_matrix, "gates": L0_ffn_gates,
        "q_proj": L0_ffn_q_proj, "k_proj": L0_ffn_k_proj, "v_proj": L0_ffn_v_proj, "o_proj": L0_ffn_o_proj,
        "w_att": np.stack([np.asarray(w).T for w in (L1_xattn_W0, L1_xattn_W1, L1_xattn_W2, L1_xattn_W3)], 1),
        "b_att": np.stack([np.asarray(w) for w in (L1_xattn_b0, L1_xattn_b1, L1_xattn_b2, L1_xattn_b3)], 1),
        "w_r": L1_ffn_Wr.T, "b_r": L1_ffn_br,
        "w1": L1_ffn_W1.transpose(2, 0, 1).reshape(D, NX * F),
        "b1": L1_ffn_b1.reshape(NX * FC, P).T,
        "w2": L1_ffn_W2.transpose(0, 2, 1).reshape(NX * FC, P, D).transpose(1, 0, 2),
        "b2": L1_ffn_b2, "gamma1": L1_ffn_gamma, "beta1": L1_ffn_beta,
    }
    arrays.update(constants())
    nc = bacc.Bacc("TRN2", target_bir_lowering=False, num_devices=1)
    sent, aps = {}, {}
    for name, value in arrays.items():
        value = np.ascontiguousarray(value)
        sent[f"in_{name}"] = value
        aps[name] = nc.dram_tensor(f"in_{name}", value.shape, mybir.dt.from_np(value.dtype),
                                   kind="ExternalInput").ap()
    out = nc.dram_tensor("out", (B, S, D), F32, kind="ExternalOutput").ap()
    program(nc, aps, out)
    result = run_bass_kernel_spmd(nc, [sent], core_ids=[0])
    return result.results[0]["out"]
```

```python
from contextlib import ExitStack

import numpy as np

import concourse.bass as bass
from concourse import mybir

ALU = mybir.AluOpType
ACT = mybir.ActivationFunctionType
AX = mybir.AxisListType
F32 = mybir.dt.float32
F32R = mybir.dt.float32r
BF16 = mybir.dt.bfloat16
I32 = mybir.dt.int32

B, S, D, SK = 4, 512, 128, 154
P = 128
NT = S // P
KT = 32
KP = P + KT
TAIL = SK - P
H0, DK0 = 16, 64
NE = 16
DH = 64
H1, DK1 = 16, 8
NG = 4
NX, F = 8, 512
FC = F // P
VZP = P + DK1
VTP = P + 4 * DK1
LN_EPS = 1e-5
NEG = -1e9
HUGE = 1e30
MAGIC, STEP_A, STEP_B = 1595932665.0, 0.703952253 * 2.38924456, 0.703952253
SCALE1 = float(DK1) ** -0.5


def constants():
    i = np.arange(P)
    eye = np.eye(P, dtype=np.float32)
    q, r = i // 32, i % 32
    perm64 = (i[:, None] == (i[None, :] + 64) % P)
    perm32 = (i[:, None] == (i[None, :] ^ 32))
    same = r[:, None] == r[None, :]
    after = i[None, :] > i[:, None]
    mats = np.stack([eye, perm64, perm32, same, after], 1).astype(np.float32)
    into = [[0, 2], [1], [0, 1], [2]]
    rep = np.zeros((P, 4, P), np.float32)
    for n, quads in enumerate(into):
        for z in quads:
            rep[i, n, 32 * z + r] = 1
    band = (r[:, None] // DK1 == np.arange(4)[None, :]).astype(np.float32)
    maxrow = np.zeros((32, 4, KP), np.float32)
    for j in range(4):
        maxrow[j, j] = maxrow[4 + j, j] = 1
    pick = np.tile(np.eye(NE, dtype=np.float32), (3, 1))
    pick8 = np.tile(np.eye(NX, dtype=np.float32), (3, 1))
    first = np.zeros((P, NT, NE), np.float32)
    first[:] = NE - np.arange(NE)
    vz = np.zeros((P, H1 * VZP), np.float32)
    vzt = np.zeros((P, NG * VTP), np.float32)
    for h in range(H1):
        at = 64 + DK1 * h if h < 8 else DK1 * (h - 8)
        vz[:, P * h + at:P * h + at + DK1] = 1
        g, j = divmod(h, 4)
        vzt[32 * j:32 * j + TAIL, P * g + at:P * g + at + DK1] = 1
    return {"c_mats": mats, "c_rep": rep, "c_band": band, "c_maxrow": maxrow, "c_pick": pick,
            "c_pick8": pick8, "c_first": first, "c_vz": vz, "c_vzt": vzt}


DVE_STEPS, FIRST_STEPS, LAST_STEPS, POOL_STEPS = 127, 13, 22, 6


class Signal:

    def __init__(self, sem, per_batch):
        self.sem, self.per_batch = sem, per_batch

    def after(self, b, k):
        assert 1 <= k <= self.per_batch
        return b * self.per_batch + k


def program(nc, a, out):
    ctx = ExitStack()
    with ctx:
        def sb(name, shape, dt=F32):
            return ctx.enter_context(nc.sbuf_tensor(name, shape, dt))

        def sem(name):
            return ctx.enter_context(nc.semaphore(name))

        def sig(name, per_batch):
            return Signal(sem(name), per_batch)

        duo = [ctx.enter_context(nc.psum_tensor(f"duo{n}", [P, 2, 512], F32)) for n in range(4)]
        bank = [duo[n // 2][:, n % 2] for n in range(8)]

        mats = sb("mats", [P, 5, P])
        ident, perm64, perm32, same, after_ = (mats[:, n, :] for n in range(5))
        ident_b = sb("ident_b", [P, P], BF16)
        causal_b = sb("causal_b", [P, P], BF16)
        neg_b = sb("neg_b", [P, P], BF16)
        ones_b = sb("ones_b", [P, P], BF16)
        rep = sb("rep", [P, 4, P], F32R)
        band = sb("band", [P, 4])
        pick = sb("pick", [3 * NE, NE], BF16)
        pick8 = sb("pick8", [3 * NX, NX], BF16)
        first = sb("first", [P, NT, NE])
        mq = sb("mq", [P, H0, P])
        mo = sb("mo", [P, H0, P])
        qk_w = sb("qk_w", [P, NE, 2 * DH])
        v_w = sb("v_w", [P, NE, DH])
        o_w = sb("o_w", [P, NE // 2, D])
        sim = sb("sim", [P, NE])
        sim_n = sb("sim_n", [P, NE])
        gate = sb("gate", [P, NE])
        ln0 = sb("ln0", [P, 2, D])
        w_att = sb("w_att", [P, 4, D])
        b_att = sb("b_att", [P, 4])
        bq = sb("bq", [P, 1])
        bo_rows = sb("bo_rows", [P, D])
        w_r = sb("w_r", [P, NX])
        b_r = sb("b_r", [P, NX])
        w2 = sb("w2", [P, NX * FC, D])
        maxrow = sb("maxrow", [P, 4, KP], BF16)
        w1_hi = sb("w1_hi", [P, NX * F], F32R)
        w1_lo = sb("w1_lo", [P, NX * F], F32R)
        b1 = sb("b1", [P, NX * FC])

        b2_parts = sb("b2_parts", [3 * NX, 3, D], BF16)
        ln1 = sb("ln1", [P, 2, D])
        vz = sb("vz", [P, H1 * VZP])
        vz_t = sb("vz_t", [P, NG * VTP])

        x_in = sb("x_in", [P, NT, D])
        h_rows = sb("h_rows", [P, NT, D])
        y_rows = sb("y_rows", [P, NT, D])
        x_rows = sb("x_rows", [P, NT, D])
        x4_rows = sb("x4_rows", [P, NT, D])
        h4_rows = sb("h4_rows", [P, NT, D])
        h4_hi = sb("h4_hi", [P, S], F32R)
        h4_lo = sb("h4_lo", [P, S], F32R)
        rw4T = sb("rw4T", [3 * NX, S], BF16)
        hid = sb("hid", [P, 3, S])
        rw_b = sb("rw_b", [P, 3, S])
        acc = sb("acc", [P, S])
        ctx_T = sb("ctx_T", [P, KP])

        hT = sb("hT", [P, S])
        hT_hi = sb("hT_hi", [P, S], F32R)
        hT_lo = sb("hT_lo", [P, S], F32R)
        oT = den_p = hT

        stats = sb("stats", [P, NT, 6])
        mv = sb("mv", [P, NT, 2])
        nv = sb("nv", [P, NT])
        square_sums = sb("square_sums", [P, NT])
        ny = sb("ny", [P, NT])
        nt_ = sb("nt_", [P, NT])
        nu = sb("nu", [P, NT])
        lg = sb("lg", [P, NT, NE])
        lg2 = sb("lg2", [P, NT, NE])
        eq = sb("eq", [P, NT, NE])
        pr = sb("pr", [P, NT, NE])
        s1 = sb("s1", [P, NT, NE])
        s2 = sb("s2", [P, NT, NE])
        gated = sb("gated", [P, NT, NE])
        rw = sb("rw", [P, NT, NE])
        top = sb("top", [P, 2, NT])
        col = sb("col", [P, 4, NT])
        rw_parts = sb("rw_parts", [P, NT, 3 * NE], BF16)
        rw_rest = sb("rw_rest", [P, 2, NT, NE])
        rwT = sb("rwT", [3 * NE, S], BF16)

        def arena(*specs):
            with ExitStack() as own:
                return [own.enter_context(nc.sbuf_tensor(n, sh, dt)) for n, sh, dt in specs]

        _, cst, wq_T, wk_T = arena(
            ("first_keys", [P, 2 * H0 * KP], F32), ("cst", [P, 40 * P], F32), ("wq_T", [P, H0 // 2, D], F32),
            ("wk_T", [P, H0 // 2, D], F32))
        wv_T, wo_n = (t[:].rearrange("p n c -> p (n c)")[:, 0:H0 // 2 * D].rearrange("p (n c) -> p n c", c=D)
                      for t in (hid, rw_b))
        w1_raw = w2[:].rearrange("p n c -> p (n c)")
        rep_raw = cst[:, 0:4 * P].rearrange("p (n c) -> p n c", n=4)
        pick_raw = cst[0:3 * NE, 4 * P:4 * P + NE]
        pick8_raw = cst[0:3 * NX, 5 * P:5 * P + NX]
        maxrow_raw = cst[96:P, 28 * P:28 * P + 4 * KP].rearrange("p (j k) -> p j k", j=4)
        ones_f = h4_rows[:, 0]
        sim_sq, sim_ss, sim_t, sim_u, sim_r = (h4_rows[:, 1, NE * n:NE * n + NE] for n in range(5))
        b2_rest = h4_rows[0:3 * NX, 2:4]
        b2 = x4_rows[0:3 * NX, 0]
        g_hi, g_lo, sc, top_m = arena(
            ("g_hi", [P, H0 * KP], F32R), ("g_lo", [P, H0 * KP], F32R), ("sc", [P, NG + H0, S], F32),
            ("top_m", [P, S], F32))
        top_t = y_rows[:].rearrange("p t c -> p (t c)")
        u_main, u_tail = arena(("u_main", [P, H0, D], F32), ("u_tail", [P, NG, D], F32))
        rh, q_T, k_T, v_T, v_dup, pa, p_T, a_T = arena(
            ("rh", [P, 3, S], F32), ("q_T", [DH, S], F32), ("k_T", [DH, S], F32), ("v_T", [DH, S], F32),
            ("v_dup", [P, NT, 2, DH], F32), ("pa", [P, NT, S], F32), ("p_T", [P, NT, S], F32),
            ("a_T", [P, S], F32))
        top_p = x_rows[:].rearrange("p t c -> p (t c)")
        ks_t, qm, q_hi, q_lo, pm, mx = arena(
            ("ks_t", [P, NG, P], F32R), ("qm", [P, S], F32),
            ("q_hi", [P, S], F32R), ("q_lo", [P, S], F32R), ("pm", [P, 4, S], F32), ("mx", [P, NT, H1], F32))
        kv_f, k_hi, k_lo = y_rows[:].rearrange("p t c -> p (t c)")[:, 0:KP], hT_hi[:, 0:KP], hT_lo[:, 0:KP]
        _, qf, rz = arena(("folded_keys", [P, 2 * H0 * KP], F32), ("qf", [P, S], F32), ("rz", [P, S], F32))
        _, g_f = arena(("first_scores", [P, 2 * H0 * KP + (NG + 10) * S], F32), ("g_f", [P, 6, 3 * KP], F32))
        _, ks, qs, nm, mask_i, maskT_i, mz, mz_T = arena(
            ("gated_buffers", [P, 16 * S], F32), ("ks", [P, NG, 4, KP], F32R), ("qs", [P, NG, S], F32R),
            ("nm", [P, NT, NG, 32], F32), ("mask_i", [P, NT, SK], I32), ("maskT_i", [P, 2, S], I32),
            ("mz", [P, NT, SK], BF16), ("mz_T", [P, 2, S], BF16))

        passed = sem("passed")
        mats_loaded, fold_loaded, tables_loaded, direct_loaded = (
            sem(n) for n in ("mats_loaded", "fold_loaded", "tables_loaded", "direct_loaded"))
        gated_loaded, experts_loaded, pads_zeroed = (
            sem(n) for n in ("gated_loaded", "experts_loaded", "pads_zeroed"))
        fold2_loaded, vz_loaded, tables_done, gate_ready, w1_rounded, w1_split = (
            sem(n) for n in ("fold2_loaded", "vz_loaded", "tables_done", "gate_ready", "w1_rounded", "w1_split"))
        x_loaded, ctx_loaded, mask_loaded = sig("x_loaded", 16), sig("ctx_loaded", 16), sig("mask_loaded", 16 * 6)
        w2_loaded, out_ready, out_stored = sem("w2_loaded"), sig("out_ready", 1), sig("out_stored", 16)
        set_step, fold_ready, fold_stored, set_ready, set_pe, set_dve = (
            sem(n) for n in ("set_step", "fold_ready", "fold_stored", "set_ready", "set_pe", "set_dve"))
        dve_step, first_step, last_step = (
            sig("dve_step", DVE_STEPS), sig("first_step", FIRST_STEPS), sig("last_step", LAST_STEPS))
        pool_step = sig("pool_step", POOL_STEPS)
        h1_ready, h1T_psum, h1T_hi_ready, h1T_lo_ready = (
            sig("h1_ready", 4), sig("h1T_psum", 1), sig("h1T_hi_ready", 1), sig("h1T_lo_ready", 1))
        h_ready, hT_psum, hT_full, h4T_hi_ready, h4T_lo_ready = (
            sig("h_ready", 12), sig("hT_psum", 3), sig("hT_full", 3), sig("h4T_hi_ready", 1), sig("h4T_lo_ready", 1))
        o_psum, oT_stored, back_psum = sig("o_psum", 2), sig("oT_stored", 2), sig("back_psum", 3)
        x_in_biased, x_rows_biased, x4_biased = (
            sig("x_in_biased", 1), sig("x_rows_biased", 1), sig("x4_biased", 1))
        g_psum, g_stored, g_lo_ready = sig("g_psum", 6), sig("g_stored", 6), sig("g_lo_ready", 6)
        u_psum, u_stored = sig("u_psum", 5), sig("u_stored", 5)
        sc_psum, sc_stored = sig("sc_psum", 20), sig("sc_stored", 20)
        tail_max, tail_turned = sig("tail_max", 2), sig("tail_turned", 2)
        top_t_ready, top_m_ready = sig("top_t_ready", 1), sig("top_m_ready", 1)
        less_dve, less_pool, exp_ready = sig("less_dve", 12), sig("less_pool", 8), sig("exp_ready", 9)
        tail_sum, pool_sum, tail_den = sig("tail_sum", 1), sig("pool_sum", 1), sig("tail_den", 1)
        inv_t_ready, inv_m_ready = sig("inv_t_ready", 1), sig("inv_m_ready", 1)
        attn_dve, attn_pool = sig("attn_dve", 12), sig("attn_pool", 8)
        squares_summed = sig("squares_summed", NT)
        logit_psum, gate_arg, gate_exp = sig("logit_psum", 2), sig("gate_arg", 2), sig("gate_exp", 2)
        rw_ready, rwT_psum, rwT_stored = sig("rw_ready", 2), sig("rwT_psum", 2), sig("rwT_stored", 2)
        bc_psum, rh_ready, rh_used = sig("bc_psum", 24), sig("rh_ready", 24), sig("rh_used", 23)
        qkv_stored, v_psum, v_stored = (
            sig("qkv_stored", 2), sig("v_psum", 1), sig("v_stored", 1))
        s_psum, s_max, p_exp, p_norm = sig("s_psum", 4), sig("s_max", 4), sig("p_exp", 4), sig("p_norm", 4)
        pT_psum, pT_stored, att_psum, att_stored = (
            sig("pT_psum", 4), sig("pT_stored", 4), sig("att_psum", 1), sig("att_stored", 1))
        mz_ready, k_full, k_hi_ready, k_lo_ready = (
            sig("mz_ready", 2), sig("k_full", 1), sig("k_hi_ready", 1), sig("k_lo_ready", 1))
        mask_padded, fixed_ready = sig("mask_padded", 1), sig("fixed_ready", 3)
        krep_psum, ks_ready, kst_ready, v8_psum, v8_stored = (
            sig("krep_psum", 4), sig("ks_ready", 4), sig("kst_ready", 1), sig("v8_psum", 1), sig("v8_stored", 1))
        q_psum, qf_ready, count_psum, q_masked, q_hi_ready, q_lo_ready = (
            sig("q_psum", 1), sig("qf_ready", 1), sig("count_psum", 1), sig("q_masked", 1), sig("q_hi_ready", 1),
            sig("q_lo_ready", 1))
        qrep_psum, qs_ready, smax_psum, smax_used = (
            sig("qrep_psum", 4), sig("qs_ready", 4), sig("smax_psum", 16), sig("smax_used", 16))
        nm_ready, nmT_psum, nm_stored = sig("nm_ready", 1), sig("nmT_psum", 1), sig("nm_stored", NG)
        st_psum, pm_ready, pm_used = sig("st_psum", 20), sig("pm_ready", 20), sig("pm_used", 20)
        pv_normed = sig("pv_normed", 1)
        item_psum, item_stored = sig("item_psum", NX + NX * FC), sig("item_stored", NX + NX * FC)
        hid_used, ex_added = sig("hid_used", NX * FC), sig("ex_added", NX)
        b2_psum, acc_begun, back4_psum = sig("b2_psum", 1), sig("acc_begun", 1), sig("back4_psum", 1)

        POOL_HEADS = [12, 13, 14, 15]
        DVE_HEADS = [h for h in range(H0) if h not in POOL_HEADS]
        MIXED = [0, 1, 2, 3, 12, 13, 4, 5, 6, 7, 14, 15, 8, 9, 10, 11]

        POOL_SUM = [12, 13, 6, 7, 14, 15]
        EARLY_MAX = 4
        FRONT_BANK = [5, 1, 2]
        U_BANK = [2, 1, 3, 2, 1]
        FOLD_HEADS = [0, 1, 8, 9]
        S_BANK, PT_BANK = [1, 2, 3, 1], [0, 2, 3, 0]
        BC_BANK = [0, 1] * (NE // 2) + [0, 2] * (NE // 4)
        KREP_BANK = [2, 0, 1, 3]
        SMAX_DUO = [2, 0, 1]
        ST_TILES = [(0, None), (1, None)] + [(h // 4, h % 4) for h in range(8)] + \
            [(2, None), (3, None)] + [(h // 4, h % 4) for h in range(8, H1)]
        v8_bank = bank[7][:, 2 * P:4 * P]
        v_bank = bank[0][:, 0:NT * DH].rearrange("p (i d) -> p i d", d=DH)
        vzt_own = vz_t[:].rearrange("p (g c) -> p g c", c=VTP)

        def weight_item(e):
            return (FC + 1) * e + FC

        def hidden_item(c):
            return c + c // FC

        def rwT_bank(n, rows_):
            return bank[n].bitcast(BF16)[0:rows_, 0:S]

        def apart(eng):
            eng.sem_inc(passed, 1)

        def one(table, e, n=P):
            return table[:, e:e + 1].to_broadcast([table.shape[0], n])

        def g_main(t, h, k):
            return t[:, h * P:(h + k) * P].rearrange("p (h c) -> p h c", c=P)

        def g_tail(t, h, k):
            at = H0 * P + h * KT
            return t[:, at:at + k * KT].rearrange("p (h c) -> p h c", c=KT)

        def rows(t):
            return t.rearrange("p (t c) -> p t c", c=D)

        block = ctx.enter_context(nc.Block())

        @block.sync
        def _(sp):
            def load_x(b):
                sp.dma_start(x_in[:], a["x"][b].rearrange("(t p) c -> p t c", p=P)).then_inc(x_loaded.sem, 16)

            def load_ctx(b):
                sp.dma_start(ctx_T[:, 0:SK], a["ctx_T"][b]).then_inc(ctx_loaded.sem, 16)

            def load_masks(b):
                sp.dma_start(mask_i[:], a["mask"][b].rearrange("(t p) k -> p t k", p=P)).then_inc(mask_loaded.sem, 16)
                sp.dma_start(maskT_i[:, 0, :], a["mask_T"][b][0:P, :]).then_inc(mask_loaded.sem, 16)
                for j in range(4):
                    sp.dma_start(maskT_i[32 * j:32 * j + TAIL, 1, :], a["mask_T"][b][P:SK, :]).then_inc(
                        mask_loaded.sem, 16)

            sp.dma_start(mats[:], a["c_mats"]).then_inc(mats_loaded, 16)
            for dst, name in ((wk_T, "wk_T"), (wq_T, "wq_T")):
                sp.dma_start(dst[:], a[name].rearrange("(n p) c -> p n c", p=P)).then_inc(fold_loaded, 16)
            load_ctx(0)
            load_x(0)
            for dst, name in ((rep_raw, "c_rep"), (band[:], "c_band"), (maxrow_raw, "c_maxrow"),
                              (pick_raw, "c_pick"), (pick8_raw, "c_pick8"),
                              (first[:], "c_first")):
                sp.dma_start(dst, a[name]).then_inc(tables_loaded, 16)
            for dst, src in ((sim[:], a["sim"]), (gate[:], a["gates"].partition_broadcast(P)),
                             (ln0[:, 0], a["gamma0"].partition_broadcast(P)),
                             (ln0[:, 1], a["beta0"].partition_broadcast(P)),
                             (ln1[:, 0], a["gamma1"].partition_broadcast(P)),
                             (ln1[:, 1], a["beta1"].partition_broadcast(P)),
                             (w_att[:], a["w_att"]), (b_att[:], a["b_att"]), (w_r[:], a["w_r"]),
                             (b_r[:], a["b_r"].partition_broadcast(P)), (b1[:], a["b1"]),
                             (bo_rows[:], a["b3"].partition_broadcast(P)),
                             (b2[0:NX], a["b2"]), (b2[NX:2 * NX], a["b2"]), (b2[2 * NX:3 * NX], a["b2"])):
                sp.dma_start(dst, src).then_inc(direct_loaded, 16)
            for dst, name in ((wv_T, "wv_T"), (wo_n, "wo")):
                sp.dma_start(dst, a[name].rearrange("(n p) c -> p n c", p=P)).then_inc(fold2_loaded, 16)

            sp.dma_start(qk_w[:, :, 0:DH], a["q_proj"].rearrange("e c d -> c e d")).then_inc(gated_loaded, 16)
            sp.dma_start(qk_w[:, :, DH:], a["k_proj"].rearrange("e c d -> c e d")).then_inc(gated_loaded, 16)
            sp.dma_start(v_w[:], a["v_proj"].rearrange("e c d -> c e d")).then_inc(gated_loaded, 16)
            sp.dma_start(o_w[:], a["o_proj"].rearrange("(n w) d c -> (w d) n c", w=2)).then_inc(gated_loaded, 16)
            sp.dma_start(w1_raw, a["w1"]).then_inc(experts_loaded, 16)
            sp.dma_start(vz[:], a["c_vz"]).then_inc(vz_loaded, 16)
            sp.dma_start(vz_t[:], a["c_vzt"]).then_inc(vz_loaded, 16)
            def batch(b, more):
                sp.wait_ge(mask_padded.sem, mask_padded.after(b, 1))
                apart(sp)
                load_masks(b)
                if more:
                    sp.wait_ge(h_ready.sem, h_ready.after(b, 4))
                    apart(sp)
                    load_x(b + 1)
                    sp.wait_ge(v8_stored.sem, v8_stored.after(b, 1))
                    sp.wait_ge(k_full.sem, k_full.after(b, 1))
                    apart(sp)
                    load_ctx(b + 1)

            def store(b):
                sp.wait_ge(out_ready.sem, out_ready.after(b, 1))
                apart(sp)
                sp.dma_start(out[b].rearrange("(t p) c -> p t c", p=P), x4_rows[:]).then_inc(out_stored.sem, 16)
                sp.wait_ge(out_stored.sem, out_stored.after(b, 16))
                apart(sp)

            batch(0, True)
            sp.wait_ge(w1_split, 8)
            sp.dma_start(w2[:], a["w2"]).then_inc(w2_loaded, 16)
            with sp.Fori(1, B - 1) as b:
                batch(b, True)
                store(b - 1)
            batch(B - 1, False)
            store(B - 2)
            store(B - 1)

        @block.gpsimd
        def _(pool):
            pool.memset(ctx_T[:, SK:KP], 0.0).then_inc(pads_zeroed, 1)

            def batch(b):
                steps = [0]

                def link(ins):
                    steps[0] += 1
                    ins.then_inc(pool_step.sem, 1)
                    pool.wait_ge(pool_step.sem, pool_step.after(b, steps[0]))

                pool.wait_ge(h1_ready.sem, h1_ready.after(b, 4))
                pool.tensor_tensor(x_in[:], x_in[:], ln0[:, 1].unsqueeze(1).to_broadcast([P, NT, D]), ALU.add).then_inc(
                    x_in_biased.sem, 1)
                pool.wait_ge(top_t_ready.sem, top_t_ready.after(b, 1))
                for g in range(NG):
                    pool.tensor_tensor(sc[:, g], sc[:, g], top_t[:], ALU.subtract).then_inc(less_pool.sem, 1)
                pool.wait_ge(top_m_ready.sem, top_m_ready.after(b, 1))
                for h in POOL_HEADS:
                    pool.tensor_tensor(sc[:, NG + h], sc[:, NG + h], top_m[:], ALU.subtract).then_inc(less_pool.sem, 1)
                for n, h in enumerate(POOL_SUM[1:]):
                    pool.wait_ge(exp_ready.sem, exp_ready.after(b, MIXED.index(h) // 2 + 1))
                    ins = pool.tensor_tensor(den_p[:], den_p[:] if n else sc[:, NG + POOL_SUM[0]], sc[:, NG + h],
                                             ALU.add)
                    if h != POOL_SUM[-1]:
                        link(ins)
                ins.then_inc(pool_sum.sem, 1)
                pool.wait_ge(exp_ready.sem, exp_ready.after(b, H0 // 2 + 1))
                link(pool.tensor_tensor(top_t[:], sc[:, 0], sc[:, 1], ALU.add))
                link(pool.tensor_tensor(top_t[:], top_t[:], sc[:, 2], ALU.add))
                pool.tensor_tensor(top_t[:], top_t[:], sc[:, 3], ALU.add).then_inc(tail_sum.sem, 1)
                pool.wait_ge(inv_m_ready.sem, inv_m_ready.after(b, 1))
                for h in POOL_HEADS:
                    pool.tensor_tensor(sc[:, NG + h], sc[:, NG + h], top_m[:], ALU.mult).then_inc(attn_pool.sem, 1)
                pool.wait_ge(inv_t_ready.sem, inv_t_ready.after(b, 1))
                for g in range(NG):
                    pool.tensor_tensor(sc[:, g], sc[:, g], top_t[:], ALU.mult).then_inc(attn_pool.sem, 1)
                pool.wait_ge(h_ready.sem, h_ready.after(b, 4))
                apart(pool)
                pool.memset(maskT_i[:, 1, :], 0).then_inc(mask_padded.sem, 1)
                pool.wait_ge(mask_padded.sem, mask_padded.after(b, 1))
                apart(pool)
                pool.memset(nm[:], 0.0).then_inc(fixed_ready.sem, 1)
                pool.wait_ge(fixed_ready.sem, fixed_ready.after(b, 1))
                apart(pool)
                pool.memset(qs[96:P].bitcast(F32), 0.0).then_inc(fixed_ready.sem, 1)
                pool.wait_ge(fixed_ready.sem, fixed_ready.after(b, 2))
                apart(pool)
                pool.tensor_copy(ks[96:P], maxrow[96:P].unsqueeze(1).to_broadcast([32, NG, 4, KP])).then_inc(
                    fixed_ready.sem, 1)
                pool.wait_ge(fixed_ready.sem, fixed_ready.after(b, 3))
                pool.wait_ge(mask_loaded.sem, mask_loaded.after(b, 96))
                apart(pool)
                pool.tensor_scalar(mz[:], mask_i[:], 0.0, None, ALU.is_equal).then_inc(mz_ready.sem, 1)
                pool.tensor_scalar(mz_T[:], maskT_i[:], 0.0, None, ALU.is_equal).then_inc(mz_ready.sem, 1)
                pool.wait_ge(h_ready.sem, h_ready.after(b, 8))
                pool.tensor_tensor(x_rows[:], x_rows[:], bo_rows[:].unsqueeze(1).to_broadcast([P, NT, D]),
                                   ALU.add).then_inc(x_rows_biased.sem, 1)
                assert steps[0] == POOL_STEPS

            def last_beta(b):
                pool.wait_ge(h_ready.sem, h_ready.after(b, 12))
                pool.tensor_tensor(x4_rows[:], x4_rows[:], ln1[:, 1].unsqueeze(1).to_broadcast([P, NT, D]),
                                   ALU.add).then_inc(x4_biased.sem, 1)

            def low_keys(b):
                for n in range(6):
                    k = min(3, H0 - 3 * n)
                    pool.wait_ge(g_stored.sem, g_stored.after(b, n + 1))
                    src = g_f[:, n, 0:KP * k].rearrange("p (h c) -> p h c", c=KP)
                    pool.tensor_tensor(g_main(g_lo, 3 * n, k), src[:, :, 0:P], g_main(g_hi, 3 * n, k), ALU.subtract)
                    pool.tensor_tensor(g_tail(g_lo, 3 * n, k), src[:, :, P:KP], g_tail(g_hi, 3 * n, k),
                                       ALU.subtract).then_inc(g_lo_ready.sem, 1)

            pool.wait_ge(direct_loaded, 16 * 15)
            low_keys(0)
            batch(0)
            pool.wait_ge(w1_rounded, 4)
            for n in range(8):
                w = bass.ts(n, NX * F // 8)
                pool.tensor_tensor(w1_lo[:, w], w1_raw[:, w], w1_hi[:, w], ALU.subtract).then_inc(w1_split, 1)
            low_keys(1)
            last_beta(0)
            with pool.Fori(1, B - 1) as b:
                batch(b)
                low_keys(b + 1)
                last_beta(b)
            batch(B - 1)
            last_beta(B - 1)

        @block.scalar
        def _(act):
            def store_folds(n0, n1):
                for n in range(n0, n1):
                    act.wait_ge(fold_ready, n + 1)
                    dst, scale = (mq, DK0 ** -0.5) if n < 4 else (mo, 1.0)
                    h = FOLD_HEADS[n % 4]
                    act.activation(dst[:, h:h + 7:2], bank[n].rearrange("p (h c) -> p h c", c=D), ACT.Copy,
                                   scale=scale).then_inc(fold_stored, 1)

            def round_w1():
                act.wait_ge(experts_loaded, 16)
                for n in range(4):
                    w = bass.ts(n, NX * F // 4)
                    act.activation(w1_hi[:, w], w1_raw[:, w], ACT.Copy).then_inc(w1_rounded, 1)

            def expert_items(b, c0, c1):
                def store_weights(e):
                    act.wait_ge(item_psum.sem, item_psum.after(b, weight_item(e) + 1))
                    if e >= 3:
                        act.wait_ge(ex_added.sem, ex_added.after(b, e - 2))
                    act.activation(rw_b[:, e % 3], bank[4 + weight_item(e) % 2], ACT.Copy).then_inc(item_stored.sem, 1)

                for c in range(c0, c1):
                    e, j = divmod(c, FC)
                    if j == 0 and e > 0:
                        store_weights(e - 1)
                    act.wait_ge(item_psum.sem, item_psum.after(b, hidden_item(c) + 1))
                    if c >= 3:
                        act.wait_ge(hid_used.sem, hid_used.after(b, c - 2))
                    act.activation(hid[:, c % 3], bank[4 + hidden_item(c) % 2], ACT.Relu, bias=b1[:, c:c + 1]).then_inc(
                        item_stored.sem, 1)
                    if c == NX * FC - 1:
                        store_weights(e)

            def store_h1T(b):
                act.wait_ge(h1T_psum.sem, h1T_psum.after(b, 1))
                act.activation(hT_hi[:], bank[4], ACT.Copy).then_inc(h1T_hi_ready.sem, 1)

            def store_keys(b, *jobs):
                for n in jobs:
                    k = min(3, H0 - 3 * n)
                    act.wait_ge(g_psum.sem, g_psum.after(b, n + 1))
                    src = bank[FRONT_BANK[n % 3]][:, 0:KP * k]
                    own = src.rearrange("p (h c) -> p h c", c=KP)
                    act.activation(g_main(g_hi, 3 * n, k), own[:, :, 0:P], ACT.Copy)
                    act.activation(g_tail(g_hi, 3 * n, k), own[:, :, P:KP], ACT.Copy)
                    act.activation(g_f[:, n, 0:KP * k], src, ACT.Copy).then_inc(g_stored.sem, 1)

            def store_scores(b, t0, t1):
                for t in range(t0, t1):
                    act.wait_ge(sc_psum.sem, sc_psum.after(b, t + 1))
                    act.activation(sc[:, t], bank[FRONT_BANK[t % 3]], ACT.Copy).then_inc(sc_stored.sem, 1)

            def store_values(b, n0, n1):
                for n in range(n0, n1):
                    act.wait_ge(u_psum.sem, u_psum.after(b, n + 1))
                    dst = u_main[:, 4 * n:4 * n + 4] if n < 4 else u_tail[:]
                    act.activation(dst.rearrange("p h c -> p (h c)"), bank[U_BANK[n]], ACT.Copy).then_inc(u_stored.sem, 1)

            def batch(b, behind=True, more=True):
                def items(c0, c1):
                    if behind:
                        expert_items(b - 1, c0, c1)

                items(0, 2)
                store_values(b, 2, 5)
                items(2, 3)
                for n in range(H0 // 2):
                    h = MIXED[2 * n]
                    if h in POOL_HEADS:
                        act.wait_ge(less_pool.sem, less_pool.after(b, NG + POOL_HEADS.index(h) + 2))
                    else:
                        act.wait_ge(less_dve.sem, less_dve.after(b, DVE_HEADS.index(h) + 2))
                    act.activation(sc[:, NG + h:NG + h + 2], sc[:, NG + h:NG + h + 2], ACT.Exp).then_inc(
                        exp_ready.sem, 1)
                    if n in (0, 2, 4, 6):
                        items(3 + n // 2, 4 + n // 2)
                items(7, 8)
                act.wait_ge(less_pool.sem, less_pool.after(b, NG))
                act.activation(sc[:, 0:NG], sc[:, 0:NG], ACT.Exp).then_inc(exp_ready.sem, 1)
                items(8, 12)
                act.wait_ge(o_psum.sem, o_psum.after(b, 1))
                act.activation(oT[:], bank[0], ACT.Copy).then_inc(oT_stored.sem, 1)
                if behind:
                    items(12, 19)
                else:
                    round_w1()
                act.wait_ge(h_ready.sem, h_ready.after(b, 4))
                for t in range(NT):
                    act.activation(y_rows[:, t], h_rows[:, t], ACT.Square, accum_out=square_sums[:, t:t + 1]).then_inc(
                        squares_summed.sem, 1)
                act.wait_ge(hT_psum.sem, hT_psum.after(b, 1))
                act.activation(hT[:], bank[0], ACT.Copy).then_inc(hT_full.sem, 1)
                items(19, 24)
                act.wait_ge(gate_arg.sem, gate_arg.after(b, 1))
                act.activation(gated[:], gated[:], ACT.Exp).then_inc(gate_exp.sem, 1)
                items(24, 25)
                act.wait_ge(rwT_psum.sem, rwT_psum.after(b, 1))
                act.activation(rwT[:], rwT_bank(2, 3 * NE), ACT.Copy).then_inc(rwT_stored.sem, 1)
                items(25, 26)
                act.wait_ge(rh_used.sem, rh_used.after(b, NE))
                act.activation(q_T[:], bank[2][0:DH], ACT.Copy)
                act.activation(k_T[:], bank[2][DH:P], ACT.Copy).then_inc(qkv_stored.sem, 1)
                act.activation(v_T[:], bank[3][0:DH], ACT.Copy).then_inc(qkv_stored.sem, 1)
                act.wait_ge(v_psum.sem, v_psum.after(b, 1))
                act.activation(v_dup[:, :, 0], v_bank, ACT.Copy)
                act.activation(v_dup[:, :, 1], v_bank, ACT.Copy).then_inc(v_stored.sem, 1)
                items(26, 27)
                for i in range(NT):
                    n = P * (i + 1)
                    act.wait_ge(s_max.sem, s_max.after(b, i + 1))
                    act.activation(pa[:, i, 0:n], bank[S_BANK[i]][:, 0:n], ACT.Exp, bias=col[:, 0, i:i + 1],
                                   scale=DH ** -0.5, accum_out=col[:, 1, i:i + 1]).then_inc(p_exp.sem, 1)
                items(27, 28)
                for i in range(NT):
                    act.wait_ge(pT_psum.sem, pT_psum.after(b, i + 1))
                    act.activation(p_T[:, 0:i + 1, bass.ts(i, P)],
                                   bank[PT_BANK[i]][:, 0:P * (i + 1)].rearrange("p (j q) -> p j q", q=P),
                                   ACT.Copy).then_inc(pT_stored.sem, 1)
                act.wait_ge(att_psum.sem, att_psum.after(b, 1))
                act.activation(a_T[:], bank[1], ACT.Copy).then_inc(att_stored.sem, 1)

                act.wait_ge(v8_psum.sem, v8_psum.after(b, 1))
                act.activation(kv_f, bank[7][:, 0:KP], ACT.Identity, bias=b_att[:, 1:2]).then_inc(k_full.sem, 1)
                act.wait_ge(k_full.sem, k_full.after(b, 1))
                act.activation(k_hi, kv_f, ACT.Copy).then_inc(k_hi_ready.sem, 1)
                if not behind:
                    act.wait_ge(vz_loaded, 32)
                act.activation(vz[:].rearrange("p (h c) -> p h c", c=VZP)[:, :, 0:DK1],
                               v8_bank[:, 0:P].rearrange("p (h d) -> p h d", d=DK1), ACT.Copy)
                for j in range(4):
                    q = slice(32 * j, 32 * j + 32)
                    ins = act.activation(vzt_own[q, :, DK1 * j:DK1 * j + DK1],
                                         v8_bank[q, P:2 * P].rearrange("p (g c) -> p g c", g=NG)[
                                             :, :, DK1 * j:DK1 * j + DK1], ACT.Copy)
                ins.then_inc(v8_stored.sem, 1)

                act.wait_ge(o_psum.sem, o_psum.after(b, 2))
                act.activation(oT[:], bank[3], ACT.Copy).then_inc(oT_stored.sem, 1)
                items(28, 30)
                act.wait_ge(hT_psum.sem, hT_psum.after(b, 2))
                act.activation(hT[:], bank[3], ACT.Copy).then_inc(hT_full.sem, 1)
                items(30, 31)
                act.wait_ge(q_psum.sem, q_psum.after(b, 1))
                act.activation(qf[:], bank[2], ACT.Identity, bias=bq[:], scale=SCALE1).then_inc(qf_ready.sem, 1)
                act.wait_ge(ks_ready.sem, ks_ready.after(b, 4))
                act.wait_ge(fixed_ready.sem, fixed_ready.after(b, 3))
                act.activation(ks_t[:].rearrange("p g (j k) -> p g j k", j=4), ks[:, :, :, P:KP], ACT.Copy).then_inc(
                    kst_ready.sem, 1)

                items(31, 32)
                for g in range(NG):
                    act.wait_ge(qrep_psum.sem, qrep_psum.after(b, g + 1))
                    act.activation(qs[0:96, g], bank[g][0:96], ACT.Copy).then_inc(qs_ready.sem, 1)
                act.wait_ge(nmT_psum.sem, nmT_psum.after(b, 1))
                for g in range(NG):
                    act.activation(qs[96:104, g], bank[0][32 * g:32 * g + 8], ACT.Copy).then_inc(nm_stored.sem, 1)
                for t in range(NG + H1):
                    act.wait_ge(st_psum.sem, st_psum.after(b, t + 1))
                    if t >= 4:
                        act.wait_ge(pm_used.sem, pm_used.after(b, t - 3))
                    act.activation(pm[:, t % 4], bank[4 + t % 2], ACT.Exp).then_inc(pm_ready.sem, 1)
                if more:
                    store_h1T(b + 1)
                    store_keys(b + 1, 0, 1, 2)
                if more:
                    store_keys(b + 1, 3, 4, 5)
                    store_scores(b + 1, 0, 8)

                act.wait_ge(hT_psum.sem, hT_psum.after(b, 3))
                act.activation(hT[:], bank[0], ACT.Copy).then_inc(hT_full.sem, 1)
                act.activation(h4_hi[:], bank[0], ACT.Copy).then_inc(h4T_hi_ready.sem, 1)
                if more:
                    store_scores(b + 1, 8, 16)
                else:
                    expert_items(b, 0, 3)
                act.wait_ge(gate_arg.sem, gate_arg.after(b, 2))
                act.activation(col[:, 1], col[:, 0], ACT.Exp).then_inc(gate_exp.sem, 1)
                if not more:
                    expert_items(b, 3, 4)
                if more:
                    store_scores(b + 1, 16, NG + H0)
                act.wait_ge(rwT_psum.sem, rwT_psum.after(b, 2))
                act.activation(rw4T[:], rwT_bank(3, 3 * NX), ACT.Copy).then_inc(rwT_stored.sem, 1)
                if more:
                    store_values(b + 1, 0, 1)
                act.wait_ge(b2_psum.sem, b2_psum.after(b, 1))
                act.activation(acc[:], bank[3], ACT.Copy).then_inc(acc_begun.sem, 1)
                if more:
                    store_values(b + 1, 1, 2)

            store_folds(0, 4)
            store_h1T(0)
            store_keys(0, *range(6))
            act.wait_ge(tables_done, 1)
            store_scores(0, 0, NG + H0)
            act.wait_ge(direct_loaded, 16 * 15)
            act.activation(gate[:], gate[:], ACT.Exp, scale=-1.0).then_inc(gate_ready, 1)
            store_folds(4, 8)
            store_values(0, 0, 2)
            batch(0, behind=False)
            with act.Fori(1, B - 1) as b:
                batch(b)
            batch(B - 1, more=False)
            expert_items(B - 1, 4, NX * FC)

        @block.tensor
        def _(pe):
            def folds(n0, n1):
                for n in range(n0, n1):
                    for i in range(4):
                        h = FOLD_HEADS[n % 4] + 2 * i
                        q = slice(DK0 * (h % 2), DK0 * (h % 2) + DK0)
                        l, r = (wk_T, wq_T) if n < 4 else (wv_T, wo_n)
                        mm = pe.matmul(bank[n][:, bass.ts(i, P)], l[q, h // 2], r[q, h // 2], start=True, stop=True)
                    mm.then_inc(fold_ready, 1)
            def turn_in(h, dst, done=hT_psum):
                for i in range(NT):
                    mm = pe.transpose(dst[:, bass.ts(i, P)], h[:, i], ident)
                mm.then_inc(done.sem, 1)

            def turn_back(src, dst, done):
                for i in range(NT):
                    mm = pe.transpose(dst[:, bass.ts(i, P)], src[:, bass.ts(i, P)], ident)
                mm.then_inc(done.sem, 1)

            def split3(dst, hi, lo, m_hi, m_lo):
                pe.matmul(dst, hi, m_hi, start=True, stop=False)
                pe.matmul(dst, hi, m_lo, start=False, stop=False)
                return pe.matmul(dst, lo, m_hi, start=False, stop=True)

            def logits(dst, w, n):
                for i in range(NT):
                    mm = pe.matmul(dst[:, n * i:n * i + n], hT[:, bass.ts(i, P)], w, start=True, stop=True)
                mm.then_inc(logit_psum.sem, 1)

            def turn_weights(b, k, n, dst_rw):
                pe.wait_ge(rw_ready.sem, rw_ready.after(b, k))
                apart(pe)
                for i in range(NT):
                    mm = pe.transpose(dst_rw[:, bass.ts(i, P)], rw_parts[:, i, 0:3 * n], ident_b[:])
                mm.then_inc(rwT_psum.sem, 1)

            def expert_weights(b, e):
                i = weight_item(e)
                if i >= 2:
                    pe.wait_ge(item_stored.sem, item_stored.after(b, i - 1))
                pe.matmul(bank[4 + i % 2], one(pick8, e), rw4T[:], start=True, stop=True).then_inc(item_psum.sem, 1)

            def layer1(b, c):
                if c % FC == 0 and c > 0:
                    expert_weights(b, c // FC - 1)
                i = hidden_item(c)
                if i >= 2:
                    pe.wait_ge(item_stored.sem, item_stored.after(b, i - 1))
                w = bass.ts(c, P)
                split3(bank[4 + i % 2], w1_hi[:, w], w1_lo[:, w], h4_hi[:], h4_lo[:]).then_inc(item_psum.sem, 1)
                if c == NX * FC - 1:
                    expert_weights(b, NX - 1)

            def layer2(b, c):
                e, j = divmod(c, FC)
                if j == 0 and e >= 2:
                    pe.wait_ge(ex_added.sem, ex_added.after(b, e - 1))
                pe.wait_ge(item_stored.sem, item_stored.after(b, hidden_item(c) + 1))
                pe.matmul(bank[6 + e % 2], w2[:, c], hid[:, c % 3], start=(j == 0), stop=(j == FC - 1)).then_inc(
                    hid_used.sem, 1)

            def expert_steps(b, c0, c1):
                for half in range(int(2 * c0), int(2 * c1)):
                    c = half // 2
                    if half % 2 == 0:
                        layer2(b, c)
                    elif c + 2 < NX * FC:
                        layer1(b, c + 2)

            def turn_h1(b):
                pe.wait_ge(h1_ready.sem, h1_ready.after(b, 4))
                turn_in(h_rows, bank[4], h1T_psum)

            def folded_keys(b, *jobs):
                for n in jobs:
                    if n == 0:
                        pe.wait_ge(ctx_loaded.sem, ctx_loaded.after(b, 16))
                    if n >= 3:
                        pe.wait_ge(g_stored.sem, g_stored.after(b, n - 2))
                    for i in range(min(3, H0 - 3 * n)):
                        mm = pe.matmul(bank[FRONT_BANK[n % 3]][:, KP * i:KP * i + KP], mq[:, 3 * n + i], ctx_T[:],
                                       start=True, stop=True)
                    mm.then_inc(g_psum.sem, 1)

            def scores(b, t0, t1):
                for t in range(t0, t1):
                    if t == 0:
                        pe.wait_ge(h1T_lo_ready.sem, h1T_lo_ready.after(b, 1))
                    if t < NG:
                        pe.wait_ge(g_lo_ready.sem, g_lo_ready.after(b, (4 * t + 3) // 3 + 1))
                        pe.wait_ge(g_stored.sem, g_stored.after(b, min(6, t + 4)))
                    if t >= 3:
                        pe.wait_ge(sc_stored.sem, sc_stored.after(b, t - 2))
                    at = H0 * P + t * P if t < NG else (t - NG) * P
                    hi, lo = (g[:, at:at + P] for g in (g_hi, g_lo))
                    split3(bank[FRONT_BANK[t % 3]], hi, lo, hT_hi[:], hT_lo[:]).then_inc(sc_psum.sem, 1)

            def folded_values(b, n0, n1):
                for n in range(n0, n1):
                    dst = bank[U_BANK[n]]
                    if n < 2:
                        pe.wait_ge(sc_stored.sem, sc_stored.after(b, (18, 20)[n]))
                    elif n == 2:
                        pe.wait_ge(sc_stored.sem, sc_stored.after(b, NG + H0))
                    else:
                        pe.wait_ge(u_stored.sem, u_stored.after(b, n - 2))
                    if n < 4:
                        mm = pe.matmul(dst, ctx_T[:, 0:P], mo[:, 4 * n:4 * n + 4].rearrange("p h c -> p (h c)"),
                                       start=True, stop=True)
                    else:
                        for j in range(4):
                            mm = pe.matmul(dst[32 * j:32 * j + 32].rearrange("p (g c) -> p g c", g=NG),
                                           ctx_T[:, P:KP], mo[:].rearrange("p (g j) c -> p j g c", j=4)[:, j],
                                           start=True, stop=True, tile_position=(0, 32 * j))
                    mm.then_inc(u_psum.sem, 1)

            def turn_tails(b, n):
                pe.wait_ge(tail_max.sem, tail_max.after(b, n))
                pe.matmul(bank[0], (perm64, perm32)[n - 1], top_t[:], start=True, stop=True).then_inc(tail_turned.sem, 1)

            def batch(b, behind=True, more=True):
                def steps(c0, c1):
                    if behind:
                        expert_steps(b - 1, c0, c1)

                pe.wait_ge(sc_stored.sem, sc_stored.after(b, NG + H0))
                if behind:
                    layer1(b - 1, 0)
                    layer1(b - 1, 1)
                folded_values(b, 2, 5)
                steps(0, 10.5)
                pe.wait_ge(u_stored.sem, u_stored.after(b, 5))
                for n, h in enumerate(MIXED):
                    if h in POOL_HEADS:
                        pe.wait_ge(attn_pool.sem, attn_pool.after(b, POOL_HEADS.index(h) + 1))
                    else:
                        pe.wait_ge(attn_dve.sem, attn_dve.after(b, DVE_HEADS.index(h) + 1))
                    pe.matmul(bank[0], u_main[:, h], sc[:, NG + h], start=(n == 0), stop=False)
                    if n == 2:
                        pe.wait_ge(tail_sum.sem, tail_sum.after(b, 1))
                        pe.matmul(bank[1], same, top_t[:], start=True, stop=True).then_inc(tail_den.sem, 1)
                for g in range(NG):
                    pe.wait_ge(attn_pool.sem, attn_pool.after(b, len(POOL_HEADS) + g + 1))
                    mm = pe.matmul(bank[0], u_tail[:, g], sc[:, g], start=False, stop=(g == NG - 1))
                mm.then_inc(o_psum.sem, 1)
                steps(10.5, 11)
                pe.wait_ge(oT_stored.sem, oT_stored.after(b, 1))
                turn_back(oT, bank[2], back_psum)
                steps(11, 18)

                pe.wait_ge(h_ready.sem, h_ready.after(b, 4))
                turn_in(h_rows, bank[0])
                steps(18, 18.5)
                pe.wait_ge(hT_full.sem, hT_full.after(b, 1))
                if not behind:
                    pe.wait_ge(set_dve, 1)
                logits(bank[1], sim_n[:], NE)
                steps(18.5, 23.5)
                turn_weights(b, 1, NE, rwT_bank(2, 3 * NE))
                steps(23.5, 24)
                pe.wait_ge(rwT_stored.sem, rwT_stored.after(b, 1))

                def spread(table, n):
                    pe.matmul(bank[BC_BANK[n]], table, rwT[:], start=True, stop=True).then_inc(bc_psum.sem, 1)

                def spread_pair(n):
                    m = NE + n
                    pe.matmul(bank[BC_BANK[m]][0:DH], one(pick, 2 * n, DH), rwT[:], start=True, stop=True)
                    pe.matmul(bank[BC_BANK[m]][DH:P], one(pick, 2 * n + 1, DH), rwT[:], start=True,
                              stop=True).then_inc(bc_psum.sem, 1)

                spread(one(pick, 0), 0)
                spread(one(pick, 1), 1)
                steps(24, 24.5)
                for e in range(NE):
                    pe.wait_ge(rh_ready.sem, rh_ready.after(b, e + 1))
                    pe.matmul(bank[2], qk_w[:, e], rh[:, e % 3], start=(e == 0), stop=(e == NE - 1))
                    mm = pe.matmul(bank[3][0:DH], v_w[:, e], rh[:, e % 3], start=(e == 0), stop=(e == NE - 1))
                    mm.then_inc(rh_used.sem, 1)
                    if e + 2 < NE:
                        spread(one(pick, e + 2), e + 2)
                steps(24.5, 25)
                pe.wait_ge(qkv_stored.sem, qkv_stored.after(b, 1))
                for i in range(NT):
                    if i == 2:
                        pe.wait_ge(qkv_stored.sem, qkv_stored.after(b, 2))
                        apart(pe)
                        for j in range(NT):
                            mm = pe.transpose(v_bank[:, j], v_T[:, bass.ts(j, P)], ident[0:DH, 0:DH])
                        mm.then_inc(v_psum.sem, 1)
                    if i == 3:
                        pe.wait_ge(p_exp.sem, p_exp.after(b, 1))
                    dst = bank[S_BANK[i]]
                    pe.matmul(dst[:, 0:P * (i + 1)], q_T[:, bass.ts(i, P)], k_T[:, 0:P * (i + 1)], start=True,
                              stop=False)
                    pe.matmul(dst[:, bass.ts(i, P)], ident_b[:], causal_b[:], start=False, stop=True).then_inc(
                        s_psum.sem, 1)
                pe.wait_ge(v_stored.sem, v_stored.after(b, 1))
                steps(25, 26)
                for i in range(NT):
                    pe.wait_ge(p_norm.sem, p_norm.after(b, i + 1))
                    if i == 3:
                        pe.wait_ge(pT_stored.sem, pT_stored.after(b, 1))
                    for j in range(i + 1):
                        mm = pe.transpose(bank[PT_BANK[i]][:, bass.ts(j, P)], pa[:, i, bass.ts(j, P)], ident)
                    mm.then_inc(pT_psum.sem, 1)
                pe.wait_ge(pT_stored.sem, pT_stored.after(b, 4))
                for j in range(NT):
                    mm = pe.matmul(bank[1][:, P * j:S], v_dup[:, j].rearrange("p a d -> p (a d)"),
                                   p_T[:, j, P * j:S], start=(j == 0), stop=(j == NT - 1))
                mm.then_inc(att_psum.sem, 1)
                spread_pair(0)
                spread_pair(1)
                if behind:
                    pe.wait_ge(ex_added.sem, ex_added.after(b - 1, 6))
                pe.matmul(bank[7][:, 0:KP], w_att[:, 1], ctx_T[:], start=True, stop=True)
                pe.matmul(v8_bank[:, 0:P], ctx_T[:, 0:P], w_att[:, 2], start=True, stop=True)
                for j in range(4):
                    mm = pe.matmul(v8_bank[32 * j:32 * j + 32, P:2 * P], ctx_T[:, P:KP], w_att[:, 2], start=True,
                                   stop=True, tile_position=(0, 32 * j))
                mm.then_inc(v8_psum.sem, 1)
                for n in range(NE // 2):
                    pe.wait_ge(rh_ready.sem, rh_ready.after(b, NE + n + 1))
                    mm = pe.matmul(bank[3], o_w[:, n], rh[:, (NE + n) % 3], start=(n == 0), stop=(n == NE // 2 - 1))
                    if n < NE // 2 - 1:
                        mm.then_inc(rh_used.sem, 1)
                    else:
                        mm.then_inc(o_psum.sem, 1)
                    if n + 2 < NE // 2:
                        spread_pair(n + 2)
                steps(26, 26.5)
                pe.wait_ge(oT_stored.sem, oT_stored.after(b, 2))
                turn_back(oT, bank[1], back_psum)
                pe.wait_ge(v8_stored.sem, v8_stored.after(b, 1))
                steps(26.5, 29.5)

                def keys(g):
                    q = slice(32 * g, 32 * g + 32)
                    dst = bank[KREP_BANK[g]][:, 0:KP]
                    pe.matmul(dst, rep[q, 0], k_hi[q], start=True, stop=False)
                    pe.matmul(dst, rep[q, 1], k_lo[q], start=False, stop=True).then_inc(krep_psum.sem, 1)

                pe.wait_ge(k_lo_ready.sem, k_lo_ready.after(b, 1))
                keys(0)
                keys(1)

                pe.wait_ge(h_ready.sem, h_ready.after(b, 8))
                turn_in(h_rows, bank[3])
                keys(2)
                pe.wait_ge(hT_full.sem, hT_full.after(b, 2))
                keys(3)
                pe.wait_ge(ks_ready.sem, ks_ready.after(b, 1))
                pe.matmul(bank[2], w_att[:, 0], hT[:], start=True, stop=True).then_inc(q_psum.sem, 1)
                pe.wait_ge(mz_ready.sem, mz_ready.after(b, 2))
                pe.wait_ge(ks_ready.sem, ks_ready.after(b, 2))
                pe.matmul(bank[0], ones_b[:], mz_T[:, 0], start=True, stop=False)
                pe.matmul(bank[0], ones_b[0:32], mz_T[0:32, 1], start=False, stop=True).then_inc(count_psum.sem, 1)
                steps(29.5, 30)
                pe.wait_ge(q_lo_ready.sem, q_lo_ready.after(b, 1))
                pe.wait_ge(v8_stored.sem, v8_stored.after(b, 1))
                for g in range(NG):
                    q = slice(32 * g, 32 * g + 32)
                    pe.matmul(bank[g], rep[q, 2], q_hi[q], start=True, stop=False)
                    pe.matmul(bank[g], rep[q, 3], q_lo[q], start=False, stop=True).then_inc(qrep_psum.sem, 1)
                for i in range(NT):
                    for g in range(NG):
                        n = NG * i + g
                        if n == 0 and behind:
                            pe.wait_ge(item_stored.sem, item_stored.after(b - 1, NX + NX * FC))
                        if n < 3:
                            pe.wait_ge(qs_ready.sem, qs_ready.after(b, (1, 2, 4)[n]))
                        if n >= 3:
                            pe.wait_ge(smax_used.sem, smax_used.after(b, n - 2))
                        for w in range(2):
                            dst = duo[SMAX_DUO[n % 3]][:, w, 0:2 * SK].rearrange("p (j k) -> p j k", j=2)
                            pe.matmul(dst, qs[0:96, g, bass.ts(i, P)], ks[0:96, g, 2 * w:2 * w + 2, 0:SK], start=True,
                                      stop=False)
                            mm = pe.matmul(dst, neg_b[:], mz[:, i].unsqueeze(1).to_broadcast([P, 2, SK]),
                                           start=False, stop=True)
                        mm.then_inc(smax_psum.sem, 1)
                        if n == 4:
                            steps(30, 31)
                        if n == 9:
                            steps(31, 32)
                pe.wait_ge(fixed_ready.sem, fixed_ready.after(b, 3))
                pe.wait_ge(nm_ready.sem, nm_ready.after(b, 1))
                for i in range(NT):
                    mm = pe.transpose(bank[0][:, bass.ts(i, P)], nm[:, i].rearrange("p g c -> p (g c)"), ident)
                mm.then_inc(nmT_psum.sem, 1)

                def scores_T(t):
                    g, j = ST_TILES[t]
                    pe.wait_ge(nm_stored.sem, nm_stored.after(b, g + 1))
                    if t >= 2:
                        pe.wait_ge(pm_ready.sem, pm_ready.after(b, t - 1))
                    if j is None:
                        pe.wait_ge(kst_ready.sem, kst_ready.after(b, 1))
                    keys = ks_t[:, g] if j is None else ks[:, g, j, 0:P]
                    pe.matmul(bank[4 + t % 2], keys, qs[:, g], start=True, stop=False)
                    pe.matmul(bank[4 + t % 2], neg_b[:], mz_T[:, int(j is None)], start=False, stop=True).then_inc(
                        st_psum.sem, 1)

                scores_T(0)
                scores_T(1)
                if behind:
                    pe.wait_ge(ex_added.sem, ex_added.after(b - 1, NX - 1))
                for t, (g, j) in enumerate(ST_TILES):
                    pe.wait_ge(pm_ready.sem, pm_ready.after(b, t + 1))
                    w = vz_t[:, P * g:P * g + P] if j is None else vz[:, P * (4 * g + j):P * (4 * g + j) + P]
                    mm = pe.matmul(bank[6 + g // 2], w, pm[:, t % 4], start=(t % 10 == 0), stop=(t % 10 == 9))
                    mm.then_inc(pm_used.sem, 1)
                    if t + 2 < NG + H1:
                        scores_T(t + 2)
                    if t == 4 and behind:
                        pe.wait_ge(ex_added.sem, ex_added.after(b - 1, NX))
                        turn_back(acc, bank[1], back4_psum)
                if more:
                    turn_h1(b + 1)
                    folded_keys(b + 1, 0, 1, 2, 3)
                pe.wait_ge(pv_normed.sem, pv_normed.after(b, 1))
                for i in range(NT):
                    mm = pe.matmul(bank[3][:, bass.ts(i, D)], qf[:, bass.ts(i, P)], w_att[:, 3], start=True, stop=True)
                mm.then_inc(back_psum.sem, 1)
                if more:
                    folded_keys(b + 1, 4, 5)
                    scores(b + 1, 0, 8)

                pe.wait_ge(h_ready.sem, h_ready.after(b, 12))
                turn_in(h4_rows, bank[0])
                if more:
                    scores(b + 1, 8, 10)
                pe.wait_ge(hT_full.sem, hT_full.after(b, 3))
                logits(bank[3], w_r[:], NX)
                if more:
                    scores(b + 1, 10, 14)
                    pe.wait_ge(h4T_lo_ready.sem, h4T_lo_ready.after(b, 1))
                    turn_tails(b + 1, 1)
                    scores(b + 1, 14, NG + H0)
                    turn_tails(b + 1, 2)
                else:
                    pe.wait_ge(h4T_lo_ready.sem, h4T_lo_ready.after(b, 1))
                    layer1(b, 0)
                    layer1(b, 1)
                    expert_steps(b, 0, 2.5)
                turn_weights(b, 2, NX, rwT_bank(3, 3 * NX))
                if more:
                    folded_values(b + 1, 0, 1)
                pe.wait_ge(rwT_stored.sem, rwT_stored.after(b, 2))
                for n in range(3):
                    mm = pe.matmul(bank[3], b2_parts[:, n], rw4T[:], start=(n == 0), stop=(n == 2))
                mm.then_inc(b2_psum.sem, 1)
                if more:
                    folded_values(b + 1, 1, 2)
                pe.wait_ge(h4T_lo_ready.sem, h4T_lo_ready.after(b, 1))
                pe.wait_ge(acc_begun.sem, acc_begun.after(b, 1))

            pe.wait_ge(fold_loaded, 32)
            folds(0, 4)
            pe.wait_ge(mats_loaded, 16)
            turn_h1(0)
            pe.wait_ge(fold_stored, 4)
            pe.wait_ge(pads_zeroed, 1)
            folded_keys(0, *range(6))
            scores(0, 0, NG + H0)
            pe.wait_ge(fold2_loaded, 32)
            pe.wait_ge(sc_stored.sem, sc_stored.after(0, NG + H0))
            folds(4, 6)
            turn_tails(0, 1)

            folds(6, 7)
            turn_tails(0, 2)
            folds(7, 8)
            pe.wait_ge(fold_stored, 8)
            pe.wait_ge(set_ready, 1)
            pe.matmul(bank[6][:, 0:NE], ones_f, sim_sq, start=True, stop=True).then_inc(set_pe, 1)
            pe.matmul(bank[7][:, 0:D], b_att[:, 2:3].to_broadcast([P, P]), w_att[:, 3], start=True, stop=True).then_inc(
                set_pe, 1)
            folded_values(0, 0, 2)
            pe.wait_ge(gated_loaded, 64)
            batch(0, behind=False)
            pe.wait_ge(w1_split, 8)
            pe.wait_ge(w2_loaded, 16)
            with pe.Fori(1, B - 1) as b:
                batch(b)
            batch(B - 1, more=False)
            expert_steps(B - 1, 2.5, NX * FC)
            pe.wait_ge(ex_added.sem, ex_added.after(B - 1, NX))
            turn_back(acc, bank[1], back4_psum)

        @block.vector
        def _(dve):
            def rsqrt(v, y, t, u, link):
                link(dve.tensor_scalar(t.bitcast(I32), v.bitcast(I32), 1, None, ALU.arith_shift_right))
                link(dve.tensor_scalar(y.bitcast(I32), t.bitcast(I32), -1.0, MAGIC, ALU.mult, ALU.add))
                link(dve.scalar_tensor_tensor(t, y, -0.375 * STEP_B, v, ALU.mult, ALU.mult))
                link(dve.tensor_tensor(u, t, y, ALU.mult))
                link(dve.scalar_tensor_tensor(y, u, 0.375 * STEP_A, y, ALU.add, ALU.mult))
                link(dve.scalar_tensor_tensor(t, y, 0.375 ** -2, v, ALU.mult, ALU.mult))
                link(dve.tensor_tensor(u, t, y, ALU.mult))
                link(dve.scalar_tensor_tensor(t, u, -10 / 3, u, ALU.add, ALU.mult))
                link(dve.scalar_tensor_tensor(y, t, 5.0, y, ALU.add, ALU.mult))

            done = [0]

            def set_link(ins):
                done[0] += 1
                ins.then_inc(set_step, 1)
                dve.wait_ge(set_step, done[0])

            def tables():
                dve.memset(ones_b[:], 1.0)
                dve.memset(ones_f, 1.0)
                dve.wait_ge(mats_loaded, 16)
                dve.tensor_copy(ident_b[:], ident)
                dve.tensor_scalar(causal_b[:], after_, -HUGE, None, ALU.mult)
                dve.tensor_scalar(neg_b[:], ident, NEG, None, ALU.mult)
                dve.wait_ge(tables_loaded, 16 * 6)
                dve.tensor_copy(rep[:], rep_raw)
                dve.tensor_copy(pick[:], pick_raw)
                dve.tensor_copy(pick8[:], pick8_raw)
                dve.tensor_copy(maxrow[96:P], maxrow_raw).then_inc(tables_done, 1)

            def split_b2():
                dve.wait_ge(direct_loaded, 16 * 15)
                dve.tensor_scalar(bq[:], b_att[:, 0:1], SCALE1, None, ALU.mult)
                set_link(dve.tensor_copy(b2_parts[:, 0], b2))
                set_link(dve.tensor_tensor(b2_rest[:, 0], b2, b2_parts[:, 0], ALU.subtract))
                set_link(dve.tensor_copy(b2_parts[:, 1], b2_rest[:, 0]))
                set_link(dve.tensor_tensor(b2_rest[:, 1], b2_rest[:, 0], b2_parts[:, 1], ALU.subtract))
                dve.tensor_copy(b2_parts[:, 2], b2_rest[:, 1])
                dve.tensor_tensor(sim_sq, sim[:], sim[:], ALU.mult).then_inc(set_ready, 1)

            def norms_and_gates():
                dve.wait_ge(set_pe, 2)
                dve.tensor_tensor(bo_rows[:], bank[7][:, 0:D], bo_rows[:], ALU.add)
                set_link(dve.tensor_scalar(sim_ss, bank[6][:, 0:NE], 1e-24, None, ALU.max))
                rsqrt(sim_ss, sim_r, sim_t, sim_u, set_link)
                dve.tensor_tensor(sim_n[:], sim[:], sim_r, ALU.mult)
                dve.wait_ge(gate_ready, 1)
                set_link(dve.tensor_scalar(gate[:], gate[:], 1.0, None, ALU.add))
                dve.reciprocal(gate[:], gate[:]).then_inc(set_dve, 1)

            def over_tokens(v, n):
                return v.unsqueeze(2).to_broadcast([P, NT, n])

            def over_tiles(v, n):
                return v.unsqueeze(1).to_broadcast([P, NT, n])

            def moments(src, link):
                for t in range(NT):
                    ins = dve.bn_stats(stats[:, t], src[:, t])
                link(ins)
                apart(dve)
                for t in range(NT):
                    ins = dve.bn_aggr(mv[:, t], stats[:, t])
                link(ins)
                link(dve.tensor_scalar(nv[:], mv[:, :, 1], LN_EPS, None, ALU.add))
                rsqrt(nv[:], ny[:], nt_[:], nu[:], link)

            def normalise(src, dst, link, ready, value):
                moments(src, link)
                for t in range(NT):
                    dve.tensor_scalar(dst[:, t], src[:, t], mv[:, t, 0:1], ny[:, t:t + 1], ALU.subtract,
                                      ALU.mult).then_inc(ready.sem, 1)
                dve.wait_ge(ready.sem, value)

            def post_norm(y, gamma, rest, dst, link):
                moments(y, link)
                for t in range(NT):
                    ins = dve.scalar_tensor_tensor(y[:, t], y[:, t], mv[:, t, 0:1], gamma, ALU.subtract, ALU.mult)
                link(ins)
                for t in range(NT):
                    ins = dve.scalar_tensor_tensor(dst[:, t], y[:, t], ny[:, t:t + 1], rest[:, t], ALU.mult, ALU.add)
                return ins

            def first_chain(b, done):
                count = [done]

                def link(ins):
                    count[0] += 1
                    ins.then_inc(first_step.sem, 1)
                    dve.wait_ge(first_step.sem, first_step.after(b, count[0]))

                return link, count

            def first_norm(b):
                link, count = first_chain(b, 0)
                dve.wait_ge(x_loaded.sem, x_loaded.after(b, 16))
                normalise(x_in, h_rows, link, h1_ready, h1_ready.after(b, 4))
                assert count[0] == FIRST_STEPS - 1, count

            def split_h1(b):
                dve.wait_ge(h1T_hi_ready.sem, h1T_hi_ready.after(b, 1))
                dve.tensor_tensor(hT_lo[:], bank[4], hT_hi[:], ALU.subtract).then_inc(h1T_lo_ready.sem, 1)

            def over_sc(dst, t, n, op):
                return dve.tensor_reduce(dst, sc[:, t:t + n].rearrange("p t q -> p q t"), AX.X, op)

            def early_maxima(b):
                link, count = first_chain(b, FIRST_STEPS - 1)
                dve.wait_ge(sc_stored.sem, sc_stored.after(b, NG))
                over_sc(top_t[:], 0, NG, ALU.max).then_inc(tail_max.sem, 1)
                dve.wait_ge(sc_stored.sem, sc_stored.after(b, NG + EARLY_MAX))
                link(over_sc(top_m[:], NG, EARLY_MAX, ALU.max))
                assert count[0] == FIRST_STEPS, count

            def turned_tails(b, n):
                dve.wait_ge(tail_turned.sem, tail_turned.after(b, n))
                dve.wait_ge(tail_max.sem, tail_max.after(b, n))
                dve.tensor_tensor(top_t[:], top_t[:], bank[0], ALU.max).then_inc(
                    (tail_max if n == 1 else top_t_ready).sem, 1)

            def add_expert(b, e):
                if e == 0:
                    dve.wait_ge(acc_begun.sem, acc_begun.after(b, 1))
                dve.wait_ge(item_stored.sem, item_stored.after(b, weight_item(e) + 1))
                dve.wait_ge(hid_used.sem, hid_used.after(b, FC * (e + 1)))
                dve.tensor_tensor(rw_b[:, e % 3], bank[6 + e % 2], rw_b[:, e % 3], ALU.mult).then_inc(last_step.sem, 1)
                dve.wait_ge(last_step.sem, last_step.after(b, e + 1))
                dve.tensor_tensor(acc[:], acc[:], rw_b[:, e % 3], ALU.add).then_inc(ex_added.sem, 1)
                dve.wait_ge(ex_added.sem, ex_added.after(b, e + 1))

            def last_norm(b):
                count = [NX]

                def link(ins):
                    count[0] += 1
                    ins.then_inc(last_step.sem, 1)
                    dve.wait_ge(last_step.sem, last_step.after(b, count[0]))

                dve.wait_ge(back4_psum.sem, back4_psum.after(b, 1))
                link(dve.tensor_tensor(y_rows[:], rows(bank[1]), h4_rows[:], ALU.add))
                dve.wait_ge(x4_biased.sem, x4_biased.after(b, 1))
                post_norm(y_rows, ln1[:, 0], x4_rows, x4_rows, link).then_inc(out_ready.sem, 1)
                assert count[0] == LAST_STEPS, count

            def batch(b, behind=True, more=True):
                steps = [0]

                def link(ins):
                    steps[0] += 1
                    ins.then_inc(dve_step.sem, 1)
                    dve.wait_ge(dve_step.sem, dve_step.after(b, steps[0]))

                def add_experts(*experts):
                    if behind:
                        for e in experts:
                            add_expert(b - 1, e)

                def first_best(src, n, best, sel):
                    link(dve.tensor_reduce(best, src, AX.X, ALU.max))
                    link(dve.tensor_tensor(eq[:, :, 0:n], src, over_tokens(best, n), ALU.is_equal))
                    link(dve.tensor_tensor(pr[:, :, 0:n], eq[:, :, 0:n], first[:, :, 0:n], ALU.mult))
                    link(dve.tensor_reduce(col[:, 3], pr[:, :, 0:n], AX.X, ALU.max))
                    link(dve.tensor_tensor(sel, pr[:, :, 0:n], over_tokens(col[:, 3], n), ALU.is_equal))

                def best_two(n):
                    v, v2 = lg[:, :, 0:n], lg2[:, :, 0:n]
                    first_best(v, n, top[:, 0], s1[:, :, 0:n])
                    link(dve.scalar_tensor_tensor(v2, s1[:, :, 0:n], -HUGE, v, ALU.mult, ALU.add))
                    first_best(v2, n, top[:, 1], s2[:, :, 0:n])

                def split_weights(n):
                    w, rest = rw[:, :, 0:n], [rw_rest[:, k, :, 0:n] for k in range(2)]
                    part_of = [rw_parts[:, :, n * k:n * k + n] for k in range(3)]
                    link(dve.tensor_copy(part_of[0], w))
                    link(dve.tensor_tensor(rest[0], w, part_of[0], ALU.subtract))
                    link(dve.tensor_copy(part_of[1], rest[0]))
                    link(dve.tensor_tensor(rest[1], rest[0], part_of[1], ALU.subtract))
                    dve.tensor_copy(part_of[2], rest[1]).then_inc(rw_ready.sem, 1)

                turned_tails(b, 2)
                dve.wait_ge(sc_stored.sem, sc_stored.after(b, NG + H0))
                link(over_sc(top_p[:], NG + EARLY_MAX, H0 - EARLY_MAX, ALU.max))
                dve.tensor_tensor(top_m[:], top_m[:], top_p[:], ALU.max).then_inc(top_m_ready.sem, 1)
                dve.wait_ge(top_m_ready.sem, top_m_ready.after(b, 1))
                for h in DVE_HEADS:
                    dve.tensor_tensor(sc[:, NG + h], sc[:, NG + h], top_m[:], ALU.subtract).then_inc(less_dve.sem, 1)
                dve.wait_ge(less_pool.sem, less_pool.after(b, NG + len(POOL_HEADS)))
                dve.wait_ge(less_dve.sem, less_dve.after(b, len(DVE_HEADS)))
                dve.wait_ge(exp_ready.sem, exp_ready.after(b, MIXED.index(5) // 2 + 1))
                link(over_sc(top_m[:], NG, 6, ALU.add))
                add_experts(0)
                dve.wait_ge(exp_ready.sem, exp_ready.after(b, MIXED.index(11) // 2 + 1))
                link(over_sc(top_p[:], NG + 8, 4, ALU.add))
                link(dve.tensor_tensor(top_m[:], top_m[:], top_p[:], ALU.add))
                dve.wait_ge(pool_sum.sem, pool_sum.after(b, 1))
                link(dve.tensor_tensor(top_m[:], top_m[:], den_p[:], ALU.add))
                dve.reciprocal(top_m[:], top_m[:]).then_inc(inv_m_ready.sem, 1)
                dve.wait_ge(inv_m_ready.sem, inv_m_ready.after(b, 1))
                for h in DVE_HEADS:
                    dve.tensor_tensor(sc[:, NG + h], sc[:, NG + h], top_m[:], ALU.mult).then_inc(attn_dve.sem, 1)
                    if h == 7:
                        dve.wait_ge(tail_den.sem, tail_den.after(b, 1))
                        dve.reciprocal(top_t[:], bank[1]).then_inc(inv_t_ready.sem, 1)
                add_experts(1)
                if not behind:
                    norms_and_gates()
                dve.wait_ge(back_psum.sem, back_psum.after(b, 1))
                link(dve.tensor_tensor(y_rows[:], rows(bank[2]), h_rows[:], ALU.add))
                dve.wait_ge(x_in_biased.sem, x_in_biased.after(b, 1))
                link(post_norm(y_rows, ln0[:, 0], x_in, x_rows, link))
                add_experts(2)

                normalise(x_rows, h_rows, link, h_ready, h_ready.after(b, 4))
                add_experts(3)
                dve.wait_ge(squares_summed.sem, squares_summed.after(b, NT))
                link(dve.tensor_scalar(nv[:], square_sums[:], 1e-24, None, ALU.max))
                rsqrt(nv[:], ny[:], nt_[:], nu[:], link)
                dve.wait_ge(logit_psum.sem, logit_psum.after(b, 1))
                link(dve.tensor_tensor(lg[:], bank[1][:, 0:NT * NE].rearrange("p (t e) -> p t e", e=NE),
                                       over_tokens(ny[:], NE), ALU.mult))
                link(dve.tensor_tensor(lg[:], lg[:], over_tiles(gate[:], NE), ALU.subtract))
                best_two(NE)
                dve.tensor_scalar(gated[:], lg[:], 0.0, None, ALU.max)
                link(dve.tensor_scalar(eq[:], lg[:], 0.0, None, ALU.is_gt))
                link(dve.tensor_tensor(s1[:], s1[:], s2[:], ALU.add))
                dve.tensor_reduce(top[:, 0], gated[:], AX.X, ALU.max)
                link(dve.tensor_reduce(col[:, 2], eq[:], AX.X, ALU.max))
                dve.tensor_tensor(gated[:], gated[:], over_tokens(top[:, 0], NE), ALU.subtract).then_inc(gate_arg.sem, 1)
                link(dve.tensor_scalar(col[:, 2], col[:, 2], -1.0, 1.0, ALU.mult, ALU.add))
                link(dve.tensor_tensor(s1[:], s1[:], over_tokens(col[:, 2], NE), ALU.mult))
                link(dve.tensor_tensor(s1[:], s1[:], eq[:], ALU.add))
                dve.wait_ge(gate_exp.sem, gate_exp.after(b, 1))
                link(dve.tensor_tensor(rw[:], gated[:], s1[:], ALU.mult))
                link(dve.tensor_reduce(top[:, 0], rw[:], AX.X, ALU.add))
                link(dve.reciprocal(top[:, 1], top[:, 0]))
                link(dve.tensor_tensor(rw[:], rw[:], over_tokens(top[:, 1], NE), ALU.mult))
                split_weights(NE)
                add_experts(4)
                def weigh(m, src):
                    dve.wait_ge(bc_psum.sem, bc_psum.after(b, m + 1))
                    if m >= 3:
                        dve.wait_ge(rh_used.sem, rh_used.after(b, m - 2))
                    dve.tensor_tensor(rh[:, m % 3], src, bank[BC_BANK[m]], ALU.mult).then_inc(rh_ready.sem, 1)

                for e in range(NE):
                    weigh(e, hT[:])
                    if e == 2:
                        add_experts(5)

                def row_max(i):
                    dve.wait_ge(s_psum.sem, s_psum.after(b, i + 1))
                    link(dve.tensor_reduce(col[:, 3, i:i + 1], bank[S_BANK[i]][:, 0:P * (i + 1)], AX.X, ALU.max))
                    dve.tensor_scalar(col[:, 0, i:i + 1], col[:, 3, i:i + 1], -(DH ** -0.5), None, ALU.mult).then_inc(
                        s_max.sem, 1)

                def row_norm(i):
                    dve.wait_ge(p_exp.sem, p_exp.after(b, i + 1))
                    link(dve.reciprocal(col[:, 2, i:i + 1], col[:, 1, i:i + 1]))
                    n = P * (i + 1)
                    dve.tensor_scalar(pa[:, i, 0:n], pa[:, i, 0:n], col[:, 2, i:i + 1], None, ALU.mult).then_inc(
                        p_norm.sem, 1)

                for i in range(3):
                    row_max(i)
                row_norm(0)
                row_max(3)
                for i in range(1, NT):
                    row_norm(i)
                dve.wait_ge(att_stored.sem, att_stored.after(b, 1))
                for n in range(NE // 2):
                    weigh(NE + n, a_T[:])
                dve.wait_ge(k_hi_ready.sem, k_hi_ready.after(b, 1))
                dve.tensor_tensor(k_lo, kv_f, k_hi, ALU.subtract).then_inc(k_lo_ready.sem, 1)
                dve.wait_ge(back_psum.sem, back_psum.after(b, 2))
                link(dve.tensor_tensor(x_rows[:], x_rows[:], rows(bank[1]), ALU.add))

                normalise(x_rows, h_rows, link, h_ready, h_ready.after(b, 8))
                for g in range(NG):
                    dve.wait_ge(krep_psum.sem, krep_psum.after(b, g + 1))
                    src = bank[KREP_BANK[g]][0:96, 0:KP]
                    dve.tensor_tensor(ks[0:96, g], src.unsqueeze(1).to_broadcast([96, 4, KP]),
                                      band[0:96].unsqueeze(2).to_broadcast([96, 4, KP]), ALU.mult).then_inc(
                                          ks_ready.sem, 1)
                dve.wait_ge(qf_ready.sem, qf_ready.after(b, 1))
                dve.wait_ge(count_psum.sem, count_psum.after(b, 1))
                dve.scalar_tensor_tensor(qm[:], bank[0], KP - 0.5, qf[:], ALU.is_lt, ALU.mult).then_inc(q_masked.sem, 1)
                dve.wait_ge(q_masked.sem, q_masked.after(b, 1))
                dve.tensor_copy(q_hi[:], qm[:]).then_inc(q_hi_ready.sem, 1)
                dve.wait_ge(q_hi_ready.sem, q_hi_ready.after(b, 1))
                dve.tensor_tensor(q_lo[:], qm[:], q_hi[:], ALU.subtract).then_inc(q_lo_ready.sem, 1)
                add_experts(6)
                for n in range(NT * NG):
                    i, g = divmod(n, NG)
                    dve.wait_ge(smax_psum.sem, smax_psum.after(b, n + 1))
                    dve.tensor_reduce(mx[:, i, 4 * g:4 * g + 4].rearrange("p (w j) -> p w j", w=2),
                                      duo[SMAX_DUO[n % 3]][:, :, 0:2 * SK].rearrange("p w (j k) -> p w j k", j=2),
                                      AX.X, ALU.max).then_inc(smax_used.sem, 1)
                dve.wait_ge(smax_used.sem, smax_used.after(b, NT * NG))
                dve.wait_ge(fixed_ready.sem, fixed_ready.after(b, 3))
                m4 = mx[:].rearrange("p t (g j) -> p t g j", g=NG)
                link(dve.tensor_scalar(nm[:].bitcast(F32R)[:, :, :, 0:4], m4, -1.0, None, ALU.mult))
                dve.scalar_tensor_tensor(nm[:, :, :, 4:8], m4, -1.0, nm[:, :, :, 0:4], ALU.mult,
                                         ALU.subtract).then_inc(nm_ready.sem, 1)
                add_experts(7)
                if behind:
                    last_norm(b - 1)
                dve.wait_ge(pm_used.sem, pm_used.after(b, (NG + H1) // 2))
                link(dve.reciprocal(rz[0:64], bank[6][64:P]))
                dve.tensor_tensor(qf[0:64], bank[6][0:64], rz[0:64], ALU.mult)
                if more:
                    first_norm(b + 1)
                dve.wait_ge(pm_used.sem, pm_used.after(b, NG + H1))
                link(dve.reciprocal(rz[64:P], bank[7][0:64]))
                dve.tensor_tensor(qf[64:P], bank[7][64:P], rz[64:P], ALU.mult).then_inc(pv_normed.sem, 1)
                if more:
                    split_h1(b + 1)
                if behind:
                    dve.wait_ge(out_stored.sem, out_stored.after(b - 1, 16))
                dve.wait_ge(x_rows_biased.sem, x_rows_biased.after(b, 1))
                dve.wait_ge(back_psum.sem, back_psum.after(b, 3))
                link(dve.tensor_tensor(x4_rows[:], x_rows[:], rows(bank[3]), ALU.add))

                normalise(x4_rows, h4_rows, link, h_ready, h_ready.after(b, 12))
                if more:
                    early_maxima(b + 1)
                dve.wait_ge(h4T_hi_ready.sem, h4T_hi_ready.after(b, 1))
                dve.tensor_tensor(h4_lo[:], bank[0], h4_hi[:], ALU.subtract).then_inc(h4T_lo_ready.sem, 1)
                dve.wait_ge(logit_psum.sem, logit_psum.after(b, 2))
                link(dve.tensor_tensor(lg[:, :, 0:NX], bank[3][:, 0:NT * NX].rearrange("p (t e) -> p t e", e=NX),
                                       over_tiles(b_r[:], NX), ALU.add))
                best_two(NX)
                dve.tensor_tensor(col[:, 0], top[:, 1], top[:, 0], ALU.subtract).then_inc(gate_arg.sem, 1)
                if more:
                    turned_tails(b + 1, 1)
                dve.wait_ge(gate_exp.sem, gate_exp.after(b, 2))
                link(dve.tensor_scalar(col[:, 2], col[:, 1], 1.0, None, ALU.add))
                link(dve.reciprocal(col[:, 3], col[:, 2]))
                link(dve.tensor_tensor(col[:, 2], col[:, 1], col[:, 3], ALU.mult))
                dve.tensor_tensor(s1[:, :, 0:NX], s1[:, :, 0:NX], over_tokens(col[:, 3], NX), ALU.mult)
                link(dve.tensor_tensor(s2[:, :, 0:NX], s2[:, :, 0:NX], over_tokens(col[:, 2], NX), ALU.mult))
                link(dve.tensor_tensor(rw[:, :, 0:NX], s1[:, :, 0:NX], s2[:, :, 0:NX], ALU.add))
                split_weights(NX)
                assert steps[0] == DVE_STEPS, steps

            tables()
            first_norm(0)
            split_h1(0)
            split_b2()
            early_maxima(0)
            turned_tails(0, 1)
            batch(0, behind=False)
            with dve.Fori(1, B - 1) as b:
                batch(b)
            batch(B - 1, more=False)
            for e in range(NX):
                add_expert(B - 1, e)
            last_norm(B - 1)


_SHAPES = ["x", "ctx_T", "mask", "mask_T", "wq_T", "wk_T", "wv_T", "wo", "gamma0", "beta0", "sim", "gates", "q_proj",
           "k_proj", "v_proj", "o_proj", "w_att", "b_att", "w_r", "b_r", "w1", "b1", "w2", "b2", "gamma1", "beta1"]


def kernel(x, ctx_1024, mask_BxSxS2_if1, L0_xattn_W_Q, L0_xattn_W_K, L0_xattn_W_V, L0_xattn_W_O, L0_xattn_ln_gamma,
           L0_xattn_ln_beta, L0_ffn_sim_matrix, L0_ffn_gates, L0_ffn_q_proj, L0_ffn_k_proj, L0_ffn_v_proj,
           L0_ffn_o_proj, L1_xattn_W0, L1_xattn_b0, L1_xattn_W1, L1_xattn_b1, L1_xattn_W2, L1_xattn_b2, L1_xattn_W3,
           L1_xattn_b3, L1_ffn_Wr, L1_ffn_br, L1_ffn_W1, L1_ffn_b1, L1_ffn_W2, L1_ffn_b2, L1_ffn_gamma, L1_ffn_beta):
    import concourse.bacc as bacc
    from concourse.bass_utils import run_bass_kernel_spmd

    arrays = {
        "x": x,
        "ctx_T": ctx_1024.transpose(0, 2, 1),
        "mask": mask_BxSxS2_if1,
        "mask_T": mask_BxSxS2_if1.transpose(0, 2, 1),
        "wq_T": L0_xattn_W_Q.T, "wk_T": L0_xattn_W_K.T, "wv_T": L0_xattn_W_V.T, "wo": L0_xattn_W_O,
        "gamma0": L0_xattn_ln_gamma, "beta0": L0_xattn_ln_beta,
        "sim": L0_ffn_sim_matrix, "gates": L0_ffn_gates,
        "q_proj": L0_ffn_q_proj, "k_proj": L0_ffn_k_proj, "v_proj": L0_ffn_v_proj, "o_proj": L0_ffn_o_proj,
        "w_att": np.stack([np.asarray(w).T for w in (L1_xattn_W0, L1_xattn_W1, L1_xattn_W2, L1_xattn_W3)], 1),
        "b_att": np.stack([np.asarray(w) for w in (L1_xattn_b0, L1_xattn_b1, L1_xattn_b2, L1_xattn_b3)], 1),
        "w_r": L1_ffn_Wr.T, "b_r": L1_ffn_br,
        "w1": L1_ffn_W1.transpose(2, 0, 1).reshape(D, NX * F),
        "b1": L1_ffn_b1.reshape(NX * FC, P).T,
        "w2": L1_ffn_W2.transpose(0, 2, 1).reshape(NX * FC, P, D).transpose(1, 0, 2),
        "b2": L1_ffn_b2, "b3": L1_xattn_b3, "gamma1": L1_ffn_gamma, "beta1": L1_ffn_beta,
    }
    arrays.update(constants())
    nc = bacc.Bacc("TRN2", target_bir_lowering=False, num_devices=1)
    sent, aps = {}, {}
    for name, value in arrays.items():
        value = np.ascontiguousarray(value)
        sent[f"in_{name}"] = value
        aps[name] = nc.dram_tensor(f"in_{name}", value.shape, mybir.dt.from_np(value.dtype),
                                   kind="ExternalInput").ap()
    out = nc.dram_tensor("out", (B, S, D), F32, kind="ExternalOutput").ap()
    program(nc, aps, out)
    result = run_bass_kernel_spmd(nc, [sent], core_ids=[0])
    return result.results[0]["out"]
```
